# Optimizing a Trainium2 kernel written in Bass

```python
import numpy as np
import jax
import jax.numpy as jnp

def _softmax(x, axis=-1):
    return jax.nn.softmax(x, axis=axis)
def _gelu(x):
    return jax.nn.gelu(x, approximate=True)
def _silu(x):
    return jax.nn.silu(x)
def _sigmoid(x):
    return jax.nn.sigmoid(x)
def _layernorm(x, axis=-1, eps=1e-5):
    m = jnp.mean(x, axis=axis, keepdims=True)
    v = jnp.var(x, axis=axis, keepdims=True)
    return (x - m) / jnp.sqrt(v + eps)
def _scatter_add(tgt, idx, src, axis=0):
    return tgt.at[idx].add(src)
def _segment_sum(src, seg, n):
    return jax.ops.segment_sum(src, seg, n)

kernel_name = 'mk_conv_seq_d4_conv_nchw128_387844'

def setup_inputs(seed: int = 0):
    np.random.seed(seed)
    _w = jnp.asarray
    def _rec_inputs():
        import jax
        import jax.numpy as jnp
        _gk = jax.random.key(seed)
        x = -0.0002023 + 1 * jax.random.normal(jax.random.fold_in(_gk, 1), (1, 128, 224, 224), jnp.float32)
        return x
    x = _rec_inputs()
    def _L0_conv_setup():
        import jax, jax.numpy as jnp
        import numpy as np
        from jax import lax
        S = 7
        HEADS = 8
        DIM = 128
        HD = DIM // HEADS
        B, H, W = (1, 224, 224)
        SCALE = HD ** (-0.5)

        def _conv1x1(x, w, b):
            return jnp.einsum('oc,bchw->bohw', w, x) + b[None, :, None, None]

        def _lepe(x, w, b):
            y = lax.conv_general_dilated(x, w, window_strides=(1, 1), padding=((1, 1), (1, 1)), feature_group_count=x.shape[1], dimension_numbers=('NCHW', 'OIHW', 'NCHW'))
            y = y + b[None, :, None, None]
            return x + jax.nn.gelu(y, approximate=False)

        def _tiled_bias(small_ssh, tiles):
            b = small_ssh.transpose(2, 0, 1)
            b = jnp.repeat(b, tiles, axis=1)
            b = jnp.repeat(b, tiles, axis=2)
            return b
        key = jax.random.key(seed)
        ks = jax.random.split(key, 14)
        f = jax.random.normal
        return {'x': f(ks[0], (B, DIM, H, W), jnp.float32), 'qkv_h_w': f(ks[1], (3 * DIM, DIM), jnp.float32) * 0.05, 'qkv_h_b': f(ks[2], (3 * DIM,), jnp.float32) * 0.02, 'qkv_v_w': f(ks[3], (3 * DIM, DIM), jnp.float32) * 0.05, 'qkv_v_b': f(ks[4], (3 * DIM,), jnp.float32) * 0.02, 'proj_w': f(ks[5], (DIM, DIM), jnp.float32) * 0.05, 'proj_b': f(ks[6], (DIM,), jnp.float32) * 0.02, 'lepe_h_w': f(ks[7], (DIM, 1, 3, 3), jnp.float32) * 0.1, 'lepe_h_b': f(ks[8], (DIM,), jnp.float32) * 0.02, 'lepe_v_w': f(ks[9], (DIM, 1, 3, 3), jnp.float32) * 0.1, 'lepe_v_b': f(ks[10], (DIM,), jnp.float32) * 0.02, 'table_h': f(ks[11], (2 * S - 1, 2 * S - 1, HEADS), jnp.float32) * 0.02, 'table_v': f(ks[12], (2 * S - 1, 2 * S - 1, HEADS), jnp.float32) * 0.02}
    _L0_conv_all = _L0_conv_setup()
    _L0_conv_in = {k: v for k, v in _L0_conv_all.items() if k in ('qkv_h_w', 'qkv_h_b', 'qkv_v_w', 'qkv_v_b', 'proj_w', 'proj_b', 'lepe_h_w', 'lepe_h_b', 'lepe_v_w', 'lepe_v_b', 'table_h', 'table_v', )}
    del _L0_conv_all

    def _L1_conv_setup():
        import jax, jax.numpy as jnp
        import numpy as np
        D_MODEL = 128
        D_INNER = 256
        D_STATE = 16
        DT_RANK = 8
        D_CONV = 2
        GROUPS = 4
        EPS = 1e-05

        def _mamba_dir(x, W_in, conv_w, conv_b, W_x, W_dt, b_dt, A_log, D, W_out):
            B, L, _ = x.shape
            xz = x @ W_in
            xp, z = (xz[..., :D_INNER], xz[..., D_INNER:])
            xprev = jnp.pad(xp, ((0, 0), (1, 0), (0, 0)))[:, :L]
            xc = jax.nn.silu(xprev * conv_w[:, 0] + xp * conv_w[:, 1] + conv_b)
            xdb = xc @ W_x
            dt_r = xdb[..., :DT_RANK]
            Bc = xdb[..., DT_RANK:DT_RANK + D_STATE]
            Cc = xdb[..., DT_RANK + D_STATE:]
            dt = jax.nn.softplus(dt_r @ W_dt + b_dt)
            A = -jnp.exp(A_log)

            def step(h, inp):
                dt_t, B_t, C_t, x_t = inp
                dA = jnp.exp(dt_t[:, :, None] * A)
                h = dA * h + (dt_t * x_t)[:, :, None] * B_t[:, None, :]
                y = jnp.einsum('bds,bs->bd', h, C_t)
                return (h, y)
            h0 = jnp.zeros((B, D_INNER, D_STATE), x.dtype)
            xs = (jnp.moveaxis(dt, 1, 0), jnp.moveaxis(Bc, 1, 0), jnp.moveaxis(Cc, 1, 0), jnp.moveaxis(xc, 1, 0))
            _, ys = jax.lax.scan(step, h0, xs)
            y = jnp.moveaxis(ys, 0, 1) + D * xc
            y = y * jax.nn.silu(z)
            return y @ W_out

        def _groupnorm_silu(x, gamma, beta):
            B, C, H, W = x.shape
            xg = x.reshape(B, GROUPS, C // GROUPS, H, W)
            mu = xg.mean(axis=(2, 3, 4), keepdims=True)
            var = xg.var(axis=(2, 3, 4), keepdims=True)
            xn = ((xg - mu) * jax.lax.rsqrt(var + EPS)).reshape(B, C, H, W)
            return jax.nn.silu(xn * gamma[None, :, None, None] + beta[None, :, None, None])
        key = jax.random.key(seed)
        ks = jax.random.split(key, 24)
        s = 0.02
        A_log = jnp.log(jnp.tile(jnp.arange(1, D_STATE + 1, dtype=jnp.float32)[None, :], (D_INNER, 1)))
        inp = {'x': jax.random.normal(ks[0], (4, D_MODEL, 64, 64), jnp.float32)}
        for i, sfx in enumerate(('f', 'b')):
            o = 1 + 9 * i
            inp[f'W_in_{sfx}'] = jax.random.normal(ks[o], (D_MODEL, 2 * D_INNER)) * s
            inp[f'conv_w_{sfx}'] = jax.random.normal(ks[o + 1], (D_INNER, D_CONV)) * 0.5
            inp[f'conv_b_{sfx}'] = jnp.zeros((D_INNER,))
            inp[f'W_x_{sfx}'] = jax.random.normal(ks[o + 2], (D_INNER, DT_RANK + 2 * D_STATE)) * s
            inp[f'W_dt_{sfx}'] = jax.random.normal(ks[o + 3], (DT_RANK, D_INNER)) * s
            inp[f'b_dt_{sfx}'] = jnp.full((D_INNER,), -3.0)
            inp[f'A_log_{sfx}'] = A_log
            inp[f'D_{sfx}'] = jnp.ones((D_INNER,))
            inp[f'W_out_{sfx}'] = jax.random.normal(ks[o + 4], (D_INNER, D_MODEL)) * s
        inp['gn_gamma'] = jnp.ones((D_MODEL,))
        inp['gn_beta'] = jnp.zeros((D_MODEL,))
        return inp
    _L1_conv_all = _L1_conv_setup()
    _L1_conv_in = {k: v for k, v in _L1_conv_all.items() if k in ('W_in_f', 'conv_w_f', 'conv_b_f', 'W_x_f', 'W_dt_f', 'b_dt_f', 'A_log_f', 'D_f', 'W_out_f', 'W_in_b', 'conv_w_b', 'conv_b_b', 'W_x_b', 'W_dt_b', 'b_dt_b', 'A_log_b', 'D_b', 'W_out_b', 'gn_gamma', 'gn_beta', )}
    del _L1_conv_all

    def _L2_conv_setup():
        import jax, jax.numpy as jnp
        import numpy as np
        MIDC = 128
        HEADS = 8
        HEADC = MIDC // HEADS
        EPS = 1e-05

        def _ln(t, w, b):
            m = t.mean(-1, keepdims=True)
            s = jnp.std(t, axis=-1, ddof=1, keepdims=True)
            return w * ((t - m) / (s + EPS)) + b
        key = jax.random.key(seed)
        ks = jax.random.split(key, 8)
        B, C, H, W = (8, MIDC, 256, 256)
        s = 1.0 / np.sqrt(C)
        x = jax.random.normal(ks[0], (B, C, H, W), dtype=jnp.float32)
        qkv_w = jax.random.normal(ks[1], (3 * C, C), dtype=jnp.float32) * s
        o1_w = jax.random.normal(ks[2], (C, C), dtype=jnp.float32) * s
        o2_w = jax.random.normal(ks[3], (C, C), dtype=jnp.float32) * s
        kln_w = 1.0 + 0.1 * jax.random.normal(ks[4], (HEADS, 1, HEADC), dtype=jnp.float32)
        kln_b = 0.1 * jax.random.normal(ks[5], (HEADS, 1, HEADC), dtype=jnp.float32)
        vln_w = 1.0 + 0.1 * jax.random.normal(ks[6], (HEADS, 1, HEADC), dtype=jnp.float32)
        vln_b = 0.1 * jax.random.normal(ks[7], (HEADS, 1, HEADC), dtype=jnp.float32)
        return {'x': x, 'qkv_w': qkv_w, 'o1_w': o1_w, 'o2_w': o2_w, 'kln_w': kln_w, 'kln_b': kln_b, 'vln_w': vln_w, 'vln_b': vln_b}
    _L2_conv_all = _L2_conv_setup()
    _L2_conv_in = {k: v for k, v in _L2_conv_all.items() if k in ('qkv_w', 'o1_w', 'o2_w', 'kln_w', 'kln_b', 'vln_w', 'vln_b', )}
    del _L2_conv_all

    def _L3_conv_setup():
        import jax, jax.numpy as jnp
        import numpy as np
        B_, C_, H_, W_ = (16, 128, 64, 64)
        D_MODEL = C_ // 4
        D_STATE = 16
        D_CONV = 4
        EXPAND = 2
        D_INNER = EXPAND * D_MODEL
        DT_RANK = (D_MODEL + 15) // 16
        EPS = 1e-05

        def _mamba(x, in_proj_w, conv_w, conv_b, x_proj_w, dt_proj_w, dt_proj_b, A_log, D, out_proj_w):
            G, L, _ = x.shape
            xz = jnp.einsum('gld,ed->gle', x, in_proj_w)
            xi, z = jnp.split(xz, 2, axis=-1)
            xc = jax.lax.conv_general_dilated(xi.transpose(0, 2, 1), conv_w[:, None, :], window_strides=(1,), padding=[(D_CONV - 1, 0)], feature_group_count=D_INNER)
            u = jax.nn.silu(xc.transpose(0, 2, 1) + conv_b)
            x_dbl = jnp.einsum('gld,ed->gle', u, x_proj_w)
            dt, Bm, Cm = jnp.split(x_dbl, [DT_RANK, DT_RANK + D_STATE], axis=-1)
            delta = jax.nn.softplus(jnp.einsum('glr,dr->gld', dt, dt_proj_w) + dt_proj_b)
            A = -jnp.exp(A_log)

            def step(h, inputs):
                d_t, u_t, B_t, C_t = inputs
                dA = jnp.exp(d_t[..., None] * A)
                h = h * dA + (d_t * u_t)[..., None] * B_t[:, None, :]
                y = jnp.einsum('gdn,gn->gd', h, C_t)
                return (h, y)
            h0 = jnp.zeros((G, D_INNER, D_STATE), x.dtype)
            xs = (delta.transpose(1, 0, 2), u.transpose(1, 0, 2), Bm.transpose(1, 0, 2), Cm.transpose(1, 0, 2))
            _, ys = jax.lax.scan(step, h0, xs)
            y = ys.transpose(1, 0, 2) + u * D
            y = y * jax.nn.silu(z)
            return jnp.einsum('gld,ed->gle', y, out_proj_w)
        key = jax.random.key(seed)
        ks = jax.random.split(key, 8)

        def n(k, shape, scale=0.02):
            return jax.random.normal(k, shape, dtype=jnp.float32) * scale
        A = jnp.broadcast_to(jnp.arange(1, D_STATE + 1, dtype=jnp.float32), (D_INNER, D_STATE))
        return {'input': jax.random.normal(ks[0], (B_, C_, H_, W_), dtype=jnp.float32), 'ln_g': jnp.ones((C_,), jnp.float32), 'ln_b': jnp.zeros((C_,), jnp.float32), 'in_proj_w': n(ks[1], (2 * D_INNER, D_MODEL)), 'conv_w': n(ks[2], (D_INNER, D_CONV), 0.1), 'conv_b': jnp.zeros((D_INNER,), jnp.float32), 'x_proj_w': n(ks[3], (DT_RANK + 2 * D_STATE, D_INNER)), 'dt_proj_w': n(ks[4], (D_INNER, DT_RANK), 0.5), 'dt_proj_b': jnp.full((D_INNER,), -4.6, jnp.float32), 'A_log': jnp.log(A), 'D': jnp.ones((D_INNER,), jnp.float32), 'out_proj_w': n(ks[5], (D_MODEL, D_INNER))}
    _L3_conv_all = _L3_conv_setup()
    _L3_conv_in = {k: v for k, v in _L3_conv_all.items() if k in ('ln_g', 'ln_b', 'in_proj_w', 'conv_w', 'conv_b', 'x_proj_w', 'dt_proj_w', 'dt_proj_b', 'A_log', 'D', 'out_proj_w', )}
    del _L3_conv_all

    return {
        "x": x,
        "L0_conv_qkv_h_w": _L0_conv_in["qkv_h_w"],
        "L0_conv_qkv_h_b": _L0_conv_in["qkv_h_b"],
        "L0_conv_qkv_v_w": _L0_conv_in["qkv_v_w"],
        "L0_conv_qkv_v_b": _L0_conv_in["qkv_v_b"],
        "L0_conv_proj_w": _L0_conv_in["proj_w"],
        "L0_conv_proj_b": _L0_conv_in["proj_b"],
        "L0_conv_lepe_h_w": _L0_conv_in["lepe_h_w"],
        "L0_conv_lepe_h_b": _L0_conv_in["lepe_h_b"],
        "L0_conv_lepe_v_w": _L0_conv_in["lepe_v_w"],
        "L0_conv_lepe_v_b": _L0_conv_in["lepe_v_b"],
        "L0_conv_table_h": _L0_conv_in["table_h"],
        "L0_conv_table_v": _L0_conv_in["table_v"],
        "L1_conv_W_in_f": _L1_conv_in["W_in_f"],
        "L1_conv_conv_w_f": _L1_conv_in["conv_w_f"],
        "L1_conv_conv_b_f": _L1_conv_in["conv_b_f"],
        "L1_conv_W_x_f": _L1_conv_in["W_x_f"],
        "L1_conv_W_dt_f": _L1_conv_in["W_dt_f"],
        "L1_conv_b_dt_f": _L1_conv_in["b_dt_f"],
        "L1_conv_A_log_f": _L1_conv_in["A_log_f"],
        "L1_conv_D_f": _L1_conv_in["D_f"],
        "L1_conv_W_out_f": _L1_conv_in["W_out_f"],
        "L1_conv_W_in_b": _L1_conv_in["W_in_b"],
        "L1_conv_conv_w_b": _L1_conv_in["conv_w_b"],
        "L1_conv_conv_b_b": _L1_conv_in["conv_b_b"],
        "L1_conv_W_x_b": _L1_conv_in["W_x_b"],
        "L1_conv_W_dt_b": _L1_conv_in["W_dt_b"],
        "L1_conv_b_dt_b": _L1_conv_in["b_dt_b"],
        "L1_conv_A_log_b": _L1_conv_in["A_log_b"],
        "L1_conv_D_b": _L1_conv_in["D_b"],
        "L1_conv_W_out_b": _L1_conv_in["W_out_b"],
        "L1_conv_gn_gamma": _L1_conv_in["gn_gamma"],
        "L1_conv_gn_beta": _L1_conv_in["gn_beta"],
        "L2_conv_qkv_w": _L2_conv_in["qkv_w"],
        "L2_conv_o1_w": _L2_conv_in["o1_w"],
        "L2_conv_o2_w": _L2_conv_in["o2_w"],
        "L2_conv_kln_w": _L2_conv_in["kln_w"],
        "L2_conv_kln_b": _L2_conv_in["kln_b"],
        "L2_conv_vln_w": _L2_conv_in["vln_w"],
        "L2_conv_vln_b": _L2_conv_in["vln_b"],
        "L3_conv_ln_g": _L3_conv_in["ln_g"],
        "L3_conv_ln_b": _L3_conv_in["ln_b"],
        "L3_conv_in_proj_w": _L3_conv_in["in_proj_w"],
        "L3_conv_conv_w": _L3_conv_in["conv_w"],
        "L3_conv_conv_b": _L3_conv_in["conv_b"],
        "L3_conv_x_proj_w": _L3_conv_in["x_proj_w"],
        "L3_conv_dt_proj_w": _L3_conv_in["dt_proj_w"],
        "L3_conv_dt_proj_b": _L3_conv_in["dt_proj_b"],
        "L3_conv_A_log": _L3_conv_in["A_log"],
        "L3_conv_D": _L3_conv_in["D"],
        "L3_conv_out_proj_w": _L3_conv_in["out_proj_w"],
    }

def reference(x, L0_conv_qkv_h_w, L0_conv_qkv_h_b, L0_conv_qkv_v_w, L0_conv_qkv_v_b, L0_conv_proj_w, L0_conv_proj_b, L0_conv_lepe_h_w, L0_conv_lepe_h_b, L0_conv_lepe_v_w, L0_conv_lepe_v_b, L0_conv_table_h, L0_conv_table_v, L1_conv_W_in_f, L1_conv_conv_w_f, L1_conv_conv_b_f, L1_conv_W_x_f, L1_conv_W_dt_f, L1_conv_b_dt_f, L1_conv_A_log_f, L1_conv_D_f, L1_conv_W_out_f, L1_conv_W_in_b, L1_conv_conv_w_b, L1_conv_conv_b_b, L1_conv_W_x_b, L1_conv_W_dt_b, L1_conv_b_dt_b, L1_conv_A_log_b, L1_conv_D_b, L1_conv_W_out_b, L1_conv_gn_gamma, L1_conv_gn_beta, L2_conv_qkv_w, L2_conv_o1_w, L2_conv_o2_w, L2_conv_kln_w, L2_conv_kln_b, L2_conv_vln_w, L2_conv_vln_b, L3_conv_ln_g, L3_conv_ln_b, L3_conv_in_proj_w, L3_conv_conv_w, L3_conv_conv_b, L3_conv_x_proj_w, L3_conv_dt_proj_w, L3_conv_dt_proj_b, L3_conv_A_log, L3_conv_D, L3_conv_out_proj_w):
    import jax
    import jax.numpy as jnp
    def _L0_conv_ref(x, qkv_h_w, qkv_h_b, qkv_v_w, qkv_v_b, proj_w, proj_b, lepe_h_w, lepe_h_b, lepe_v_w, lepe_v_b, table_h, table_v):
        import jax, jax.numpy as jnp
        import numpy as np
        from jax import lax
        S = 7
        HEADS = 8
        DIM = 128
        HD = DIM // HEADS
        B, H, W = (1, 224, 224)
        SCALE = HD ** (-0.5)

        def _conv1x1(x, w, b):
            return jnp.einsum('oc,bchw->bohw', w, x) + b[None, :, None, None]

        def _lepe(x, w, b):
            y = lax.conv_general_dilated(x, w, window_strides=(1, 1), padding=((1, 1), (1, 1)), feature_group_count=x.shape[1], dimension_numbers=('NCHW', 'OIHW', 'NCHW'))
            y = y + b[None, :, None, None]
            return x + jax.nn.gelu(y, approximate=False)

        def _tiled_bias(small_ssh, tiles):
            b = small_ssh.transpose(2, 0, 1)
            b = jnp.repeat(b, tiles, axis=1)
            b = jnp.repeat(b, tiles, axis=2)
            return b
        b_, c, h, w = x.shape
        idx = jnp.arange(S)
        rel = idx[:, None] - idx[None, :] + S - 1
        qkv = _conv1x1(x, qkv_h_w, qkv_h_b).reshape(b_, 3, HEADS, HD, h, w)
        q, k, v = (qkv[:, 0], qkv[:, 1], qkv[:, 2])
        bias_h = _tiled_bias(table_h[S - 1, rel, :], w // S)
        scores = jnp.einsum('bhdiw,bhdix->bhiwx', q, k) * SCALE + bias_h[None, :, None]
        attn = jax.nn.softmax(scores, axis=-1)
        out_h = jnp.einsum('bhiwx,bhdix->bhdiw', attn, v).reshape(b_, c, h, w)
        out_h = _lepe(out_h, lepe_h_w, lepe_h_b)
        qkv = _conv1x1(x, qkv_v_w, qkv_v_b).reshape(b_, 3, HEADS, HD, h, w)
        q, k, v = (qkv[:, 0], qkv[:, 1], qkv[:, 2])
        bias_v = _tiled_bias(table_v[rel, S - 1, :], h // S)
        scores = jnp.einsum('bhdiw,bhdjw->bhwij', q, k) * SCALE + bias_v[None, :, None]
        attn = jax.nn.softmax(scores, axis=-1)
        out_v = jnp.einsum('bhwij,bhdjw->bhdiw', attn, v).reshape(b_, c, h, w)
        out_v = _lepe(out_v, lepe_v_w, lepe_v_b)
        return _conv1x1(out_h + out_v, proj_w, proj_b)

    def _L1_conv_ref(x, W_in_f, conv_w_f, conv_b_f, W_x_f, W_dt_f, b_dt_f, A_log_f, D_f, W_out_f, W_in_b, conv_w_b, conv_b_b, W_x_b, W_dt_b, b_dt_b, A_log_b, D_b, W_out_b, gn_gamma, gn_beta):
        import jax, jax.numpy as jnp
        import numpy as np
        D_MODEL = 128
        D_INNER = 256
        D_STATE = 16
        DT_RANK = 8
        D_CONV = 2
        GROUPS = 4
        EPS = 1e-05

        def _mamba_dir(x, W_in, conv_w, conv_b, W_x, W_dt, b_dt, A_log, D, W_out):
            B, L, _ = x.shape
            xz = x @ W_in
            xp, z = (xz[..., :D_INNER], xz[..., D_INNER:])
            xprev = jnp.pad(xp, ((0, 0), (1, 0), (0, 0)))[:, :L]
            xc = jax.nn.silu(xprev * conv_w[:, 0] + xp * conv_w[:, 1] + conv_b)
            xdb = xc @ W_x
            dt_r = xdb[..., :DT_RANK]
            Bc = xdb[..., DT_RANK:DT_RANK + D_STATE]
            Cc = xdb[..., DT_RANK + D_STATE:]
            dt = jax.nn.softplus(dt_r @ W_dt + b_dt)
            A = -jnp.exp(A_log)

            def step(h, inp):
                dt_t, B_t, C_t, x_t = inp
                dA = jnp.exp(dt_t[:, :, None] * A)
                h = dA * h + (dt_t * x_t)[:, :, None] * B_t[:, None, :]
                y = jnp.einsum('bds,bs->bd', h, C_t)
                return (h, y)
            h0 = jnp.zeros((B, D_INNER, D_STATE), x.dtype)
            xs = (jnp.moveaxis(dt, 1, 0), jnp.moveaxis(Bc, 1, 0), jnp.moveaxis(Cc, 1, 0), jnp.moveaxis(xc, 1, 0))
            _, ys = jax.lax.scan(step, h0, xs)
            y = jnp.moveaxis(ys, 0, 1) + D * xc
            y = y * jax.nn.silu(z)
            return y @ W_out

        def _groupnorm_silu(x, gamma, beta):
            B, C, H, W = x.shape
            xg = x.reshape(B, GROUPS, C // GROUPS, H, W)
            mu = xg.mean(axis=(2, 3, 4), keepdims=True)
            var = xg.var(axis=(2, 3, 4), keepdims=True)
            xn = ((xg - mu) * jax.lax.rsqrt(var + EPS)).reshape(B, C, H, W)
            return jax.nn.silu(xn * gamma[None, :, None, None] + beta[None, :, None, None])
        B, C, H, W = x.shape
        xs = x.transpose(0, 2, 3, 1).reshape(B, H * W, C)
        y_f = _mamba_dir(xs, W_in_f, conv_w_f, conv_b_f, W_x_f, W_dt_f, b_dt_f, A_log_f, D_f, W_out_f)
        xr = xs[:, ::-1]
        y_b = _mamba_dir(xr, W_in_b, conv_w_b, conv_b_b, W_x_b, W_dt_b, b_dt_b, A_log_b, D_b, W_out_b)[:, ::-1]
        y = y_f + y_b
        y = y.reshape(B, H, W, C).transpose(0, 3, 1, 2)
        y = _groupnorm_silu(y, gn_gamma, gn_beta)
        return y + x

    def _L2_conv_ref(x, qkv_w, o1_w, o2_w, kln_w, kln_b, vln_w, vln_b):
        import jax, jax.numpy as jnp
        import numpy as np
        MIDC = 128
        HEADS = 8
        HEADC = MIDC // HEADS
        EPS = 1e-05

        def _ln(t, w, b):
            m = t.mean(-1, keepdims=True)
            s = jnp.std(t, axis=-1, ddof=1, keepdims=True)
            return w * ((t - m) / (s + EPS)) + b
        B, C, H, W = x.shape
        hc = C // HEADS
        N = H * W
        qkv = jnp.einsum('oc,bchw->bhwo', qkv_w, x)
        qkv = qkv.reshape(B, N, HEADS, 3 * hc).transpose(0, 2, 1, 3)
        q, k, v = jnp.split(qkv, 3, axis=-1)
        k = _ln(k, kln_w, kln_b)
        v = _ln(v, vln_w, vln_b)
        kv = jnp.einsum('bhnd,bhne->bhde', k, v) / N
        o = jnp.einsum('bhnd,bhde->bhne', q, kv)
        o = o.transpose(0, 2, 1, 3).reshape(B, H, W, C).transpose(0, 3, 1, 2)
        ret = o + x
        u = jnp.einsum('oc,bchw->bohw', o1_w, ret)
        u = jax.nn.gelu(u, approximate=False)
        u = jnp.einsum('oc,bchw->bohw', o2_w, u) + x
        return jax.nn.gelu(u, approximate=False)

    def _L3_conv_ref(input, ln_g, ln_b, in_proj_w, conv_w, conv_b, x_proj_w, dt_proj_w, dt_proj_b, A_log, D, out_proj_w):
        import jax, jax.numpy as jnp
        import numpy as np
        B_, C_, H_, W_ = (16, 128, 64, 64)
        D_MODEL = C_ // 4
        D_STATE = 16
        D_CONV = 4
        EXPAND = 2
        D_INNER = EXPAND * D_MODEL
        DT_RANK = (D_MODEL + 15) // 16
        EPS = 1e-05

        def _mamba(x, in_proj_w, conv_w, conv_b, x_proj_w, dt_proj_w, dt_proj_b, A_log, D, out_proj_w):
            G, L, _ = x.shape
            xz = jnp.einsum('gld,ed->gle', x, in_proj_w)
            xi, z = jnp.split(xz, 2, axis=-1)
            xc = jax.lax.conv_general_dilated(xi.transpose(0, 2, 1), conv_w[:, None, :], window_strides=(1,), padding=[(D_CONV - 1, 0)], feature_group_count=D_INNER)
            u = jax.nn.silu(xc.transpose(0, 2, 1) + conv_b)
            x_dbl = jnp.einsum('gld,ed->gle', u, x_proj_w)
            dt, Bm, Cm = jnp.split(x_dbl, [DT_RANK, DT_RANK + D_STATE], axis=-1)
            delta = jax.nn.softplus(jnp.einsum('glr,dr->gld', dt, dt_proj_w) + dt_proj_b)
            A = -jnp.exp(A_log)

            def step(h, inputs):
                d_t, u_t, B_t, C_t = inputs
                dA = jnp.exp(d_t[..., None] * A)
                h = h * dA + (d_t * u_t)[..., None] * B_t[:, None, :]
                y = jnp.einsum('gdn,gn->gd', h, C_t)
                return (h, y)
            h0 = jnp.zeros((G, D_INNER, D_STATE), x.dtype)
            xs = (delta.transpose(1, 0, 2), u.transpose(1, 0, 2), Bm.transpose(1, 0, 2), Cm.transpose(1, 0, 2))
            _, ys = jax.lax.scan(step, h0, xs)
            y = ys.transpose(1, 0, 2) + u * D
            y = y * jax.nn.silu(z)
            return jnp.einsum('gld,ed->gle', y, out_proj_w)
        B, C, H, W = input.shape
        L = H * W
        xf = input.reshape(B, C, L).transpose(0, 2, 1)
        mu = xf.mean(-1, keepdims=True)
        var = ((xf - mu) ** 2).mean(-1, keepdims=True)
        xn = (xf - mu) / jnp.sqrt(var + EPS) * ln_g + ln_b
        chunks = xn.reshape(B, L, 4, C // 4).transpose(2, 0, 1, 3).reshape(4 * B, L, C // 4)
        y = chunks + _mamba(chunks, in_proj_w, conv_w, conv_b, x_proj_w, dt_proj_w, dt_proj_b, A_log, D, out_proj_w)
        out = y.reshape(4, B, L, C // 4).transpose(1, 2, 0, 3).reshape(B, L, C)
        return out.transpose(0, 2, 1).reshape(B, C, H, W)

    def _gn(v, G=32, eps=1e-5):
        B_, C_, H_, W_ = v.shape
        g = v.reshape(B_, G, C_ // G, H_, W_)
        m = jnp.mean(g, axis=(2, 3, 4), keepdims=True)
        s = jnp.var(g, axis=(2, 3, 4), keepdims=True)
        return ((g - m) / jnp.sqrt(s + eps)).reshape(v.shape)

    def _ln_c(v, eps=1e-6):
        m = jnp.mean(v, axis=1, keepdims=True)
        s = jnp.var(v, axis=1, keepdims=True)
        return (v - m) / jnp.sqrt(s + eps)

    def _ln_t(v, eps=1e-5):
        m = jnp.mean(v, axis=-1, keepdims=True)
        s = jnp.var(v, axis=-1, keepdims=True)
        return (v - m) / jnp.sqrt(s + eps)

    def _to_tokens(v):
        B_, C_, H_, W_ = v.shape
        return v.reshape(B_, C_, H_ * W_).transpose(0, 2, 1)
    def _from_tokens(t, like):
        B_, C_, H_, W_ = like.shape
        return t.transpose(0, 2, 1).reshape(B_, C_, H_, W_)

    x = _L0_conv_ref(x, L0_conv_qkv_h_w, L0_conv_qkv_h_b, L0_conv_qkv_v_w, L0_conv_qkv_v_b, L0_conv_proj_w, L0_conv_proj_b, L0_conv_lepe_h_w, L0_conv_lepe_h_b, L0_conv_lepe_v_w, L0_conv_lepe_v_b, L0_conv_table_h, L0_conv_table_v)
    x = _L1_conv_ref(x, L1_conv_W_in_f, L1_conv_conv_w_f, L1_conv_conv_b_f, L1_conv_W_x_f, L1_conv_W_dt_f, L1_conv_b_dt_f, L1_conv_A_log_f, L1_conv_D_f, L1_conv_W_out_f, L1_conv_W_in_b, L1_conv_conv_w_b, L1_conv_conv_b_b, L1_conv_W_x_b, L1_conv_W_dt_b, L1_conv_b_dt_b, L1_conv_A_log_b, L1_conv_D_b, L1_conv_W_out_b, L1_conv_gn_gamma, L1_conv_gn_beta)
    x = _L2_conv_ref(x, L2_conv_qkv_w, L2_conv_o1_w, L2_conv_o2_w, L2_conv_kln_w, L2_conv_kln_b, L2_conv_vln_w, L2_conv_vln_b)
    x = _L3_conv_ref(x, L3_conv_ln_g, L3_conv_ln_b, L3_conv_in_proj_w, L3_conv_conv_w, L3_conv_conv_b, L3_conv_x_proj_w, L3_conv_dt_proj_w, L3_conv_dt_proj_b, L3_conv_A_log, L3_conv_D, L3_conv_out_proj_w)
    return x


_drawn_inputs = setup_inputs


def setup_inputs(seed=0):
    import zlib

    import numpy as np

    out = dict(_drawn_inputs(seed))
    spreads = {'L1_conv_conv_b_f': (0.0, 0.1),
     'L1_conv_b_dt_f': (-3.0, 0.6),
     'L1_conv_D_f': (1.0, 0.2),
     'L1_conv_conv_b_b': (0.0, 0.1),
     'L1_conv_b_dt_b': (-3.0, 0.6),
     'L1_conv_D_b': (1.0, 0.2),
     'L1_conv_gn_gamma': (1.0, 0.2),
     'L1_conv_gn_beta': (0.0, 0.1),
     'L3_conv_ln_g': (1.0, 0.2),
     'L3_conv_ln_b': (0.0, 0.1),
     'L3_conv_conv_b': (0.0, 0.8),
     'L3_conv_dt_proj_b': (-4.599999904632568, 0.6),
     'L3_conv_D': (1.0, 0.6)}
    factors = {'L0_conv_table_h': 7.364,
     'L0_conv_table_v': 7.745,
     'L1_conv_conv_w_f': 2.916,
     'L1_conv_W_x_f': 45.802,
     'L1_conv_W_dt_f': 64.0,
     'L1_conv_A_log_f': 43.574,
     'L1_conv_W_x_b': 64.0,
     'L1_conv_W_dt_b': 64.0,
     'L1_conv_A_log_b': 64.0,
     'L3_conv_in_proj_w': 8.0,
     'L3_conv_conv_w': 8.0,
     'L3_conv_x_proj_w': 8.0,
     'L3_conv_dt_proj_w': 8.0,
     'L3_conv_A_log': 8.0,
     'L3_conv_out_proj_w': 8.0}
    for name, (base, spread) in spreads.items():
        noise = np.random.default_rng([zlib.crc32(name.encode()), seed]).standard_normal(out[name].shape)
        drawn = base * np.exp(spread * noise) if base else spread * noise
        out[name] = jnp.asarray(drawn.astype(out[name].dtype))
    for name, factor in factors.items():
        out[name] = (out[name] * factor).astype(out[name].dtype)
    return out
```

```python
from contextlib import ExitStack

import numpy as np

import concourse.bass as bass
from concourse import mybir
from concourse.alu_op_type import AluOpType as ALU

ACT = mybir.ActivationFunctionType
F32 = mybir.dt.float32
BF16 = mybir.dt.bfloat16
AX_X = mybir.AxisListType.X

C = 128
SIDE = 224
TOKENS = SIDE * SIDE
T = 512
CHUNKS = TOKENS // T
EPS = 1e-5

S7 = 7
HEADS = 8
HD = C // HEADS
LINES = SIDE
BLOCK = 28
HALF = SIDE // 2
MAXROW = HD + S7

STATE = 16
UNITS = 2 * STATE
RING = 4

ATTN_COLS = {"wq": 256, "wk": 256, "wv": 128, "onehot": SIDE, "bq": 2, "ck": 2 * SIDE, "bv": 1}
LEPE_COLS = {"tap_h": 9, "tap_v": 9, "b_h": 1, "b_v": 1, "proj_b": 1, "proj": 128}
MAMBA1_COLS = {"win": 256, "tapw": 2 * 256, "wz": 256, "wbc": 2 * 96, "wdtr": 2 * 32, "wdt": 256,
               "bdt": 2, "convb": 2, "dskip": 2, "alog": UNITS, "wout": 256}
MAMBA3_COLS = {"win": 256, "tapw": 4 * 256, "wz": 256, "wb": 96, "wc": 96, "wdtr": 2 * 32, "wdt": 256,
               "bdt": 2, "convb": 2, "dskip": 2, "alog": UNITS, "wout": 256, "ln_g": 1, "ln_b": 1}
GLOBAL_COLS = {"gamma": 1, "beta": 1, "wkv": 256, "wq": 128, "o1t": 128, "o2t": 128,
               "ln_w": 256, "ln_b": 256, "groups": 128, "headmask": 128}


def offsets(cols):
    at, out = 0, {}
    for name, n in cols.items():
        out[name] = (at, at + n)
        at += n
    return out, at


def need(eng, sem, count):
    if not isinstance(count, int) or count > 0:
        eng.wait_ge(sem, count)


def clear_semaphores(nc, sems):
    with nc.Block() as block:
        @block.sync
        def _(eng):
            for sem in sems:
                eng.sem_clear(sem)


def make_identity(pool, tile, n, zeroed, made):
    pool.memset(tile[:, :], 0.0).then_inc(zeroed, 1)
    pool.wait_ge(zeroed, 1)
    pool.affine_select(out=tile[:, :], in_=tile[:, :], compare_op=ALU.not_equal, fill=1.0, base=0,
                       pattern=[[-1, n]], channel_multiplier=1).then_inc(made, 1)



def mamba_phase(nc, kind, x_dram, w_dram, out_dram, addend_dram=None, stats_dram=None):
    layer3 = kind == "chunked"
    rev = kind == "backward"
    cols = MAMBA3_COLS if layer3 else MAMBA1_COLS
    at, width = offsets(cols)
    TAPS = 4 if layer3 else 2
    NBC = 4 if layer3 else 1
    PER = 1 if layer3 else 2
    KB = UNITS // PER
    HALO = TAPS - 1

    if layer3:
        order = [("mean", 0), ("var", 1), ("conv0", 0), ("conv1", 1), ("gate0", 0), ("gate1", 1),
                 ("bc0", 0), ("bc1", 1), ("bc2", 0), ("bc3", 1), ("dtr", 1), ("dt0", 0), ("dt1", 1)]
    else:
        order = [("conv0", 0), ("conv1", 1), ("gate0", 0), ("gate1", 1),
                 ("bc0", 0), ("dtr", 1), ("dt0", 0), ("dt1", 1)]
    bank_of = dict(order)
    rank = {name: sum(1 for n, b in order[:i] if b == bank) for i, (name, bank) in enumerate(order)}
    fills = [sum(1 for _, b in order if b == bank) for bank in (0, 1)]

    def index(name, m):
        if name == "out":
            return (min(m + 2, CHUNKS) if isinstance(m, int) else m + 2) * fills[1] + m
        before = m * fills[bank_of[name]] + rank[name]
        if bank_of[name] == 1:
            before = before + (max(m - 1, 0) if isinstance(m, int) else m - 1)
        return before

    with ExitStack() as ctx:
        def sb(name, shape, dt=F32):
            return ctx.enter_context(nc.sbuf_tensor(f"{kind}_{name}", shape, dt))

        def pb(name, shape):
            return ctx.enter_context(nc.psum_tensor(f"{kind}_{name}", shape, F32))

        sems = []

        def sem(name):
            sems.append(ctx.enter_context(nc.semaphore(f"{kind}_{name}")))
            return sems[-1]

        w = sb("w", [C, width])
        W = {n: w[:, a:b] for n, (a, b) in at.items()}
        wconv = sb("wconv", [C, TAPS, 2, 128])
        decay = sb("decay", [C, UNITS])
        epst = sb("epst", [C, 1])
        ident = sb("ident", [C, 128])
        ones = sb("ones", [C, 128])
        select = sb("select", [96, 32, 128], BF16)
        xin = [sb(f"xin{p}", [C, T + 2]) for p in (0, 1)]
        xn = [sb(f"xn{p}", [C, HALO + T]) for p in (0, 1)] if layer3 else None
        cen = sb("cen", [C, T]) if layer3 else None
        sq = sb("sq", [C, T]) if layer3 else None
        xc = [sb(f"xc{p}", [C, 2, T]) for p in (0, 1)]
        zs = [sb(f"zs{p}", [C, 2, T]) for p in (0, 1)]
        bcs = [sb(f"bcs{p}", [96, NBC, T], BF16) for p in (0, 1)]
        rest = sb("rest", [96, T])
        mid = sb("mid", [96, T], BF16)
        dtr = sb("dtr", [32, T])
        sp = sb("sp", [C, 2, T])
        sp1 = sb("sp1", [C, 2, T])
        spl = sb("spl", [C, 2, T])
        dt = [sb(f"dt{p}", [C, 2, T]) for p in (0, 1)]
        dtx = [sb(f"dtx{p}", [C, 2, T]) for p in (0, 1)]
        da = sb("da", [C, RING, T])
        dbx = sb("dbx", [C, RING, T])
        hs = sb("hs", [C, UNITS, T])
        cb = sb("cb", [C, RING, T])
        hc = sb("hc", [C, RING, T])
        yv = sb("yv", [C, 2, T])
        yout = [sb(f"yout{p}", [C, T]) for p in (0, 1)]
        yadd = [sb(f"yadd{p}", [C, T]) for p in (0, 1)] if rev else None
        stats = sb("stats", [C, CHUNKS, 6]) if rev else None
        aggr = sb("aggr", [C, 2]) if rev else None

        prep = [pb(f"prep{b}", [C, T]) for b in (0, 1)]
        psB = [pb(f"psB{b}", [C, T]) for b in (0, 1)]
        psC = [pb(f"psC{b}", [C, T]) for b in (0, 1)]
        psY = [pb(f"psY{b}", [C, T]) for b in (0, 1)]

        w_loaded = sem("w_loaded")
        zeroed = sem("zeroed")
        consts = sem("consts")
        wconv_ready = sem("wconv_ready")
        alog_min = sem("alog_min")
        alog_exp = sem("alog_exp")
        x_loaded = [sem(f"x_loaded{p}") for p in (0, 1)]
        add_loaded = [sem(f"add_loaded{p}") for p in (0, 1)]
        filled = [sem(f"filled{b}") for b in (0, 1)]
        drained = [sem(f"drained{b}") for b in (0, 1)]
        sq_ready = sem("sq_ready")
        lnvar_ready = sem("lnvar_ready")
        rstd_ready = sem("rstd_ready")
        xhat_ready = sem("xhat_ready")
        halo_ready = sem("halo_ready")
        xn_ready = sem("xn_ready")
        hi_ready = sem("hi_ready")
        mid_ready = sem("mid_ready")
        lo_ready = sem("lo_ready")
        abs_ready = sem("abs_ready")
        expneg_ready = sem("expneg_ready")
        plus1_ready = sem("plus1_ready")
        log_ready = sem("log_ready")
        lost_ready = sem("lost_ready")
        log_added = sem("log_added")
        relu_ready = sem("relu_ready")
        dt_ready = sem("dt_ready")
        dtx_ready = sem("dtx_ready")
        b_filled = sem("b_filled")
        c_filled = sem("c_filled")
        c_copied = sem("c_copied")
        exp_done = sem("exp_done")
        dbx_done = sem("dbx_done")
        scan_done = sem("scan_done")
        prod_done = sem("prod_done")
        sum_done = sem("sum_done")
        skip_added = sem("skip_added")
        y_ready = sem("y_ready")
        stats_done = sem("stats_done")
        stored = [sem(f"stored{p}") for p in (0, 1)]

        def wait_filled(eng, name, m):
            b = 1 if name == "out" else bank_of[name]
            need(eng, filled[b], index(name, m) + 1)

        def wait_drained(eng, name, m):
            b = 1 if name == "out" else bank_of[name]
            need(eng, drained[b], index(name, m) + 1)

        def wait_bank(eng, name, m):
            b = 1 if name == "out" else bank_of[name]
            need(eng, drained[b], index(name, m))

        def token0(m):
            return m * -T + (CHUNKS - 1) * T if rev else m * T

        def run(eng, prepare, chunk, post):
            prepare(0, 0)
            chunk(0, 0, False)
            chunk(1, 1, False)
            with eng.Fori(1, CHUNKS // 2 - 1) as i:
                chunk(2 * i, 0, False)
                chunk(2 * i + 1, 1, False)
            chunk(CHUNKS - 2, 0, False)
            chunk(CHUNKS - 1, 1, True)
            post(CHUNKS - 1, 1)

        ctx.callback(clear_semaphores, nc, sems)
        block = ctx.enter_context(nc.Block())

        @block.sync
        def _(eng):
            eng.dma_start(w[:, :], w_dram).then_inc(w_loaded, 16)

            def load(m, p):
                start = token0(m)
                if layer3:
                    if not isinstance(m, int) or m >= 2:
                        wait_drained(eng, "mean", m - 2)
                    eng.dma_start(xin[p][:, 0:T], x_dram[:, bass.ds(start, T)]).then_inc(x_loaded[p], 16)
                else:
                    if not isinstance(m, int) or m >= 2:
                            wait_filled(eng, "gate1", m - 2)
                    eng.dma_start(xin[p][:, :], x_dram[:, bass.ds(start, T + 2)]).then_inc(x_loaded[p], 16)
                if rev:
                    if not isinstance(m, int) or m >= 2:
                            wait_drained(eng, "out", m - 2)
                    eng.dma_start(yadd[p][:, :], addend_dram[:, bass.ds(start, T)]).then_inc(add_loaded[p], 16)

            def store(m, p):
                start = token0(m)
                wait_drained(eng, "out", m)
                eng.dma_start(out_dram[:, bass.ds(start, T)], yout[p][:, :]).then_inc(stored[p], 16)

            load(0, 0)
            load(1, 1)
            load(2, 0)
            store(0, 0)
            with eng.Fori(1, CHUNKS // 2 - 1) as i:
                load(2 * i + 1, 1)
                store(2 * i - 1, 1)
                load(2 * i + 2, 0)
                store(2 * i, 0)
            load(CHUNKS - 1, 1)
            store(CHUNKS - 3, 1)
            store(CHUNKS - 2, 0)
            store(CHUNKS - 1, 1)
            if rev:
                eng.wait_ge(stats_done, CHUNKS + 1)
                eng.dma_start(stats_dram, aggr[:, :]).then_inc(stored[0], 16)
            eng.wait_ge(stored[0], 8 * CHUNKS + (16 if rev else 0))
            eng.wait_ge(stored[1], 8 * CHUNKS)

        @block.gpsimd
        def _(eng):
            make_identity(eng, ident, 128, zeroed, consts)
            eng.memset(ones[:, :], 1.0 / C).then_inc(consts, 1)
            eng.memset(select[:, :, :], 0.0).then_inc(zeroed, 1)
            if layer3:
                for p in (0, 1):
                    eng.memset(xn[p][:, 0:HALO], 0.0).then_inc(consts, 1)
            eng.memset(hs[:, :, 0:1] if rev else hs[:, :, T - 1:T], 0.0).then_inc(consts, 1)
            eng.wait_ge(zeroed, 2)
            turn = 2
            for part in range(3):
                if layer3:
                    for half in range(2):
                        view = select[:, 0:STATE, 64 * half:64 * half + 64]
                        eng.affine_select(out=view, in_=view, compare_op=ALU.not_equal, fill=1.0,
                                          base=-32 * part - 16 * half, pattern=[[-1, STATE], [0, 64]],
                                          channel_multiplier=1).then_inc(zeroed, 1)
                        turn += 1
                        eng.wait_ge(zeroed, turn)
                else:
                    eng.affine_select(out=select[:, :, :], in_=select[:, :, :], compare_op=ALU.not_equal,
                                      fill=1.0, base=-32 * part, pattern=[[-1, 32], [0, 128]],
                                      channel_multiplier=1).then_inc(zeroed, 1)
                    turn += 1
                    eng.wait_ge(zeroed, turn)

            def chunk(c, p, last):
                for u in range(UNITS):
                    g = c * UNITS + u
                    k = c * KB + u // PER
                    need(eng, scan_done, g + 1)
                    need(eng, c_copied, k + 1)
                    need(eng, sum_done, g - RING + 1)
                    eng.tensor_tensor(hc[:, u % RING, :], hs[:, u, :], cb[:, (u // PER) % RING, :],
                                      ALU.mult).then_inc(prod_done, 1)

            run(eng, lambda m, p: None, chunk, lambda m, p: None)

        ALL_CONSTS = 5 if layer3 else 3
        SELECT_MADE = 2 + (6 if layer3 else 3)

        @block.scalar
        def _(eng):
            eng.wait_ge(alog_min, 1)
            eng.activation(decay[:, :], decay[:, :], ACT.Exp).then_inc(alog_exp, 1)
            eng.wait_ge(wconv_ready, 2)

            eps_col = epst[:, 0:1]

            def silus(m, p):
                need(eng, y_ready, m - 1)
                for b in (0, 1):
                    wait_filled(eng, f"conv{b}", m)
                    eng.activation(xc[p][:, b, :], prep[b][:, :], ACT.Silu,
                                   bias=W["convb"][:, b:b + 1]).then_inc(drained[b], 1)
                for b in (0, 1):
                    wait_filled(eng, f"gate{b}", m)
                    eng.activation(zs[p][:, b, :], prep[b][:, :], ACT.Silu).then_inc(drained[b], 1)

            def split_hi(m, p, q):
                wait_filled(eng, f"bc{q}", m)
                need(eng, b_filled, KB * (m - 1))
                need(eng, c_filled, KB * (m - 1))
                eng.activation(bcs[p][:, q, :], prep[bank_of[f"bc{q}"]][0:96, :], ACT.Copy).then_inc(hi_ready, 1)

            def split_mid(m, p, q):
                n = m * NBC + q
                wait_drained(eng, f"bc{q}", m)
                eng.activation(bcs[p][32:64, q, :], rest[32:64, :], ACT.Copy).then_inc(mid_ready, 1)
                need(eng, lo_ready, n)
                eng.activation(mid[64:96, :], rest[64:96, :], ACT.Copy).then_inc(mid_ready, 1)

            def copy_dtr(m, p):
                wait_filled(eng, "dtr", m)
                if not isinstance(m, int) or m >= 1:
                    wait_filled(eng, "dt1", m - 1)
                eng.activation(dtr[:, :], prep[bank_of["dtr"]][0:32, :], ACT.Copy).then_inc(drained[1], 1)

            def dt_abs(m, p):
                need(eng, dt_ready, m)
                for b in (0, 1):
                    wait_filled(eng, f"dt{b}", m)
                    eng.activation(sp[:, b, :], prep[b][:, :], ACT.Abs,
                                   bias=W["bdt"][:, b:b + 1]).then_inc(abs_ready, 1)

            def dt_log(m, p):
                need(eng, abs_ready, 2 * m + 2)
                eng.activation(sp[:, :, :], sp[:, :, :], ACT.Exp, scale=-1.0).then_inc(expneg_ready, 1)
                need(eng, expneg_ready, m + 1)
                eng.activation(sp1[:, :, :], sp[:, :, :], ACT.Identity, bias=1.0).then_inc(plus1_ready, 1)
                need(eng, plus1_ready, m + 1)
                eng.activation(spl[:, :, :], sp1[:, :, :], ACT.Ln).then_inc(log_ready, 1)

            def square(m, p):
                wait_drained(eng, "mean", m)
                if not isinstance(m, int) or m >= 1:
                    need(eng, xhat_ready, m)
                eng.activation(sq[:, :], cen[:, :], ACT.Square).then_inc(sq_ready, 1)

            def rstd(m, p):
                wait_filled(eng, "var", m)
                eng.activation(sq[:, :], prep[1][:, :], ACT.Ln, bias=eps_col).then_inc(lnvar_ready, 1)
                need(eng, lnvar_ready, m + 1)
                eng.activation(sq[:, :], sq[:, :], ACT.Exp, scale=-0.5).then_inc(drained[1], 1)

            def evacuate(m, p):
                wait_filled(eng, "out", m)
                need(eng, stored[p], 8 * (m - p))
                eng.activation(yout[p][:, :], prep[1][:, :], ACT.Copy).then_inc(drained[1], 1)

            steps = {}
            if layer3:
                steps = {6: [square], 8: [rstd], 11: [silus]}
                for at_unit, q in ((14, 0), (18, 2)):
                    steps[at_unit] = [lambda m, p, q=q: split_hi(m, p, q)]
                    steps[at_unit + 1] = [lambda m, p, q=q: split_mid(m, p, q),
                                          lambda m, p, q=q: split_hi(m, p, q + 1)]
                    steps[at_unit + 2] = [lambda m, p, q=q: split_mid(m, p, q + 1)]
                steps[22] = [copy_dtr]
                steps[24] = [dt_abs, dt_log]
            else:
                steps = {6: [silus],
                         11: [lambda m, p: split_hi(m, p, 0), lambda m, p: split_mid(m, p, 0), copy_dtr],
                         15: [dt_abs, dt_log]}

            def prepare(m, p):
                for pos in sorted(steps):
                    for step in steps[pos]:
                        step(m, p)

            def chunk(c, p, last):
                for u in range(UNITS):
                    g = c * UNITS + u
                    k = c * KB + u // PER
                    if u == 0:
                        need(eng, dt_ready, c + 1)
                    need(eng, scan_done, g - RING + 1)
                    eng.activation(da[:, u % RING, :], dt[p][:, u % 2, :], ACT.Exp,
                                   scale=decay[:, u:u + 1]).then_inc(exp_done, 1)
                    if u % PER == 0:
                        need(eng, c_filled, k + 1)
                        need(eng, prod_done, (k - RING + 1) * PER)
                        eng.activation(cb[:, (u // PER) % RING, :], psC[(u // PER) % 2][:, :],
                                       ACT.Copy).then_inc(c_copied, 1)
                    if u == 5 and kind == "forward" and not (isinstance(c, int) and c == 0):
                        evacuate(c - 1, 1 - p)
                    if not last:
                        for step in steps.get(u, []):
                            step(c + 1, 1 - p)

            run(eng, prepare, chunk, (lambda m, p: evacuate(m, p)) if kind == "forward" else (lambda m, p: None))

        @block.vector
        def _(eng):
            eng.wait_ge(w_loaded, 16)
            eng.tensor_scalar(decay[:, :], W["alog"], 80.0, None, ALU.min).then_inc(alog_min, 1)
            eng.wait_ge(alog_exp, 1)
            eng.tensor_scalar(decay[:, :], decay[:, :], -1.0, None, ALU.mult).then_inc(wconv_ready, 1)
            eng.memset(epst[:, :], EPS).then_inc(wconv_ready, 1)
            for k in range(TAPS):
                eng.tensor_tensor(wconv[:, k, :, :], W["win"].rearrange("p (b m) -> p b m", b=2),
                                  W["tapw"][:, 256 * k:256 * k + 256].rearrange("p (b m) -> p b m", b=2),
                                  ALU.mult).then_inc(wconv_ready, 1)
            eng.wait_ge(consts, ALL_CONSTS)

            def center(m, p):
                wait_filled(eng, "mean", m)
                need(eng, x_loaded[p], 8 * (m - p) + 16)
                need(eng, xhat_ready, m)
                need(eng, sq_ready, m)
                eng.tensor_tensor(cen[:, :], xin[p][:, 0:T], prep[0][:, :], ALU.subtract).then_inc(drained[0], 1)

            def normalize(m, p):
                wait_drained(eng, "var", m)
                eng.tensor_tensor(cen[:, :], cen[:, :], sq[:, :], ALU.mult).then_inc(rstd_ready, 1)
                if not isinstance(m, int) or m >= 2:
                    wait_filled(eng, "gate1", m - 2)
                    wait_drained(eng, "out", m - 2)
                if not isinstance(m, int) or m >= 1:
                    eng.tensor_copy(xn[p][:, 0:HALO], xn[1 - p][:, T:T + HALO]).then_inc(halo_ready, 1)
                need(eng, rstd_ready, m + 1)
                eng.tensor_scalar(xn[p][:, HALO:HALO + T], cen[:, :], W["ln_g"], W["ln_b"],
                                  ALU.mult, ALU.add).then_inc(xhat_ready, 1)

            def split_rest(m, p, q):
                n = m * NBC + q
                need(eng, hi_ready, n + 1)
                need(eng, lo_ready, n)
                need(eng, mid_ready, 2 * n)
                b = bank_of[f"bc{q}"]
                eng.tensor_tensor(rest[:, :], prep[b][0:96, :], bcs[p][:, q, :],
                                  ALU.subtract).then_inc(drained[b], 1)

            def split_lo(m, p, q):
                n = m * NBC + q
                need(eng, mid_ready, 2 * n + 2)
                eng.tensor_tensor(bcs[p][64:96, q, :], rest[64:96, :], mid[64:96, :],
                                  ALU.subtract).then_inc(lo_ready, 1)

            def relu_dt(m, p):
                need(eng, exp_done, UNITS * (m - 1))
                for b in (0, 1):
                    need(eng, abs_ready, 2 * m + 1 + b)
                    eng.tensor_scalar(dt[p][:, b, :], prep[b][:, :], W["bdt"][:, b:b + 1], 0.0,
                                      ALU.add, ALU.max).then_inc(drained[b], 1)

            def lost_part(m, p):
                need(eng, plus1_ready, m + 1)
                eng.scalar_tensor_tensor(sp[:, :, :], sp1[:, :, :], -1.0, sp[:, :, :],
                                         ALU.add, ALU.subtract).then_inc(lost_ready, 1)

            def add_log(m, p):
                need(eng, log_ready, m + 1)
                need(eng, lost_ready, m + 1)
                eng.tensor_tensor(spl[:, :, :], spl[:, :, :], sp[:, :, :], ALU.subtract).then_inc(log_added, 1)

            def add_relu(m, p):
                need(eng, log_added, m + 1)
                for b in (0, 1):
                    wait_drained(eng, f"dt{b}", m)
                eng.tensor_tensor(dt[p][:, :, :], dt[p][:, :, :], spl[:, :, :], ALU.add).then_inc(dt_ready, 1)

            def scale_x(m, p):
                need(eng, dt_ready, m + 1)
                wait_drained(eng, "conv0", m)
                wait_drained(eng, "conv1", m)
                eng.tensor_tensor(dtx[p][:, :, :], dt[p][:, :, :], xc[p][:, :, :], ALU.mult).then_inc(dtx_ready, 1)

            def skip(m, p):
                need(eng, sum_done, UNITS * (m + 1))
                if not isinstance(m, int) or m >= 1:
                    wait_filled(eng, "out", m - 1)
                for b in (0, 1):
                    eng.scalar_tensor_tensor(yv[:, b, :], xc[p][:, b, :], W["dskip"][:, b:b + 1],
                                             psY[b][:, :], ALU.mult, ALU.add).then_inc(skip_added, 1)

            def gate(m, p):
                need(eng, skip_added, 2 * m + 2)
                wait_drained(eng, "gate0", m)
                wait_drained(eng, "gate1", m)
                eng.tensor_tensor(yv[:, :, :], yv[:, :, :], zs[p][:, :, :], ALU.mult).then_inc(y_ready, 1)

            def add_out(m, p):
                wait_filled(eng, "out", m)
                need(eng, stored[p], 8 * (m - p))
                if rev:
                    need(eng, add_loaded[p], 8 * (m - p) + 16)
                    other = yadd[p][:, :]
                else:
                    other = xn[p][:, HALO:HALO + T]
                eng.tensor_tensor(yout[p][:, :], other, prep[1][:, :], ALU.add).then_inc(drained[1], 1)
                wait_drained(eng, "out", m)
                if rev:
                    eng.bn_stats(stats[:, m, :] if isinstance(m, int) else stats[:, bass.ds(m, 1), :],
                                 yout[p][:, :]).then_inc(stats_done, 1)

            if layer3:
                steps = {6: [center], 9: [normalize], 15: [lambda m, p: split_rest(m, p, 0)],
                         16: [lambda m, p: split_lo(m, p, 0), lambda m, p: split_rest(m, p, 1)],
                         17: [lambda m, p: split_lo(m, p, 1)],
                         19: [lambda m, p: split_rest(m, p, 2)],
                         20: [lambda m, p: split_lo(m, p, 2), lambda m, p: split_rest(m, p, 3)],
                         21: [lambda m, p: split_lo(m, p, 3)],
                         25: [relu_dt], 26: [lost_part], 28: [add_log], 29: [add_relu], 31: [scale_x]}
            else:
                steps = {12: [lambda m, p: split_rest(m, p, 0)], 14: [lambda m, p: split_lo(m, p, 0)],
                         17: [relu_dt], 18: [lost_part], 20: [add_log], 21: [add_relu], 23: [scale_x]}

            def prepare(m, p):
                for pos in sorted(steps):
                    for step in steps[pos]:
                        step(m, p)

            def product(c, p, u):
                k = c * KB + u // PER
                need(eng, b_filled, k + 1)
                if u == 0:
                    need(eng, dtx_ready, c + 1)
                need(eng, scan_done, c * UNITS + u - RING + 1)
                eng.tensor_tensor(dbx[:, u % RING, :], dtx[p][:, u % 2, :], psB[(u // PER) % 2][:, :],
                                  ALU.mult).then_inc(dbx_done, 1)

            def scan(c, p, u):
                g = c * UNITS + u
                need(eng, exp_done, g + 1)
                need(eng, dbx_done, g + 1)
                need(eng, prod_done, g - UNITS + 1)
                need(eng, scan_done, g - UNITS + 1)
                if rev:
                    eng.tensor_tensor_scan(hs[:, u, ::-1], da[:, u % RING, ::-1], dbx[:, u % RING, ::-1],
                                           hs[:, u, 0:1], ALU.mult, ALU.add).then_inc(scan_done, 1)
                else:
                    eng.tensor_tensor_scan(hs[:, u, :], da[:, u % RING, :], dbx[:, u % RING, :],
                                           hs[:, u, T - 1:T], ALU.mult, ALU.add).then_inc(scan_done, 1)

            def chunk(c, p, last):
                first = isinstance(c, int) and c == 0
                for u in range(UNITS):
                    product(c, p, u)
                    if u > 0:
                        scan(c, p, u - 1)
                    if not first:
                        if u == 1:
                            skip(c - 1, 1 - p)
                        if u == 3:
                            gate(c - 1, 1 - p)
                        if u == 5 and kind != "forward":
                            add_out(c - 1, 1 - p)
                    if not last:
                        for step in steps.get(u, []):
                            step(c + 1, 1 - p)
                scan(c, p, UNITS - 1)

            def post(m, p):
                skip(m, p)
                gate(m, p)
                if kind != "forward":
                    add_out(m, p)
                if rev:
                    eng.wait_ge(stats_done, CHUNKS)
                    eng.bn_aggr(aggr[:, :], stats[:, :, :].rearrange("p n s -> p (n s)")).then_inc(stats_done, 1)

            run(eng, prepare, chunk, post)

        @block.tensor
        def _(eng):
            eng.wait_ge(w_loaded, 16)
            eng.wait_ge(wconv_ready, 2 + TAPS)
            eng.wait_ge(consts, ALL_CONSTS)
            eng.wait_ge(zeroed, SELECT_MADE)

            def source(p, shift):
                if layer3:
                    return xn[p][:, HALO - shift:HALO - shift + T]
                first = 1 + shift if rev else 1 - shift
                return xin[p][:, first:first + T]

            def mean(m, p):
                need(eng, x_loaded[p], 8 * (m - p) + 16)
                wait_bank(eng, "mean", m)
                eng.matmul(prep[0][:, :], ones[:, :], xin[p][:, 0:T], start=True, stop=True).then_inc(filled[0], 1)

            def var(m, p):
                need(eng, sq_ready, m + 1)
                wait_bank(eng, "var", m)
                eng.matmul(prep[1][:, :], ones[:, :], sq[:, :], start=True, stop=True).then_inc(filled[1], 1)

            def conv(m, p):
                if layer3:
                    need(eng, xhat_ready, m + 1)
                    if not isinstance(m, int) or m >= 1:
                        need(eng, halo_ready, m)
                else:
                    need(eng, x_loaded[p], 8 * (m - p) + 16)
                for b in (0, 1):
                    wait_bank(eng, f"conv{b}", m)
                    for k in range(TAPS):
                        mm = eng.matmul(prep[b][:, :], wconv[:, k, b, :], source(p, TAPS - 1 - k),
                                        start=(k == 0), stop=(k == TAPS - 1))
                    mm.then_inc(filled[b], 1)

            def gates(m, p):
                for b in (0, 1):
                    wait_bank(eng, f"gate{b}", m)
                    eng.matmul(prep[b][:, :], W["wz"][:, 128 * b:128 * b + 128], source(p, 0),
                               start=True, stop=True).then_inc(filled[b], 1)

            def bc(m, p, q):
                name = f"bc{q}"
                wait_bank(eng, name, m)
                out = prep[bank_of[name]][0:96, :]
                if layer3:
                    weight = W["wb"] if q < 2 else W["wc"]
                    eng.matmul(out, weight, xc[p][:, q % 2, :], start=True, stop=True).then_inc(filled[bank_of[name]], 1)
                else:
                    for b in (0, 1):
                        mm = eng.matmul(out, W["wbc"][:, 96 * b:96 * b + 96], xc[p][:, b, :],
                                        start=(b == 0), stop=(b == 1))
                    mm.then_inc(filled[0], 1)

            def rank_rows(m, p):
                wait_bank(eng, "dtr", m)
                for b in (0, 1):
                    mm = eng.matmul(prep[1][0:32, :], W["wdtr"][:, 32 * b:32 * b + 32], xc[p][:, b, :],
                                    start=(b == 0), stop=(b == 1))
                mm.then_inc(filled[1], 1)

            def dts(m, p):
                wait_drained(eng, "dtr", m)
                for b in (0, 1):
                    wait_bank(eng, f"dt{b}", m)
                    eng.matmul(prep[b][:, :], W["wdt"][0:32, 128 * b:128 * b + 128], dtr[:, :],
                               start=True, stop=True).then_inc(filled[b], 1)

            def project_out(m, p):
                need(eng, y_ready, m + 1)
                wait_bank(eng, "out", m)
                for b in (0, 1):
                    mm = eng.matmul(prep[1][:, :], W["wout"][:, 128 * b:128 * b + 128], yv[:, b, :],
                                    start=(b == 0), stop=(b == 1))
                mm.then_inc(filled[1], 1)

            if layer3:
                steps = {5: [mean], 7: [var], 10: [conv], 11: [gates],
                         13: [lambda m, p: bc(m, p, 0), lambda m, p: bc(m, p, 1)],
                         17: [lambda m, p: bc(m, p, 2), lambda m, p: bc(m, p, 3)],
                         21: [rank_rows], 23: [dts]}
            else:
                steps = {5: [conv], 6: [gates], 10: [lambda m, p: bc(m, p, 0), rank_rows], 14: [dts]}

            def prepare(m, p):
                for pos in sorted(steps):
                    for step in steps[pos]:
                        step(m, p)

            LAG = 3

            def sum_state(c, p, u):
                g = c * UNITS + u
                need(eng, prod_done, g + 1)
                if u == 0:
                    need(eng, skip_added, 2 * c)
                eng.matmul(psY[u % 2][:, :], ident[:, :], hc[:, u % RING, :], start=(u < 2),
                           stop=(u >= UNITS - 2)).then_inc(sum_done, 1)

            def chunk(c, p, last):
                for u in range(UNITS):
                    if u % PER == 0:
                        k = c * KB + u // PER
                        kk = u // PER
                        if u == 0:
                            need(eng, lo_ready, (c + 1) * NBC)
                            need(eng, mid_ready, 2 * (c + 1) * NBC)
                        qb, qc = (u % 2, 2 + u % 2) if layer3 else (0, 0)
                        rb, rc = (u // 2, u // 2) if layer3 else (kk, STATE + kk)
                        need(eng, dbx_done, (k - 1) * PER)
                        eng.matmul(psB[kk % 2][:, :], select[:, rb, :], bcs[p][:, qb, :],
                                   start=True, stop=True).then_inc(b_filled, 1)
                        need(eng, c_copied, k - 1)
                        eng.matmul(psC[kk % 2][:, :], select[:, rc, :], bcs[p][:, qc, :],
                                   start=True, stop=True).then_inc(c_filled, 1)
                    if u >= LAG:
                        sum_state(c, p, u - LAG)
                    if u == 4 and not (isinstance(c, int) and c == 0):
                        project_out(c - 1, 1 - p)
                    if not last:
                        for step in steps.get(u, []):
                            step(c + 1, 1 - p)
                for u in range(UNITS - LAG, UNITS):
                    sum_state(c, p, u)

            run(eng, prepare, chunk, project_out)



def attention_phase(nc, vertical, x_dram, w_dram, out_dram):
    tag = "av" if vertical else "ah"
    at, width = offsets(ATTN_COLS)
    BLOCKS = LINES // BLOCK

    with ExitStack() as ctx:
        def sb(name, shape, dt=F32):
            return ctx.enter_context(nc.sbuf_tensor(f"{tag}_{name}", shape, dt))

        def pb(name, shape):
            return ctx.enter_context(nc.psum_tensor(f"{tag}_{name}", shape, F32))

        sems = []

        def sem(name):
            sems.append(ctx.enter_context(nc.semaphore(f"{tag}_{name}")))
            return sems[-1]

        w = sb("w", [C, width])
        W = {n: w[:, a:b] for n, (a, b) in at.items()}
        wqs = sb("wqs", [C, 2, 128])
        bqs = sb("bqs", [C, 2])
        cq = sb("cq", [C, 2, SIDE])
        ident = sb("ident", [C, 128])
        zero_row = sb("zero_row", [C, SIDE])
        shape = [C, SIDE, BLOCK] if vertical else [C, BLOCK, SIDE]
        xb = [sb(f"xb{p}", shape) for p in (0, 1)]
        ob = [sb(f"ob{p}", shape) for p in (0, 1)]
        xr = [sb(f"xr{p}", [C, SIDE]) for p in (0, 1)]
        qa = [sb(f"qa{p}", [C, 2, SIDE]) for p in (0, 1)]
        qm = [sb(f"qm{p}", [C, 2, SIDE]) for p in (0, 1)]
        ka = [sb(f"ka{p}", [C, 2, SIDE]) for p in (0, 1)]
        va = [sb(f"va{p}", [HALF, 2, HEADS, HD + 1]) for p in (0, 1)]
        mx = [sb(f"mx{p}", [HALF, 2, 2, 128]) for p in (0, 1)]
        pt = [sb(f"pt{p}", [HALF, 8, 2, SIDE]) for p in (0, 1)]
        rec = sb("rec", [HALF, 2, HEADS, 1])
        on = [sb(f"on{p}", [HALF, 2, C]) for p in (0, 1)]
        obuf = [sb(f"obuf{p}", [C, SIDE]) for p in (0, 1)]

        psS = [pb(f"psS{b}", [HALF, 2, SIDE]) for b in (0, 1)]
        psT = [pb(f"psT{b}", [HALF, 2, SIDE]) for b in (0, 1)]
        psQK = pb("psQK", [C, 2, SIDE])
        psV = pb("psV", [HALF, 2, C])
        psM = pb("psM", [C, 2, SIDE])
        psOX = pb("psOX", [C, 512])
        NUM = HEADS * (HD + 1)
        psO = psOX[0:HALF, 0:2 * NUM].rearrange("p (a h e) -> p a h e", a=2, h=HEADS)
        psX = psOX[:, 2 * NUM:2 * NUM + SIDE]

        w_loaded = sem("w_loaded")
        zeroed = sem("zeroed")
        consts = sem("consts")
        scaled = sem("scaled")
        blk_loaded = [sem(f"blk_loaded{p}") for p in (0, 1)]
        blk_stored = [sem(f"blk_stored{p}") for p in (0, 1)]
        edge_stored = sem("edge_stored")
        line_in = sem("line_in")
        q_filled = sem("q_filled")
        k_filled = sem("k_filled")
        v_filled = sem("v_filled")
        q_ready = sem("q_ready")
        k_ready = sem("k_ready")
        v_ready = sem("v_ready")
        s_filled = sem("s_filled")
        max_ready = sem("max_ready")
        m_filled = sem("m_filled")
        qm_ready = sem("qm_ready")
        t_filled = sem("t_filled")
        p_ready = sem("p_ready")
        pv_done = sem("pv_done")
        rec_ready = sem("rec_ready")
        norm_done = sem("norm_done")
        x_filled = sem("x_filled")
        obuf_ready = sem("obuf_ready")
        line_out = sem("line_out")

        def run(eng, start, step, finish):
            start()
            step(0, 0, False)
            step(1, 1, False)
            with eng.Fori(1, LINES // 2 - 1) as i:
                step(2 * i, 0, False)
                step(2 * i + 1, 1, False)
            step(LINES - 2, 0, False)
            step(LINES - 1, 1, True)
            finish()

        ctx.callback(clear_semaphores, nc, sems)
        block = ctx.enter_context(nc.Block())

        @block.sync
        def _(eng):
            eng.dma_start(w[:, :], w_dram).then_inc(w_loaded, 16)

            def part(dram, b, first_row):
                if vertical:
                    return dram[:, first_row:first_row + SIDE, b * BLOCK:(b + 1) * BLOCK]
                return dram[:, first_row + b * BLOCK:first_row + (b + 1) * BLOCK, :]

            def load(b):
                need(eng, line_in, BLOCK * (b - 1))
                eng.dma_start(xb[b % 2][:, :, :], part(x_dram, b, 0)).then_inc(blk_loaded[b % 2], 16)

            load(0)
            load(1)
            eng.wait_ge(consts, 2)
            eng.dma_start(out_dram[:, 0, :], zero_row[:, :]).then_inc(edge_stored, 16)
            eng.dma_start(out_dram[:, SIDE + 1, :], zero_row[:, :]).then_inc(edge_stored, 16)
            for b in range(BLOCKS):
                if b + 2 < BLOCKS:
                    load(b + 2)
                eng.wait_ge(line_out, BLOCK * (b + 1))
                eng.dma_start(part(out_dram, b, 1), ob[b % 2][:, :, :]).then_inc(blk_stored[b % 2], 16)
            eng.wait_ge(edge_stored, 32)
            for p in (0, 1):
                eng.wait_ge(blk_stored[p], 16 * (BLOCKS // 2))

        @block.gpsimd
        def _(eng):
            make_identity(eng, ident, 128, zeroed, consts)
            eng.memset(zero_row[:, :], 0.0).then_inc(consts, 1)
            for p in (0, 1):
                eng.memset(mx[p][:, :, :, :], 0.0).then_inc(consts, 1)
                eng.memset(va[p][:, :, :, HD:HD + 1], 1.0).then_inc(consts, 1)

            def line(tile, r):
                at_r = slice(r, r + 1) if isinstance(r, int) else bass.ds(r, 1)
                if vertical:
                    return tile[:, :, at_r].rearrange("c s r -> c (s r)")
                return tile[:, at_r, :].rearrange("c r s -> c (r s)")

            def take(m, p, tile, r):
                need(eng, k_filled, m - 1)
                eng.tensor_copy(xr[p][:, :], line(tile, r)).then_inc(line_in, 1)

            def put(m, p, tile, r):
                need(eng, obuf_ready, m + 1)
                eng.tensor_copy(line(tile, r), obuf[p][:, :]).then_inc(line_out, 1)

            def one_block(b):
                n0, buf, last = b * BLOCK, b % 2, b == BLOCKS - 1
                need(eng, blk_stored[buf], 16 * (b // 2))
                with eng.Fori(0, BLOCK // 2 - 1) as k:
                    for j in (0, 1):
                        take(n0 + 2 * k + j + 2, j, xb[buf], 2 * k + j + 2)
                        put(n0 + 2 * k + j, j, ob[buf], 2 * k + j)
                if not last:
                    need(eng, blk_loaded[1 - buf], 16 * ((b + 1) // 2) + 16)
                for j in (0, 1):
                    if not last:
                        take(n0 + BLOCK + j, j, xb[1 - buf], j)
                    put(n0 + BLOCK - 2 + j, j, ob[buf], BLOCK - 2 + j)

            eng.wait_ge(blk_loaded[0], 16)
            take(0, 0, xb[0], 0)
            take(1, 1, xb[0], 1)
            for b in range(BLOCKS):
                one_block(b)

        @block.scalar
        def _(eng):
            eng.wait_ge(w_loaded, 16)
            eng.wait_ge(consts, 6)

            def values(m, p):
                need(eng, v_filled, m + 1)
                need(eng, pv_done, m - 1)
                eng.activation(va[p][:, :, :, 0:HD], psV[:, :, :].rearrange("p a (h e) -> p a h e", h=HEADS),
                               ACT.Copy).then_inc(v_ready, 1)

            def finished(m, p):
                need(eng, x_filled, m + 1)
                need(eng, line_out, m - 1)
                eng.activation(obuf[p][:, :], psX, ACT.Identity, bias=W["bv"]).then_inc(obuf_ready, 1)

            def step(n, p, last):
                if not (isinstance(n, int) and n == 0):
                    finished(n - 1, 1 - p)
                if not last:
                    values(n + 1, 1 - p)
                for u in range(8):
                    need(eng, t_filled, 8 * n + u + 1)
                    if u == 0:
                        need(eng, pv_done, n - 1)
                    eng.activation(pt[p][:, u, :, :], psT[u % 2][:, :, :], ACT.Exp).then_inc(p_ready, 1)

            run(eng, lambda: values(0, 0), step, lambda: finished(LINES - 1, 1))

        @block.vector
        def _(eng):
            SCALE = float(HD) ** -0.5
            eng.wait_ge(w_loaded, 16)
            eng.tensor_scalar(wqs[:, :, :], W["wq"].rearrange("c (t m) -> c t m", t=2), SCALE, None,
                              ALU.mult).then_inc(scaled, 1)
            eng.tensor_scalar(bqs[:, :], W["bq"], SCALE, None, ALU.mult).then_inc(scaled, 1)
            eng.wait_ge(scaled, 2)
            for t in (0, 1):
                eng.tensor_scalar(cq[:, t, :], W["onehot"], bqs[:, t:t + 1], None, ALU.add).then_inc(scaled, 1)
            eng.wait_ge(scaled, 4)
            eng.wait_ge(consts, 6)
            ck = W["ck"].rearrange("c (t s) -> c t s", t=2)

            def queries(m, p):
                need(eng, q_filled, m + 1)
                need(eng, s_filled, 8 * (m - 1))
                eng.tensor_tensor(qa[p][:, :, :], cq[:, :, :], psQK[:, :, :], ALU.add).then_inc(q_ready, 1)

            def keys(m, p):
                need(eng, k_filled, m + 1)
                need(eng, t_filled, 8 * (m - 1))
                eng.tensor_tensor(ka[p][:, :, :], ck, psQK[:, :, :], ALU.add).then_inc(k_ready, 1)

            def maxima(n, p):
                need(eng, m_filled, n - 1)
                for u in range(8):
                    j, half = u // 2, u % 2
                    row = 32 * j + MAXROW
                    need(eng, s_filled, 8 * n + u + 1)
                    eng.tensor_reduce(mx[p][:, half, :, row:row + 1], psS[u % 2][:, :, :], AX_X, ALU.max,
                                      negate=True).then_inc(max_ready, 1)

            def normalize(m, p):
                need(eng, pv_done, m + 1)
                need(eng, norm_done, m)
                eng.reciprocal(rec[:, :, :, :], psO[:, :, :, HD:HD + 1]).then_inc(rec_ready, 1)
                need(eng, rec_ready, m + 1)
                need(eng, x_filled, m - 1)
                eng.tensor_tensor(on[p][:, :, :].rearrange("p a (h e) -> p a h e", h=HEADS),
                                  rec[:, :, :, :].broadcast_to([HALF, 2, HEADS, HD]), psO[:, :, :, 0:HD],
                                  ALU.mult).then_inc(norm_done, 1)

            def subtract_max(n, p):
                need(eng, m_filled, n + 1)
                need(eng, t_filled, 8 * (n - 1))
                eng.tensor_tensor(qm[p][:, :, :], qa[p][:, :, :], psM[:, :, :], ALU.add).then_inc(qm_ready, 1)

            def start():
                queries(0, 0)
                keys(0, 0)

            def step(n, p, last):
                maxima(n, p)
                if not (isinstance(n, int) and n == 0):
                    normalize(n - 1, 1 - p)
                subtract_max(n, p)
                if not last:
                    queries(n + 1, 1 - p)
                    keys(n + 1, 1 - p)

            run(eng, start, step, lambda: normalize(LINES - 1, 1))

        @block.tensor
        def _(eng):
            eng.wait_ge(scaled, 4)
            eng.wait_ge(consts, 6)

            def project(m, p):
                need(eng, line_in, m + 1)
                need(eng, k_ready, m)
                for t in (0, 1):
                    mm = eng.matmul(psQK[:, t, :], wqs[:, t, :], xr[p][:, :], start=True, stop=True)
                mm.then_inc(q_filled, 1)
                need(eng, v_ready, m)
                for a in (0, 1):
                    mm = eng.matmul(psV[:, a, :], xr[p][:, HALF * a:HALF * a + HALF], W["wv"],
                                    start=True, stop=True)
                mm.then_inc(v_filled, 1)
                need(eng, q_ready, m + 1)
                for t in (0, 1):
                    mm = eng.matmul(psQK[:, t, :], W["wk"][:, 128 * t:128 * t + 128], xr[p][:, :],
                                    start=True, stop=True)
                mm.then_inc(k_filled, 1)

            def scores(n, p):
                need(eng, q_ready, n + 1)
                need(eng, k_ready, n + 1)
                for u in range(8):
                    j, half = u // 2, u % 2
                    need(eng, max_ready, 8 * n + u - 1)
                    for t in (0, 1):
                        mm = eng.matmul(psS[u % 2][:, t, :],
                                        qa[p][32 * j:32 * j + 32, t, HALF * half:HALF * half + HALF],
                                        ka[p][32 * j:32 * j + 32, t, :], start=True, stop=True)
                    mm.then_inc(s_filled, 1)

            def transpose_max(n, p):
                need(eng, max_ready, 8 * n + 8)
                need(eng, qm_ready, n)
                for half in (0, 1):
                    for t in (0, 1):
                        mm = eng.matmul(psM[:, t, HALF * half:HALF * half + HALF], mx[p][:, half, t, :],
                                        ident[0:HALF, 0:HALF], start=True, stop=True)
                mm.then_inc(m_filled, 1)

            def scores_t(n, p):
                need(eng, qm_ready, n + 1)
                for u in range(8):
                    j, half = u // 2, u % 2
                    need(eng, p_ready, 8 * n + u - 1)
                    for t in (0, 1):
                        mm = eng.matmul(psT[u % 2][:, t, :],
                                        ka[p][32 * j:32 * j + 32, t, HALF * half:HALF * half + HALF],
                                        qm[p][32 * j:32 * j + 32, t, :], start=True, stop=True)
                    mm.then_inc(t_filled, 1)

            def outputs(m, p):
                need(eng, p_ready, 8 * m + 8)
                need(eng, v_ready, m + 1)
                need(eng, norm_done, m)
                for a in (0, 1):
                    for h in range(HEADS):
                        t, j = h // 4, h % 4
                        for half in (0, 1):
                            mm = eng.matmul(psO[:, a, h, :],
                                            pt[p][:, 2 * j + half, t, HALF * a:HALF * a + HALF],
                                            va[p][:, half, h, :], start=(half == 0), stop=(half == 1))
                mm.then_inc(pv_done, 1)

            def to_channels(m, p):
                need(eng, norm_done, m + 1)
                need(eng, obuf_ready, m)
                for a in (0, 1):
                    mm = eng.transpose(psX[:, HALF * a:HALF * a + HALF], on[p][:, a, :],
                                       ident[0:HALF, 0:HALF])
                mm.then_inc(x_filled, 1)

            def step(n, p, last):
                first = isinstance(n, int) and n == 0
                scores(n, p)
                if not first:
                    outputs(n - 1, 1 - p)
                transpose_max(n, p)
                if not first:
                    to_channels(n - 1, 1 - p)
                if not last:
                    project(n + 1, 1 - p)
                scores_t(n, p)

            def finish():
                outputs(LINES - 1, 1)
                to_channels(LINES - 1, 1)

            run(eng, lambda: project(0, 0), step, finish)



def lepe_phase(nc, h_dram, v_dram, w_dram, out_dram):
    ROWS = 8
    PAIRS = ROWS // 2
    STEPS = SIDE // ROWS
    WIDE = SIDE + 2
    at, width = offsets(LEPE_COLS)

    with ExitStack() as ctx:
        def sb(name, shape):
            return ctx.enter_context(nc.sbuf_tensor(f"le_{name}", shape, F32))

        def pb(name, shape):
            return ctx.enter_context(nc.psum_tensor(f"le_{name}", shape, F32))

        sems = []

        def sem(name):
            sems.append(ctx.enter_context(nc.semaphore(f"le_{name}")))
            return sems[-1]

        w = sb("w", [C, width])
        W = {n: w[:, a:b] for n, (a, b) in at.items()}
        ident = sb("ident", [C, 128])
        taps = sb("taps", [C, 9, 128])
        hin = [sb(f"hin{p}", [C, ROWS + 2, WIDE]) for p in (0, 1)]
        vin = [sb(f"vin{p}", [C, ROWS + 2, WIDE]) for p in (0, 1)]
        acc = sb("acc", [C, ROWS, SIDE])
        gh = sb("gh", [C, ROWS, SIDE])
        gv = sb("gv", [C, ROWS, SIDE])
        both = sb("both", [C, ROWS, SIDE])
        total = sb("total", [C, ROWS, SIDE])
        xo = [sb(f"xo{p}", [C, ROWS * SIDE]) for p in (0, 1)]
        edge = sb("edge", [C, 1])
        psH = [pb(f"psH{b}", [C, 2, SIDE]) for b in (0, 1)]
        psP = [pb(f"psP{b}", [C, 2 * SIDE]) for b in (0, 1)]

        w_loaded = sem("w_loaded")
        zeroed = sem("zeroed")
        consts = sem("consts")
        taps_ready = sem("taps_ready")
        loaded = [sem(f"loaded{p}") for p in (0, 1)]
        stored = [sem(f"stored{p}") for p in (0, 1)]
        edge_stored = sem("edge_stored")
        h_filled = sem("h_filled")
        gh_ready = sem("gh_ready")
        tap_done = sem("tap_done")
        gv_ready = sem("gv_ready")
        both_ready = sem("both_ready")
        halfsum_ready = sem("halfsum_ready")
        total_ready = sem("total_ready")
        p_filled = sem("p_filled")
        out_ready = sem("out_ready")

        def run(eng, step):
            step(0, 0)
            step(1, 1)
            with eng.Fori(1, STEPS // 2) as i:
                step(2 * i, 0)
                step(2 * i + 1, 1)

        ctx.callback(clear_semaphores, nc, sems)
        block = ctx.enter_context(nc.Block())

        @block.sync
        def _(eng):
            eng.dma_start(w[:, :], w_dram).then_inc(w_loaded, 16)
            eng.wait_ge(consts, 6)
            eng.dma_start(out_dram[:, 0:1], edge[:, :], allow_slow_non_contiguous=True).then_inc(edge_stored, 16)
            eng.dma_start(out_dram[:, TOKENS + 1:TOKENS + 2], edge[:, :], allow_slow_non_contiguous=True).then_inc(edge_stored, 16)

            def load(n, p):
                need(eng, h_filled, PAIRS * (n - 1))
                need(eng, total_ready, n - 1)
                for tile, dram in ((hin, h_dram), (vin, v_dram)):
                    eng.dma_start(tile[p][:, :, 1:1 + SIDE],
                                  dram[:, bass.ds(ROWS * n, ROWS + 2), :]).then_inc(loaded[p], 16)

            def store(n, p):
                need(eng, out_ready, PAIRS * (n + 1))
                eng.dma_start(out_dram[:, bass.ds(ROWS * SIDE * n + 1, ROWS * SIDE)],
                              xo[p][:, :]).then_inc(stored[p], 16)

            load(0, 0)
            load(1, 1)
            with eng.Fori(0, STEPS // 2 - 1) as i:
                load(2 * i + 2, 0)
                store(2 * i, 0)
                load(2 * i + 3, 1)
                store(2 * i + 1, 1)
            store(STEPS - 2, 0)
            store(STEPS - 1, 1)
            eng.wait_ge(edge_stored, 32)
            for p in (0, 1):
                eng.wait_ge(stored[p], 8 * STEPS)

        @block.gpsimd
        def _(eng):
            make_identity(eng, ident, 128, zeroed, consts)
            eng.memset(edge[:, :], 0.0).then_inc(consts, 1)
            for tile in (*hin, *vin):
                eng.memset(tile[:, :, 0:WIDE:WIDE - 1], 0.0).then_inc(consts, 1)

            def step(n, p):
                need(eng, loaded[p], 16 * (n - p) + 32)
                need(eng, halfsum_ready, n)
                eng.tensor_tensor(both[:, :, :], hin[p][:, 1:1 + ROWS, 1:1 + SIDE],
                                  vin[p][:, 1:1 + ROWS, 1:1 + SIDE], ALU.add).then_inc(both_ready, 1)

            run(eng, step)

        @block.scalar
        def _(eng):
            eng.wait_ge(w_loaded, 16)

            def step(n, p):
                need(eng, total_ready, n)
                for u in range(PAIRS):
                    need(eng, h_filled, PAIRS * n + u + 1)
                    eng.activation(gh[:, 2 * u:2 * u + 2, :], psH[u % 2][:, :, :], ACT.Gelu,
                                   bias=W["b_h"]).then_inc(gh_ready, 1)
                need(eng, tap_done, 9 * (n + 1))
                eng.activation(gv[:, :, :], acc[:, :, :], ACT.Gelu, bias=W["b_v"]).then_inc(gv_ready, 1)
                need(eng, stored[p], 8 * (n - p))
                for u in range(PAIRS):
                    need(eng, p_filled, PAIRS * n + u + 1)
                    eng.activation(xo[p][:, 2 * SIDE * u:2 * SIDE * (u + 1)], psP[u % 2][:, :], ACT.Identity,
                                   bias=W["proj_b"]).then_inc(out_ready, 1)

            run(eng, step)

        @block.vector
        def _(eng):
            eng.wait_ge(w_loaded, 16)
            eng.wait_ge(consts, 6)
            for k in range(9):
                eng.tensor_scalar(taps[:, k, :], ident[:, :], W["tap_h"][:, k:k + 1], None,
                                  ALU.mult).then_inc(taps_ready, 1)

            def step(n, p):
                need(eng, loaded[p], 16 * (n - p) + 32)
                need(eng, gv_ready, n)
                for k in range(9):
                    dy, dx = k // 3, k % 3
                    source = vin[p][:, dy:dy + ROWS, dx:dx + SIDE]
                    tap = W["tap_v"][:, k:k + 1]
                    if k == 0:
                        eng.tensor_scalar(acc[:, :, :], source, tap, None, ALU.mult).then_inc(tap_done, 1)
                    else:
                        need(eng, tap_done, 9 * n + k)
                        eng.scalar_tensor_tensor(acc[:, :, :], source, tap, acc[:, :, :],
                                                 ALU.mult, ALU.add).then_inc(tap_done, 1)
                need(eng, both_ready, n + 1)
                need(eng, gh_ready, PAIRS * (n + 1))
                need(eng, p_filled, PAIRS * n)
                eng.tensor_tensor(total[:, :, :], both[:, :, :], gh[:, :, :], ALU.add).then_inc(halfsum_ready, 1)
                need(eng, gv_ready, n + 1)
                need(eng, halfsum_ready, n + 1)
                eng.tensor_tensor(total[:, :, :], total[:, :, :], gv[:, :, :], ALU.add).then_inc(total_ready, 1)

            run(eng, step)

        @block.tensor
        def _(eng):
            eng.wait_ge(taps_ready, 9)

            def convolve(n, p):
                need(eng, loaded[p], 16 * (n - p) + 32)
                for u in range(PAIRS):
                    need(eng, gh_ready, PAIRS * n + u - 1)
                    for k in range(9):
                        dy, dx = k // 3, k % 3
                        mm = eng.matmul(psH[u % 2][:, :, :], taps[:, k, :],
                                        hin[p][:, 2 * u + dy:2 * u + dy + 2, dx:dx + SIDE],
                                        start=(k == 0), stop=(k == 8))
                    mm.then_inc(h_filled, 1)

            def project(n):
                need(eng, total_ready, n + 1)
                for u in range(PAIRS):
                    need(eng, out_ready, PAIRS * n + u - 1)
                    eng.matmul(psP[u % 2][:, :], W["proj"],
                               total[:, 2 * u:2 * u + 2, :].rearrange("c r s -> c (r s)"),
                               start=True, stop=True).then_inc(p_filled, 1)

            convolve(0, 0)
            project(0)
            convolve(1, 1)
            project(1)
            with eng.Fori(1, STEPS // 2) as i:
                for p in (0, 1):
                    convolve(2 * i + p, p)
                    project(2 * i + p)



def kv_phase(nc, y_dram, stats_dram, x1_dram, w_dram, x2_dram, ut_dram):
    at, width = offsets(GLOBAL_COLS)
    SUB = T // 128
    GROUPS = 2 * HEADS

    with ExitStack() as ctx:
        def sb(name, shape):
            return ctx.enter_context(nc.sbuf_tensor(f"kv_{name}", shape, F32))

        def pb(name, shape):
            return ctx.enter_context(nc.psum_tensor(f"kv_{name}", shape, F32))

        sems = []

        def sem(name):
            sems.append(ctx.enter_context(nc.semaphore(f"kv_{name}")))
            return sems[-1]

        w = sb("w", [C, width])
        W = {n: w[:, a:b] for n, (a, b) in at.items()}
        ident = sb("ident", [C, 128])
        st = sb("st", [C, 2])
        moments = sb("moments", [C, 2])
        gm = sb("gm", [C, 2])
        gvar = sb("gvar", [C, 1])
        gsd = sb("gsd", [C, 1])
        ga = sb("ga", [C, 1])
        gb = sb("gb", [C, 1])
        epst = sb("epst", [C, 1])
        wmean = sb("wmean", [C, GROUPS, 1])
        wcen = sb("wcen", [C, GROUPS, HD])
        yin = [sb(f"yin{p}", [C, T]) for p in (0, 1)]
        xin = [sb(f"xin{p}", [C, T]) for p in (0, 1)]
        act = [sb(f"act{p}", [C, T]) for p in (0, 1)]
        x2 = [sb(f"x2{p}", [C, T]) for p in (0, 1)]
        sq = sb("sq", [C, SUB * GROUPS, HD])
        ss = sb("ss", [C, SUB * GROUPS, 1])
        sd = sb("sd", [C, SUB * GROUPS, 1])
        kvn = sb("kvn", [C, SUB, GROUPS * HD])
        kvw = sb("kvw", [C, SUB, GROUPS * HD])
        kvf = [sb(f"kvf{p}", [C, SUB, GROUPS * HD]) for p in (0, 1)]
        kvb = sb("kvb", [C, 128])
        gmat = sb("gmat", [C, 128])
        ut = sb("ut", [C, 128])
        psK = [pb(f"psK{b}", [C, 2, GROUPS * HD]) for b in range(4)]
        psG = pb("psG", [C, 128])
        psA = pb("psA", [C, 128])
        psU = pb("psU", [C, 128])

        w_loaded = sem("w_loaded")
        zeroed = sem("zeroed")
        consts = sem("consts")
        norm_step = sem("norm_step")
        sd_step = sem("sd_step")
        g_filled = sem("g_filled")
        affine_ready = sem("affine_ready")
        wcen_ready = sem("wcen_ready")
        loaded = [sem(f"loaded{p}") for p in (0, 1)]
        stored = [sem(f"stored{p}") for p in (0, 1)]
        act_ready = sem("act_ready")
        x2_ready = sem("x2_ready")
        k_filled = sem("k_filled")
        sq_ready = sem("sq_ready")
        ss_ready = sem("ss_ready")
        sd_ready = sem("sd_ready")
        sde_ready = sem("sde_ready")
        rsd_ready = sem("rsd_ready")
        kvn_ready = sem("kvn_ready")
        kvw_ready = sem("kvw_ready")
        kvf_ready = sem("kvf_ready")
        kv_summed = sem("kv_summed")
        tail = sem("tail")
        tail_mm = sem("tail_mm")
        ut_stored = sem("ut_stored")

        def run(eng, step):
            step(0, 0)
            step(1, 1)
            with eng.Fori(1, CHUNKS // 2) as i:
                step(2 * i, 0)
                step(2 * i + 1, 1)

        ctx.callback(clear_semaphores, nc, sems)
        block = ctx.enter_context(nc.Block())

        @block.sync
        def _(eng):
            eng.dma_start(w[:, :], w_dram).then_inc(w_loaded, 16)
            eng.dma_start(st[:, :], stats_dram).then_inc(w_loaded, 16)

            def load(n, p):
                need(eng, x2_ready, n - 1)
                eng.dma_start(yin[p][:, :], y_dram[:, bass.ds(T * n, T)]).then_inc(loaded[p], 16)
                eng.dma_start(xin[p][:, :], x1_dram[:, bass.ds(T * n + 1, T)]).then_inc(loaded[p], 16)

            def store(n, p):
                need(eng, x2_ready, n + 1)
                eng.dma_start(x2_dram[:, bass.ds(T * n, T)], x2[p][:, :]).then_inc(stored[p], 16)

            load(0, 0)
            load(1, 1)
            with eng.Fori(0, CHUNKS // 2 - 1) as i:
                load(2 * i + 2, 0)
                store(2 * i, 0)
                load(2 * i + 3, 1)
                store(2 * i + 1, 1)
            store(CHUNKS - 2, 0)
            store(CHUNKS - 1, 1)
            eng.wait_ge(tail, 5)
            eng.dma_start(ut_dram, ut[:, :]).then_inc(ut_stored, 16)
            eng.wait_ge(ut_stored, 16)
            for p in (0, 1):
                eng.wait_ge(stored[p], 8 * CHUNKS)

        @block.gpsimd
        def _(eng):
            make_identity(eng, ident, 128, zeroed, consts)
            eng.memset(epst[:, :], EPS).then_inc(consts, 1)
            eng.wait_ge(w_loaded, 32)

            def step(n, p):
                need(eng, act_ready, n + 1)
                need(eng, stored[p], 8 * (n - p))
                need(eng, k_filled, 4 * (n - 1))
                eng.tensor_tensor(x2[p][:, :], act[p][:, :], xin[p][:, :], ALU.add).then_inc(x2_ready, 1)
                need(eng, kvw_ready, n + 1)
                need(eng, kv_summed, n - 1)
                for s in range(SUB):
                    eng.tensor_tensor(kvf[p][:, s, :], kvw[:, s, :], W["ln_b"], ALU.add).then_inc(kvf_ready, 1)

            run(eng, step)

        @block.scalar
        def _(eng):
            eng.wait_ge(norm_step, 4)
            eng.activation(gsd[:, :], gvar[:, :], ACT.Sqrt, bias=epst[:, 0:1]).then_inc(sd_step, 1)
            eng.wait_ge(affine_ready, 3)

            def gated(n, p):
                need(eng, loaded[p], 16 * (n - p) + 32)
                need(eng, x2_ready, n - 1)
                eng.activation(act[p][:, :], yin[p][:, :], ACT.Silu, bias=gb[:, 0:1],
                               scale=ga[:, 0:1]).then_inc(act_ready, 1)

            def step(n, p):
                gated(n, p)
                need(eng, ss_ready, n)
                for half in (0, 1):
                    need(eng, k_filled, 4 * n + 2 * half + 2)
                    eng.activation(sq[:, 2 * GROUPS * half:2 * GROUPS * (half + 1), :],
                                   psK[2 * p + half][:, :, :].rearrange("p s (g e) -> p (s g) e", e=HD),
                                   ACT.Square).then_inc(sq_ready, 1)
                need(eng, ss_ready, n + 1)
                need(eng, kvn_ready, 2 * n)
                eng.activation(sd[:, :, :], ss[:, :, :], ACT.Sqrt, scale=1.0 / (HD - 1)).then_inc(sd_ready, 1)

            run(eng, step)

        @block.vector
        def _(eng):
            eng.wait_ge(w_loaded, 32)
            eng.wait_ge(consts, 2)
            eng.tensor_copy(moments[:, 0:1], st[:, 0:1]).then_inc(norm_step, 1)
            eng.scalar_tensor_tensor(moments[:, 1:2], st[:, 0:1], st[:, 0:1], st[:, 1:2],
                                     ALU.mult, ALU.add).then_inc(norm_step, 1)
            eng.wait_ge(g_filled, 1)
            eng.tensor_copy(gm[:, :], psG[:, 0:2]).then_inc(norm_step, 1)
            eng.wait_ge(norm_step, 3)
            eng.tensor_scalar(gb[:, :], gm[:, 0:1], -1.0, None, ALU.mult).then_inc(affine_ready, 1)
            eng.wait_ge(affine_ready, 1)
            eng.scalar_tensor_tensor(gvar[:, :], gm[:, 0:1], gb[:, 0:1], gm[:, 1:2],
                                     ALU.mult, ALU.add).then_inc(norm_step, 1)
            eng.wait_ge(sd_step, 1)
            eng.reciprocal(gsd[:, :], gsd[:, :]).then_inc(norm_step, 1)
            eng.wait_ge(norm_step, 5)
            eng.tensor_tensor(ga[:, :], gsd[:, :], W["gamma"], ALU.mult).then_inc(affine_ready, 1)
            eng.wait_ge(affine_ready, 2)
            eng.scalar_tensor_tensor(gb[:, :], gb[:, :], ga[:, 0:1], W["beta"],
                                     ALU.mult, ALU.add).then_inc(affine_ready, 1)
            wkv = W["wkv"].rearrange("c (g e) -> c g e", e=HD)
            eng.tensor_reduce(wmean[:, :, :], wkv, AX_X, ALU.add).then_inc(wcen_ready, 1)
            eng.wait_ge(wcen_ready, 1)
            eng.tensor_scalar(wmean[:, :, :], wmean[:, :, :], 1.0 / HD, None, ALU.mult).then_inc(wcen_ready, 1)
            eng.wait_ge(wcen_ready, 2)
            eng.tensor_tensor(wcen[:, :, :], wkv, wmean[:, :, :].broadcast_to([C, GROUPS, HD]),
                              ALU.subtract).then_inc(wcen_ready, 1)

            def step(n, p):
                need(eng, sq_ready, 2 * n + 2)
                need(eng, sd_ready, n)
                eng.tensor_reduce(ss[:, :, :], sq[:, :, :], AX_X, ALU.add).then_inc(ss_ready, 1)
                need(eng, sd_ready, n + 1)
                eng.tensor_scalar(sd[:, :, :], sd[:, :, :], EPS, None, ALU.add).then_inc(sde_ready, 1)
                need(eng, sde_ready, n + 1)
                eng.reciprocal(sd[:, :, :], sd[:, :, :]).then_inc(rsd_ready, 1)
                need(eng, rsd_ready, n + 1)
                need(eng, kvw_ready, n)
                for half in (0, 1):
                    eng.tensor_tensor(
                        kvn[:, 2 * half:2 * half + 2, :].rearrange("p s (g e) -> p (s g) e", e=HD),
                        sd[:, 2 * GROUPS * half:2 * GROUPS * (half + 1), :].broadcast_to([C, 2 * GROUPS, HD]),
                        psK[2 * p + half][:, :, :].rearrange("p s (g e) -> p (s g) e", e=HD),
                        ALU.mult).then_inc(kvn_ready, 1)
                need(eng, kvn_ready, 2 * n + 2)
                need(eng, kvf_ready, SUB * n)
                eng.tensor_tensor(kvw[:, :, :], kvn[:, :, :],
                                  W["ln_w"].unsqueeze(1).broadcast_to([C, SUB, GROUPS * HD]),
                                  ALU.mult).then_inc(kvw_ready, 1)

            run(eng, step)
            eng.wait_ge(kv_summed, CHUNKS)
            eng.tensor_tensor(kvb[:, :], W["headmask"], psA[:, :], ALU.mult).then_inc(tail, 1)
            eng.wait_ge(tail, 1)
            eng.tensor_scalar(kvb[:, :], kvb[:, :], 1.0 / TOKENS, None, ALU.mult).then_inc(tail, 1)
            eng.wait_ge(tail_mm, 1)
            eng.tensor_tensor(gmat[:, :], ident[:, :], psG[:, :], ALU.add).then_inc(tail, 1)
            eng.wait_ge(tail_mm, 2)
            eng.wait_ge(tail, 3)
            eng.tensor_copy(ut[:, :], psU[:, :]).then_inc(tail, 2)

        @block.tensor
        def _(eng):
            eng.wait_ge(w_loaded, 32)
            eng.wait_ge(norm_step, 2)
            eng.matmul(psG[:, 0:2], W["groups"], moments[:, :], start=True, stop=True).then_inc(g_filled, 1)
            eng.wait_ge(wcen_ready, 3)

            def keys_values(n, p):
                need(eng, x2_ready, n + 1)
                need(eng, kvn_ready, 2 * (n - 1))
                need(eng, sq_ready, 2 * (n - 1))
                for s in range(SUB):
                    eng.matmul(psK[2 * p + s // 2][:, s % 2, :], x2[p][:, 128 * s:128 * s + 128],
                               wcen[:, :, :].rearrange("c g e -> c (g e)"), start=True,
                               stop=True).then_inc(k_filled, 1)

            def accumulate(n, p, first, last):
                for s in range(SUB):
                    need(eng, kvf_ready, SUB * n + s + 1)
                    mm = eng.matmul(psA[:, :], kvf[p][:, s, 0:128], kvf[p][:, s, 128:256],
                                    start=(first and s == 0), stop=(last and s == SUB - 1))
                mm.then_inc(kv_summed, 1)

            keys_values(0, 0)
            keys_values(1, 1)
            accumulate(0, 0, True, False)
            keys_values(2, 0)
            accumulate(1, 1, False, False)
            with eng.Fori(1, CHUNKS // 2 - 1) as i:
                keys_values(2 * i + 1, 1)
                accumulate(2 * i, 0, False, False)
                keys_values(2 * i + 2, 0)
                accumulate(2 * i + 1, 1, False, False)
            keys_values(CHUNKS - 1, 1)
            accumulate(CHUNKS - 2, 0, False, False)
            accumulate(CHUNKS - 1, 1, False, True)
            eng.wait_ge(tail, 2)
            eng.matmul(psG[:, :], kvb[:, :], W["wq"], start=True, stop=True).then_inc(tail_mm, 1)
            eng.wait_ge(tail, 3)
            eng.matmul(psU[:, :], gmat[:, :], W["o1t"], start=True, stop=True).then_inc(tail_mm, 1)


def mlp_phase(nc, x2_dram, ut_dram, w_dram, out_dram):
    at, width = offsets(GLOBAL_COLS)
    lo, hi = at["o2t"]

    with ExitStack() as ctx:
        def sb(name, shape):
            return ctx.enter_context(nc.sbuf_tensor(f"ml_{name}", shape, F32))

        sems = []

        def sem(name):
            sems.append(ctx.enter_context(nc.semaphore(f"ml_{name}")))
            return sems[-1]

        ut = sb("ut", [C, 128])
        o2t = sb("o2t", [C, 128])
        xin = [sb(f"xin{p}", [C, T]) for p in (0, 1)]
        u = [sb(f"u{p}", [C, T]) for p in (0, 1)]
        t = [sb(f"t{p}", [C, T]) for p in (0, 1)]
        xo = [sb(f"xo{p}", [C, T]) for p in (0, 1)]
        psU = [ctx.enter_context(nc.psum_tensor(f"ml_psU{b}", [C, T], F32)) for b in (0, 1)]
        psO = [ctx.enter_context(nc.psum_tensor(f"ml_psO{b}", [C, T], F32)) for b in (0, 1)]
        w_loaded = sem("w_loaded")
        loaded = [sem(f"loaded{p}") for p in (0, 1)]
        stored = [sem(f"stored{p}") for p in (0, 1)]
        u_filled = sem("u_filled")
        u_ready = sem("u_ready")
        o_filled = sem("o_filled")
        t_ready = sem("t_ready")
        out_ready = sem("out_ready")

        def run(eng, step):
            step(0, 0)
            step(1, 1)
            with eng.Fori(1, CHUNKS // 2) as i:
                step(2 * i, 0)
                step(2 * i + 1, 1)

        ctx.callback(clear_semaphores, nc, sems)
        block = ctx.enter_context(nc.Block())

        @block.sync
        def _(eng):
            eng.dma_start(ut[:, :], ut_dram).then_inc(w_loaded, 16)
            eng.dma_start(o2t[:, :], w_dram[:, lo:hi]).then_inc(w_loaded, 16)

            def load(n, p):
                need(eng, u_filled, n - 1)
                need(eng, t_ready, n - 1)
                eng.dma_start(xin[p][:, :], x2_dram[:, bass.ds(T * n, T)]).then_inc(loaded[p], 16)

            def store(n, p):
                need(eng, out_ready, n + 1)
                eng.dma_start(out_dram[:, bass.ds(T * n, T)], xo[p][:, :]).then_inc(stored[p], 16)

            load(0, 0)
            load(1, 1)
            with eng.Fori(0, CHUNKS // 2 - 1) as i:
                load(2 * i + 2, 0)
                store(2 * i, 0)
                load(2 * i + 3, 1)
                store(2 * i + 1, 1)
            store(CHUNKS - 2, 0)
            store(CHUNKS - 1, 1)
            for p in (0, 1):
                eng.wait_ge(stored[p], 8 * CHUNKS)

        @block.scalar
        def _(eng):
            def inner(n, p):
                need(eng, u_filled, n + 1)
                need(eng, o_filled, n - 1)
                eng.activation(u[p][:, :], psU[p][:, :], ACT.Gelu).then_inc(u_ready, 1)

            def outer(n, p):
                need(eng, t_ready, n + 1)
                need(eng, stored[p], 8 * (n - p))
                eng.activation(xo[p][:, :], t[p][:, :], ACT.Gelu).then_inc(out_ready, 1)

            inner(0, 0)
            inner(1, 1)
            outer(0, 0)
            with eng.Fori(1, CHUNKS // 2) as i:
                inner(2 * i, 0)
                outer(2 * i - 1, 1)
                inner(2 * i + 1, 1)
                outer(2 * i, 0)
            outer(CHUNKS - 1, 1)

        @block.vector
        def _(eng):
            def step(n, p):
                need(eng, o_filled, n + 1)
                need(eng, loaded[p], 8 * (n - p) + 16)
                need(eng, out_ready, n - 1)
                eng.tensor_tensor(t[p][:, :], xin[p][:, :], psO[p][:, :], ALU.add).then_inc(t_ready, 1)

            run(eng, step)

        @block.tensor
        def _(eng):
            eng.wait_ge(w_loaded, 32)

            def inner(n, p):
                need(eng, loaded[p], 8 * (n - p) + 16)
                need(eng, u_ready, n - 1)
                eng.matmul(psU[p][:, :], ut[:, :], xin[p][:, :], start=True, stop=True).then_inc(u_filled, 1)

            def outer(n, p):
                need(eng, u_ready, n + 1)
                need(eng, t_ready, n - 1)
                eng.matmul(psO[p][:, :], o2t[:, :], u[p][:, :], start=True, stop=True).then_inc(o_filled, 1)

            inner(0, 0)
            inner(1, 1)
            outer(0, 0)
            with eng.Fori(1, CHUNKS // 2) as i:
                inner(2 * i, 0)
                outer(2 * i - 1, 1)
                inner(2 * i + 1, 1)
                outer(2 * i, 0)
            outer(CHUNKS - 1, 1)


def network_kernel(nc, x, w_row, w_col, w_lepe, w_fwd, w_bwd, w_global, w_chunked, out):
    def scratch(name, shape):
        return nc.dram_tensor(name, shape, F32).ap()

    h = scratch("h_att", (C, SIDE + 2, SIDE))
    v = scratch("v_att", (C, SIDE + 2, SIDE))
    x1 = scratch("x1", (C, TOKENS + 2))
    y_fwd = scratch("y_fwd", (C, TOKENS))
    y_sum = scratch("y_sum", (C, TOKENS))
    stats = scratch("stats", (C, 2))
    x2 = scratch("x2", (C, TOKENS))
    ut = scratch("ut", (C, C))
    x3 = scratch("x3", (C, TOKENS))

    attention_phase(nc, False, x, w_row, h)
    attention_phase(nc, True, x, w_col, v)
    lepe_phase(nc, h, v, w_lepe, x1)
    mamba_phase(nc, "forward", x1, w_fwd, y_fwd)
    mamba_phase(nc, "backward", x1, w_bwd, y_sum, y_fwd, stats)
    kv_phase(nc, y_sum, stats, x1, w_global, x2, ut)
    mlp_phase(nc, x2, ut, w_global, x3)
    mamba_phase(nc, "chunked", x3, w_chunked, out)





def _pack(cols, parts):
    at, width = offsets(cols)
    out = np.zeros((C, width), np.float32)
    for name, a in parts.items():
        lo, hi = at[name]
        a = a.reshape(a.shape[0], -1)
        assert a.shape[1] == hi - lo, (name, a.shape)
        out[:a.shape[0], lo:hi] = a
    return out


def _lay_mamba1(W_in, conv_w, conv_b, W_x, W_dt, b_dt, A_log, D, W_out):
    blocks = lambda a: a.reshape(2, 128, -1).transpose(1, 0, 2)
    units = lambda a: a.reshape(2, 128, STATE).transpose(1, 2, 0)
    x_rows = blocks(W_x)
    dtr = np.zeros((128, 2, 32), np.float32)
    dtr[:, :, 0:8] = x_rows[:, :, 0:8]
    return _pack(MAMBA1_COLS, {
        "win": W_in[:, 0:256], "wz": W_in[:, 256:512],
        "tapw": np.broadcast_to(conv_w.T.reshape(1, 2 * 256), (128, 512)),
        "wbc": np.tile(x_rows[:, :, 8:40], (1, 1, 3)), "wdtr": dtr, "wdt": W_dt,
        "bdt": blocks(b_dt), "convb": blocks(conv_b), "dskip": blocks(D), "alog": units(A_log),
        "wout": blocks(W_out)})


def _lay_mamba3(ln_g, ln_b, in_proj_w, conv_w, conv_b, x_proj_w, dt_proj_w, dt_proj_b, A_log, D, out_proj_w):
    win, wz = np.zeros((2, 128, 2, 128), np.float32)
    wb, wc = np.zeros((2, 128, 32), np.float32)
    dtr = np.zeros((128, 2, 32), np.float32)
    wdt = np.zeros((32, 2, 128), np.float32)
    wout = np.zeros((128, 2, 128), np.float32)
    for half in range(2):
        rows = slice(64 * half, 64 * half + 64)
        wb[rows, 16 * half:16 * half + 16] = x_proj_w[2:18].T
        wc[rows, 16 * half:16 * half + 16] = x_proj_w[18:34].T
        for b in range(2):
            q = 2 * b + half
            ch = slice(32 * q, 32 * q + 32)
            win[ch, b, rows] = in_proj_w[0:64].T
            wz[ch, b, rows] = in_proj_w[64:128].T
            dtr[rows, b, 2 * q:2 * q + 2] = x_proj_w[0:2].T
            wdt[2 * q:2 * q + 2, b, rows] = dt_proj_w.T
            wout[rows, b, ch] = out_proj_w.T
    both = lambda v: np.repeat(np.tile(v.reshape(64), 2).reshape(128, 1), 2, axis=1)
    return _pack(MAMBA3_COLS, {
        "win": win, "wz": wz, "wb": np.tile(wb, (1, 3)), "wc": np.tile(wc, (1, 3)), "wdtr": dtr,
        "tapw": np.broadcast_to(np.tile(conv_w.T.reshape(4, 64), (1, 4)).reshape(1, 1024), (128, 1024)),
        "wdt": wdt, "bdt": both(dt_proj_b), "convb": both(conv_b), "dskip": both(D),
        "alog": np.repeat(np.tile(A_log, (2, 1)), 2, axis=1), "wout": wout,
        "ln_g": ln_g.reshape(128, 1), "ln_b": ln_b.reshape(128, 1)})


def _lay_attention(qkv_w, qkv_b, table):
    def heads(a, cols):
        out = np.zeros((cols, 2, 128), np.float32)
        for h in range(HEADS):
            out[:, h // 4, 32 * (h % 4):32 * (h % 4) + HD] = a[h * HD:(h + 1) * HD].reshape(HD, cols).T
        return out
    onehot = np.zeros((128, SIDE), np.float32)
    ck = np.zeros((128, 2, SIDE), np.float32)
    ck[:, :, :] = heads(qkv_b[C:2 * C], 1).reshape(2, 128).T[:, :, None]
    for j in range(4):
        for a in range(S7):
            onehot[32 * j + HD + a, a * SIDE // S7:(a + 1) * SIDE // S7] = 1.0
            for t in range(2):
                ck[32 * j + HD + a, t] = np.repeat(table[a, :, 4 * t + j], SIDE // S7)
        ck[32 * j + MAXROW] = 1.0
    return _pack(ATTN_COLS, {
        "wq": heads(qkv_w[0:C], C), "wk": heads(qkv_w[C:2 * C], C), "wv": qkv_w[2 * C:].T,
        "onehot": onehot, "bq": heads(qkv_b[0:C], 1).reshape(2, 128).T, "ck": ck,
        "bv": qkv_b[2 * C:].reshape(C, 1)})


def _lay_lepe(h_w, h_b, v_w, v_b, proj_w, proj_b):
    col = lambda a: a.reshape(C, -1)
    return _pack(LEPE_COLS, {"tap_h": col(h_w), "tap_v": col(v_w), "b_h": col(h_b), "b_v": col(v_b),
                             "proj_b": col(proj_b), "proj": proj_w.T})


def _lay_global(gamma, beta, qkv_w, o1_w, o2_w, kln_w, kln_b, vln_w, vln_b):
    qkv = qkv_w.reshape(HEADS, 3, HD, C)
    part = lambda i: qkv[:, i].reshape(C, C)
    row = lambda k, v: np.broadcast_to(np.concatenate([k.reshape(1, C), v.reshape(1, C)], axis=1), (C, 2 * C))
    return _pack(GLOBAL_COLS, {
        "gamma": gamma.reshape(C, 1), "beta": beta.reshape(C, 1),
        "wkv": np.concatenate([part(1).T, part(2).T], axis=1), "wq": part(0),
        "o1t": o1_w.T, "o2t": o2_w.T, "ln_w": row(kln_w, vln_w), "ln_b": row(kln_b, vln_b),
        "groups": np.kron(np.eye(4), np.full((32, 32), 1.0 / 32)),
        "headmask": np.kron(np.eye(HEADS), np.ones((HD, HD)))})


def kernel(**inputs):
    import concourse.bacc as _bacc
    from concourse.bass_utils import run_bass_kernel_spmd as _run

    part = lambda layer, names: [np.asarray(inputs[f"{layer}_conv_{n}"]) for n in names.split()]
    table_h, table_v = part("L0", "table_h table_v")
    tiles = np.arange(S7)
    rel = tiles[:, None] - tiles[None, :] + S7 - 1
    mamba1 = "W_in conv_w conv_b W_x W_dt b_dt A_log D W_out".split()
    arrays = {
        "x": np.asarray(inputs["x"]).reshape(C, SIDE, SIDE),
        "w_row": _lay_attention(*part("L0", "qkv_h_w qkv_h_b"), table_h[S7 - 1, rel]),
        "w_col": _lay_attention(*part("L0", "qkv_v_w qkv_v_b"), table_v[rel, S7 - 1]),
        "w_lepe": _lay_lepe(*part("L0", "lepe_h_w lepe_h_b lepe_v_w lepe_v_b proj_w proj_b")),
        "w_fwd": _lay_mamba1(*part("L1", " ".join(n + "_f" for n in mamba1))),
        "w_bwd": _lay_mamba1(*part("L1", " ".join(n + "_b" for n in mamba1))),
        "w_global": _lay_global(*part("L1", "gn_gamma gn_beta"),
                                *part("L2", "qkv_w o1_w o2_w kln_w kln_b vln_w vln_b")),
        "w_chunked": _lay_mamba3(*part("L3", "ln_g ln_b in_proj_w conv_w conv_b x_proj_w dt_proj_w "
                                             "dt_proj_b A_log D out_proj_w")),
    }
    nc = _bacc.Bacc("TRN2", target_bir_lowering=False, num_devices=1)
    args = [nc.dram_tensor(f"in_{n}_dram", a.shape, F32, kind="ExternalInput").ap() for n, a in arrays.items()]
    args.append(nc.dram_tensor("out_0_dram", (C, TOKENS), F32, kind="ExternalOutput").ap())
    network_kernel(nc, *args)
    r = _run(nc, [{f"in_{n}_dram": np.ascontiguousarray(a) for n, a in arrays.items()}], core_ids=[0])
    return r.results[0]["out_0_dram"].reshape(1, C, SIDE, SIDE)
```

```python
from contextlib import ExitStack

import numpy as np

import concourse.bass as bass
from concourse import mybir
from concourse.alu_op_type import AluOpType as ALU

ACT = mybir.ActivationFunctionType
F32 = mybir.dt.float32
BF16 = mybir.dt.bfloat16
AX_X = mybir.AxisListType.X

C = 128
SIDE = 224
TOKENS = SIDE * SIDE
T = 512
CHUNKS = TOKENS // T
EPS = 1e-5

S7 = 7
HEADS = 8
HD = C // HEADS
LINES = SIDE
BLOCK = 28
HALF = SIDE // 2

STATE = 16
UNITS = 2 * STATE
RING = 4

ATTN_COLS = {"wq": 128, "wk": 128, "wv": 128, "bq": 1, "bk": 1, "bv": 1, "mask": 3, "onehot": SIDE,
             "selm": HEADS, "kc": HEADS * SIDE}
LEPE_COLS = {"tap_h": 9, "tap_v": 9, "b_h": 1, "b_v": 1, "proj_b": 1, "proj": 128}
MAMBA1_COLS = {"win": 256, "tapw": 2 * 256, "wz": 256, "wbc": 2 * 96, "wdtr": 2 * 32, "wdt": 256,
               "bdt": 2, "convb": 2, "dskip": 2, "alog": UNITS, "wout": 256}
MAMBA3_COLS = {"win": 256, "tapw": 4 * 256, "wz": 256, "wb": 96, "wc": 96, "wdtr": 2 * 32, "wdt": 256,
               "bdt": 2, "convb": 2, "dskip": 2, "alog": UNITS, "wout": 256, "ln_g": 1, "ln_b": 1}
GLOBAL_COLS = {"gamma": 1, "beta": 1, "wkv": 256, "wq": 128, "o1t": 128, "o2t": 128,
               "ln_w": 256, "ln_b": 256, "groups": 128, "headmask": 128}


def offsets(cols):
    at, out = 0, {}
    for name, n in cols.items():
        out[name] = (at, at + n)
        at += n
    return out, at


def need(eng, sem, count):
    if not isinstance(count, int) or count > 0:
        eng.wait_ge(sem, count)


def clear_semaphores(nc, sems):
    with nc.Block() as block:
        @block.sync
        def _(eng):
            for sem in sems:
                eng.sem_clear(sem)


def make_identity(pool, tile, n, zeroed, made):
    pool.memset(tile[:, :], 0.0).then_inc(zeroed, 1)
    pool.wait_ge(zeroed, 1)
    pool.affine_select(out=tile[:, :], in_=tile[:, :], compare_op=ALU.not_equal, fill=1.0, base=0,
                       pattern=[[-1, n]], channel_multiplier=1).then_inc(made, 1)



def mamba_phase(nc, kind, x_dram, w_dram, out_dram, addend_dram=None, stats_dram=None):
    layer3 = kind == "chunked"
    rev = kind == "backward"
    cols = MAMBA3_COLS if layer3 else MAMBA1_COLS
    at, width = offsets(cols)
    TAPS = 4 if layer3 else 2
    NBC = 4 if layer3 else 1
    PER = 1 if layer3 else 2
    KB = UNITS // PER
    HALO = TAPS - 1

    if layer3:
        order = [("mean", 0), ("var", 1), ("conv0", 0), ("conv1", 1), ("gate0", 0), ("gate1", 1),
                 ("bc0", 0), ("bc1", 1), ("bc2", 0), ("bc3", 1), ("dtr", 1), ("dt0", 0), ("dt1", 1)]
    else:
        order = [("conv0", 0), ("conv1", 1), ("gate0", 0), ("gate1", 1),
                 ("bc0", 0), ("dtr", 1), ("dt0", 0), ("dt1", 1)]
    bank_of = dict(order)
    rank = {name: sum(1 for n, b in order[:i] if b == bank) for i, (name, bank) in enumerate(order)}
    fills = [sum(1 for _, b in order if b == bank) for bank in (0, 1)]

    def index(name, m):
        if name == "out":
            return (min(m + 2, CHUNKS) if isinstance(m, int) else m + 2) * fills[1] + m
        before = m * fills[bank_of[name]] + rank[name]
        if bank_of[name] == 1:
            before = before + (max(m - 1, 0) if isinstance(m, int) else m - 1)
        return before

    with ExitStack() as ctx:
        def sb(name, shape, dt=F32):
            return ctx.enter_context(nc.sbuf_tensor(f"{kind}_{name}", shape, dt))

        def pb(name, shape):
            return ctx.enter_context(nc.psum_tensor(f"{kind}_{name}", shape, F32))

        sems = []

        def sem(name):
            sems.append(ctx.enter_context(nc.semaphore(f"{kind}_{name}")))
            return sems[-1]

        w = sb("w", [C, width])
        W = {n: w[:, a:b] for n, (a, b) in at.items()}
        wconv = sb("wconv", [C, TAPS, 2, 128])
        decay = sb("decay", [C, UNITS])
        epst = sb("epst", [C, 1])
        ident = sb("ident", [C, 128])
        ones = sb("ones", [C, 128])
        select = sb("select", [96, 32, 128], BF16)
        xin = [sb(f"xin{p}", [C, T + 2]) for p in (0, 1)]
        xn = [sb(f"xn{p}", [C, HALO + T]) for p in (0, 1)] if layer3 else None
        cen = sb("cen", [C, T]) if layer3 else None
        sq = sb("sq", [C, T]) if layer3 else None
        xc = [sb(f"xc{p}", [C, 2, T]) for p in (0, 1)]
        zs = [sb(f"zs{p}", [C, 2, T]) for p in (0, 1)]
        bcs = [sb(f"bcs{p}", [96, NBC, T], BF16) for p in (0, 1)]
        rest = sb("rest", [96, T])
        mid = sb("mid", [96, T], BF16)
        dtr = sb("dtr", [32, T])
        sp = sb("sp", [C, 2, T])
        sp1 = sb("sp1", [C, 2, T])
        spl = sb("spl", [C, 2, T])
        dt = [sb(f"dt{p}", [C, 2, T]) for p in (0, 1)]
        dtx = [sb(f"dtx{p}", [C, 2, T]) for p in (0, 1)]
        da = sb("da", [C, RING, T])
        dbx = sb("dbx", [C, RING, T])
        hs = sb("hs", [C, UNITS, T])
        cb = sb("cb", [C, RING, T])
        hc = sb("hc", [C, RING, T])
        yv = sb("yv", [C, 2, T])
        yout = [sb(f"yout{p}", [C, T]) for p in (0, 1)]
        yadd = [sb(f"yadd{p}", [C, T]) for p in (0, 1)] if rev else None
        stats = sb("stats", [C, CHUNKS, 6]) if rev else None
        aggr = sb("aggr", [C, 2]) if rev else None

        prep = [pb(f"prep{b}", [C, T]) for b in (0, 1)]
        psB = [pb(f"psB{b}", [C, T]) for b in (0, 1)]
        psC = [pb(f"psC{b}", [C, T]) for b in (0, 1)]
        psY = [pb(f"psY{b}", [C, T]) for b in (0, 1)]

        w_loaded = sem("w_loaded")
        zeroed = sem("zeroed")
        consts = sem("consts")
        wconv_ready = sem("wconv_ready")
        alog_min = sem("alog_min")
        alog_exp = sem("alog_exp")
        x_loaded = [sem(f"x_loaded{p}") for p in (0, 1)]
        add_loaded = [sem(f"add_loaded{p}") for p in (0, 1)]
        filled = [sem(f"filled{b}") for b in (0, 1)]
        drained = [sem(f"drained{b}") for b in (0, 1)]
        sq_ready = sem("sq_ready")
        lnvar_ready = sem("lnvar_ready")
        rstd_ready = sem("rstd_ready")
        xhat_ready = sem("xhat_ready")
        halo_ready = sem("halo_ready")
        xn_ready = sem("xn_ready")
        hi_ready = sem("hi_ready")
        mid_ready = sem("mid_ready")
        lo_ready = sem("lo_ready")
        abs_ready = sem("abs_ready")
        expneg_ready = sem("expneg_ready")
        plus1_ready = sem("plus1_ready")
        log_ready = sem("log_ready")
        lost_ready = sem("lost_ready")
        log_added = sem("log_added")
        relu_ready = sem("relu_ready")
        dt_ready = sem("dt_ready")
        dtx_ready = sem("dtx_ready")
        b_filled = sem("b_filled")
        c_filled = sem("c_filled")
        c_copied = sem("c_copied")
        exp_done = sem("exp_done")
        dbx_done = sem("dbx_done")
        scan_done = sem("scan_done")
        prod_done = sem("prod_done")
        sum_done = sem("sum_done")
        skip_added = sem("skip_added")
        y_ready = sem("y_ready")
        stats_done = sem("stats_done")
        stored = [sem(f"stored{p}") for p in (0, 1)]

        def wait_filled(eng, name, m):
            b = 1 if name == "out" else bank_of[name]
            need(eng, filled[b], index(name, m) + 1)

        def wait_drained(eng, name, m):
            b = 1 if name == "out" else bank_of[name]
            need(eng, drained[b], index(name, m) + 1)

        def wait_bank(eng, name, m):
            b = 1 if name == "out" else bank_of[name]
            need(eng, drained[b], index(name, m))

        def token0(m):
            return m * -T + (CHUNKS - 1) * T if rev else m * T

        def run(eng, prepare, chunk, post):
            prepare(0, 0)
            chunk(0, 0, False)
            chunk(1, 1, False)
            with eng.Fori(1, CHUNKS // 2 - 1) as i:
                chunk(2 * i, 0, False)
                chunk(2 * i + 1, 1, False)
            chunk(CHUNKS - 2, 0, False)
            chunk(CHUNKS - 1, 1, True)
            post(CHUNKS - 1, 1)

        ctx.callback(clear_semaphores, nc, sems)
        block = ctx.enter_context(nc.Block())

        @block.sync
        def _(eng):
            eng.dma_start(w[:, :], w_dram).then_inc(w_loaded, 16)

            def load(m, p):
                start = token0(m)
                if layer3:
                    if not isinstance(m, int) or m >= 2:
                        wait_drained(eng, "mean", m - 2)
                    eng.dma_start(xin[p][:, 0:T], x_dram[:, bass.ds(start, T)]).then_inc(x_loaded[p], 16)
                else:
                    if not isinstance(m, int) or m >= 2:
                            wait_filled(eng, "gate1", m - 2)
                    eng.dma_start(xin[p][:, :], x_dram[:, bass.ds(start, T + 2)]).then_inc(x_loaded[p], 16)
                if rev:
                    if not isinstance(m, int) or m >= 2:
                            wait_drained(eng, "out", m - 2)
                    eng.dma_start(yadd[p][:, :], addend_dram[:, bass.ds(start, T)]).then_inc(add_loaded[p], 16)

            def store(m, p):
                start = token0(m)
                wait_drained(eng, "out", m)
                eng.dma_start(out_dram[:, bass.ds(start, T)], yout[p][:, :]).then_inc(stored[p], 16)

            load(0, 0)
            load(1, 1)
            load(2, 0)
            store(0, 0)
            with eng.Fori(1, CHUNKS // 2 - 1) as i:
                load(2 * i + 1, 1)
                store(2 * i - 1, 1)
                load(2 * i + 2, 0)
                store(2 * i, 0)
            load(CHUNKS - 1, 1)
            store(CHUNKS - 3, 1)
            store(CHUNKS - 2, 0)
            store(CHUNKS - 1, 1)
            if rev:
                eng.wait_ge(stats_done, CHUNKS + 1)
                eng.dma_start(stats_dram, aggr[:, :]).then_inc(stored[0], 16)
            eng.wait_ge(stored[0], 8 * CHUNKS + (16 if rev else 0))
            eng.wait_ge(stored[1], 8 * CHUNKS)

        @block.gpsimd
        def _(eng):
            make_identity(eng, ident, 128, zeroed, consts)
            eng.memset(ones[:, :], 1.0 / C).then_inc(consts, 1)
            eng.memset(select[:, :, :], 0.0).then_inc(zeroed, 1)
            if layer3:
                for p in (0, 1):
                    eng.memset(xn[p][:, 0:HALO], 0.0).then_inc(consts, 1)
            eng.memset(hs[:, :, 0:1] if rev else hs[:, :, T - 1:T], 0.0).then_inc(consts, 1)
            eng.wait_ge(zeroed, 2)
            turn = 2
            for part in range(3):
                if layer3:
                    for half in range(2):
                        view = select[:, 0:STATE, 64 * half:64 * half + 64]
                        eng.affine_select(out=view, in_=view, compare_op=ALU.not_equal, fill=1.0,
                                          base=-32 * part - 16 * half, pattern=[[-1, STATE], [0, 64]],
                                          channel_multiplier=1).then_inc(zeroed, 1)
                        turn += 1
                        eng.wait_ge(zeroed, turn)
                else:
                    eng.affine_select(out=select[:, :, :], in_=select[:, :, :], compare_op=ALU.not_equal,
                                      fill=1.0, base=-32 * part, pattern=[[-1, 32], [0, 128]],
                                      channel_multiplier=1).then_inc(zeroed, 1)
                    turn += 1
                    eng.wait_ge(zeroed, turn)

            def chunk(c, p, last):
                for u in range(UNITS):
                    g = c * UNITS + u
                    k = c * KB + u // PER
                    need(eng, scan_done, g + 1)
                    need(eng, c_copied, k + 1)
                    need(eng, sum_done, g - RING + 1)
                    eng.tensor_tensor(hc[:, u % RING, :], hs[:, u, :], cb[:, (u // PER) % RING, :],
                                      ALU.mult).then_inc(prod_done, 1)

            run(eng, lambda m, p: None, chunk, lambda m, p: None)

        ALL_CONSTS = 5 if layer3 else 3
        SELECT_MADE = 2 + (6 if layer3 else 3)

        @block.scalar
        def _(eng):
            eng.wait_ge(alog_min, 1)
            eng.activation(decay[:, :], decay[:, :], ACT.Exp).then_inc(alog_exp, 1)
            eng.wait_ge(wconv_ready, 2)

            eps_col = epst[:, 0:1]

            def silus(m, p):
                need(eng, y_ready, m - 1)
                for b in (0, 1):
                    wait_filled(eng, f"conv{b}", m)
                    eng.activation(xc[p][:, b, :], prep[b][:, :], ACT.Silu,
                                   bias=W["convb"][:, b:b + 1]).then_inc(drained[b], 1)
                for b in (0, 1):
                    wait_filled(eng, f"gate{b}", m)
                    eng.activation(zs[p][:, b, :], prep[b][:, :], ACT.Silu).then_inc(drained[b], 1)

            def split_hi(m, p, q):
                wait_filled(eng, f"bc{q}", m)
                need(eng, b_filled, KB * (m - 1))
                need(eng, c_filled, KB * (m - 1))
                eng.activation(bcs[p][:, q, :], prep[bank_of[f"bc{q}"]][0:96, :], ACT.Copy).then_inc(hi_ready, 1)

            def split_mid(m, p, q):
                n = m * NBC + q
                wait_drained(eng, f"bc{q}", m)
                eng.activation(bcs[p][32:64, q, :], rest[32:64, :], ACT.Copy).then_inc(mid_ready, 1)
                need(eng, lo_ready, n)
                eng.activation(mid[64:96, :], rest[64:96, :], ACT.Copy).then_inc(mid_ready, 1)

            def copy_dtr(m, p):
                wait_filled(eng, "dtr", m)
                if not isinstance(m, int) or m >= 1:
                    wait_filled(eng, "dt1", m - 1)
                eng.activation(dtr[:, :], prep[bank_of["dtr"]][0:32, :], ACT.Copy).then_inc(drained[1], 1)

            def dt_abs(m, p):
                need(eng, dt_ready, m)
                for b in (0, 1):
                    wait_filled(eng, f"dt{b}", m)
                    eng.activation(sp[:, b, :], prep[b][:, :], ACT.Abs,
                                   bias=W["bdt"][:, b:b + 1]).then_inc(abs_ready, 1)

            def dt_log(m, p):
                need(eng, abs_ready, 2 * m + 2)
                eng.activation(sp[:, :, :], sp[:, :, :], ACT.Exp, scale=-1.0).then_inc(expneg_ready, 1)
                need(eng, expneg_ready, m + 1)
                eng.activation(sp1[:, :, :], sp[:, :, :], ACT.Identity, bias=1.0).then_inc(plus1_ready, 1)
                need(eng, plus1_ready, m + 1)
                eng.activation(spl[:, :, :], sp1[:, :, :], ACT.Ln).then_inc(log_ready, 1)

            def square(m, p):
                wait_drained(eng, "mean", m)
                if not isinstance(m, int) or m >= 1:
                    need(eng, xhat_ready, m)
                eng.activation(sq[:, :], cen[:, :], ACT.Square).then_inc(sq_ready, 1)

            def rstd(m, p):
                wait_filled(eng, "var", m)
                eng.activation(sq[:, :], prep[1][:, :], ACT.Ln, bias=eps_col).then_inc(lnvar_ready, 1)
                need(eng, lnvar_ready, m + 1)
                eng.activation(sq[:, :], sq[:, :], ACT.Exp, scale=-0.5).then_inc(drained[1], 1)

            def evacuate(m, p):
                wait_filled(eng, "out", m)
                need(eng, stored[p], 8 * (m - p))
                eng.activation(yout[p][:, :], prep[1][:, :], ACT.Copy).then_inc(drained[1], 1)

            steps = {}
            if layer3:
                steps = {6: [square], 8: [rstd], 11: [silus]}
                for at_unit, q in ((14, 0), (18, 2)):
                    steps[at_unit] = [lambda m, p, q=q: split_hi(m, p, q)]
                    steps[at_unit + 1] = [lambda m, p, q=q: split_mid(m, p, q),
                                          lambda m, p, q=q: split_hi(m, p, q + 1)]
                    steps[at_unit + 2] = [lambda m, p, q=q: split_mid(m, p, q + 1)]
                steps[22] = [copy_dtr]
                steps[24] = [dt_abs, dt_log]
            else:
                steps = {6: [silus],
                         11: [lambda m, p: split_hi(m, p, 0), lambda m, p: split_mid(m, p, 0), copy_dtr],
                         15: [dt_abs, dt_log]}

            def prepare(m, p):
                for pos in sorted(steps):
                    for step in steps[pos]:
                        step(m, p)

            def chunk(c, p, last):
                for u in range(UNITS):
                    g = c * UNITS + u
                    k = c * KB + u // PER
                    if u == 0:
                        need(eng, dt_ready, c + 1)
                    need(eng, scan_done, g - RING + 1)
                    eng.activation(da[:, u % RING, :], dt[p][:, u % 2, :], ACT.Exp,
                                   scale=decay[:, u:u + 1]).then_inc(exp_done, 1)
                    if u % PER == 0:
                        need(eng, c_filled, k + 1)
                        need(eng, prod_done, (k - RING + 1) * PER)
                        eng.activation(cb[:, (u // PER) % RING, :], psC[(u // PER) % 2][:, :],
                                       ACT.Copy).then_inc(c_copied, 1)
                    if u == 5 and kind == "forward" and not (isinstance(c, int) and c == 0):
                        evacuate(c - 1, 1 - p)
                    if not last:
                        for step in steps.get(u, []):
                            step(c + 1, 1 - p)

            run(eng, prepare, chunk, (lambda m, p: evacuate(m, p)) if kind == "forward" else (lambda m, p: None))

        @block.vector
        def _(eng):
            eng.wait_ge(w_loaded, 16)
            eng.tensor_scalar(decay[:, :], W["alog"], 80.0, None, ALU.min).then_inc(alog_min, 1)
            eng.wait_ge(alog_exp, 1)
            eng.tensor_scalar(decay[:, :], decay[:, :], -1.0, None, ALU.mult).then_inc(wconv_ready, 1)
            eng.memset(epst[:, :], EPS).then_inc(wconv_ready, 1)
            for k in range(TAPS):
                eng.tensor_tensor(wconv[:, k, :, :], W["win"].rearrange("p (b m) -> p b m", b=2),
                                  W["tapw"][:, 256 * k:256 * k + 256].rearrange("p (b m) -> p b m", b=2),
                                  ALU.mult).then_inc(wconv_ready, 1)
            eng.wait_ge(consts, ALL_CONSTS)

            def center(m, p):
                wait_filled(eng, "mean", m)
                need(eng, x_loaded[p], 8 * (m - p) + 16)
                need(eng, xhat_ready, m)
                need(eng, sq_ready, m)
                eng.tensor_tensor(cen[:, :], xin[p][:, 0:T], prep[0][:, :], ALU.subtract).then_inc(drained[0], 1)

            def normalize(m, p):
                wait_drained(eng, "var", m)
                eng.tensor_tensor(cen[:, :], cen[:, :], sq[:, :], ALU.mult).then_inc(rstd_ready, 1)
                if not isinstance(m, int) or m >= 2:
                    wait_filled(eng, "gate1", m - 2)
                    wait_drained(eng, "out", m - 2)
                if not isinstance(m, int) or m >= 1:
                    eng.tensor_copy(xn[p][:, 0:HALO], xn[1 - p][:, T:T + HALO]).then_inc(halo_ready, 1)
                need(eng, rstd_ready, m + 1)
                eng.tensor_scalar(xn[p][:, HALO:HALO + T], cen[:, :], W["ln_g"], W["ln_b"],
                                  ALU.mult, ALU.add).then_inc(xhat_ready, 1)

            def split_rest(m, p, q):
                n = m * NBC + q
                need(eng, hi_ready, n + 1)
                need(eng, lo_ready, n)
                need(eng, mid_ready, 2 * n)
                b = bank_of[f"bc{q}"]
                eng.tensor_tensor(rest[:, :], prep[b][0:96, :], bcs[p][:, q, :],
                                  ALU.subtract).then_inc(drained[b], 1)

            def split_lo(m, p, q):
                n = m * NBC + q
                need(eng, mid_ready, 2 * n + 2)
                eng.tensor_tensor(bcs[p][64:96, q, :], rest[64:96, :], mid[64:96, :],
                                  ALU.subtract).then_inc(lo_ready, 1)

            def relu_dt(m, p):
                need(eng, exp_done, UNITS * (m - 1))
                for b in (0, 1):
                    need(eng, abs_ready, 2 * m + 1 + b)
                    eng.tensor_scalar(dt[p][:, b, :], prep[b][:, :], W["bdt"][:, b:b + 1], 0.0,
                                      ALU.add, ALU.max).then_inc(drained[b], 1)

            def lost_part(m, p):
                need(eng, plus1_ready, m + 1)
                eng.scalar_tensor_tensor(sp[:, :, :], sp1[:, :, :], -1.0, sp[:, :, :],
                                         ALU.add, ALU.subtract).then_inc(lost_ready, 1)

            def add_log(m, p):
                need(eng, log_ready, m + 1)
                need(eng, lost_ready, m + 1)
                eng.tensor_tensor(spl[:, :, :], spl[:, :, :], sp[:, :, :], ALU.subtract).then_inc(log_added, 1)

            def add_relu(m, p):
                need(eng, log_added, m + 1)
                for b in (0, 1):
                    wait_drained(eng, f"dt{b}", m)
                eng.tensor_tensor(dt[p][:, :, :], dt[p][:, :, :], spl[:, :, :], ALU.add).then_inc(dt_ready, 1)

            def scale_x(m, p):
                need(eng, dt_ready, m + 1)
                wait_drained(eng, "conv0", m)
                wait_drained(eng, "conv1", m)
                eng.tensor_tensor(dtx[p][:, :, :], dt[p][:, :, :], xc[p][:, :, :], ALU.mult).then_inc(dtx_ready, 1)

            def skip(m, p):
                need(eng, sum_done, UNITS * (m + 1))
                if not isinstance(m, int) or m >= 1:
                    wait_filled(eng, "out", m - 1)
                for b in (0, 1):
                    eng.scalar_tensor_tensor(yv[:, b, :], xc[p][:, b, :], W["dskip"][:, b:b + 1],
                                             psY[b][:, :], ALU.mult, ALU.add).then_inc(skip_added, 1)

            def gate(m, p):
                need(eng, skip_added, 2 * m + 2)
                wait_drained(eng, "gate0", m)
                wait_drained(eng, "gate1", m)
                eng.tensor_tensor(yv[:, :, :], yv[:, :, :], zs[p][:, :, :], ALU.mult).then_inc(y_ready, 1)

            def add_out(m, p):
                wait_filled(eng, "out", m)
                need(eng, stored[p], 8 * (m - p))
                if rev:
                    need(eng, add_loaded[p], 8 * (m - p) + 16)
                    other = yadd[p][:, :]
                else:
                    other = xn[p][:, HALO:HALO + T]
                eng.tensor_tensor(yout[p][:, :], other, prep[1][:, :], ALU.add).then_inc(drained[1], 1)
                wait_drained(eng, "out", m)
                if rev:
                    eng.bn_stats(stats[:, m, :] if isinstance(m, int) else stats[:, bass.ds(m, 1), :],
                                 yout[p][:, :]).then_inc(stats_done, 1)

            if layer3:
                steps = {6: [center], 9: [normalize], 15: [lambda m, p: split_rest(m, p, 0)],
                         16: [lambda m, p: split_lo(m, p, 0), lambda m, p: split_rest(m, p, 1)],
                         17: [lambda m, p: split_lo(m, p, 1)],
                         19: [lambda m, p: split_rest(m, p, 2)],
                         20: [lambda m, p: split_lo(m, p, 2), lambda m, p: split_rest(m, p, 3)],
                         21: [lambda m, p: split_lo(m, p, 3)],
                         25: [relu_dt], 26: [lost_part], 28: [add_log], 29: [add_relu], 31: [scale_x]}
            else:
                steps = {12: [lambda m, p: split_rest(m, p, 0)], 14: [lambda m, p: split_lo(m, p, 0)],
                         17: [relu_dt], 18: [lost_part], 20: [add_log], 21: [add_relu], 23: [scale_x]}

            def prepare(m, p):
                for pos in sorted(steps):
                    for step in steps[pos]:
                        step(m, p)

            def product(c, p, u):
                k = c * KB + u // PER
                need(eng, b_filled, k + 1)
                if u == 0:
                    need(eng, dtx_ready, c + 1)
                need(eng, scan_done, c * UNITS + u - RING + 1)
                eng.tensor_tensor(dbx[:, u % RING, :], dtx[p][:, u % 2, :], psB[(u // PER) % 2][:, :],
                                  ALU.mult).then_inc(dbx_done, 1)

            def scan(c, p, u):
                g = c * UNITS + u
                need(eng, exp_done, g + 1)
                need(eng, dbx_done, g + 1)
                need(eng, prod_done, g - UNITS + 1)
                need(eng, scan_done, g - UNITS + 1)
                if rev:
                    eng.tensor_tensor_scan(hs[:, u, ::-1], da[:, u % RING, ::-1], dbx[:, u % RING, ::-1],
                                           hs[:, u, 0:1], ALU.mult, ALU.add).then_inc(scan_done, 1)
                else:
                    eng.tensor_tensor_scan(hs[:, u, :], da[:, u % RING, :], dbx[:, u % RING, :],
                                           hs[:, u, T - 1:T], ALU.mult, ALU.add).then_inc(scan_done, 1)

            def chunk(c, p, last):
                first = isinstance(c, int) and c == 0
                for u in range(UNITS):
                    product(c, p, u)
                    if u > 0:
                        scan(c, p, u - 1)
                    if not first:
                        if u == 1:
                            skip(c - 1, 1 - p)
                        if u == 3:
                            gate(c - 1, 1 - p)
                        if u == 5 and kind != "forward":
                            add_out(c - 1, 1 - p)
                    if not last:
                        for step in steps.get(u, []):
                            step(c + 1, 1 - p)
                scan(c, p, UNITS - 1)

            def post(m, p):
                skip(m, p)
                gate(m, p)
                if kind != "forward":
                    add_out(m, p)
                if rev:
                    eng.wait_ge(stats_done, CHUNKS)
                    eng.bn_aggr(aggr[:, :], stats[:, :, :].rearrange("p n s -> p (n s)")).then_inc(stats_done, 1)

            run(eng, prepare, chunk, post)

        @block.tensor
        def _(eng):
            eng.wait_ge(w_loaded, 16)
            eng.wait_ge(wconv_ready, 2 + TAPS)
            eng.wait_ge(consts, ALL_CONSTS)
            eng.wait_ge(zeroed, SELECT_MADE)

            def source(p, shift):
                if layer3:
                    return xn[p][:, HALO - shift:HALO - shift + T]
                first = 1 + shift if rev else 1 - shift
                return xin[p][:, first:first + T]

            def mean(m, p):
                need(eng, x_loaded[p], 8 * (m - p) + 16)
                wait_bank(eng, "mean", m)
                eng.matmul(prep[0][:, :], ones[:, :], xin[p][:, 0:T], start=True, stop=True).then_inc(filled[0], 1)

            def var(m, p):
                need(eng, sq_ready, m + 1)
                wait_bank(eng, "var", m)
                eng.matmul(prep[1][:, :], ones[:, :], sq[:, :], start=True, stop=True).then_inc(filled[1], 1)

            def conv(m, p):
                if layer3:
                    need(eng, xhat_ready, m + 1)
                    if not isinstance(m, int) or m >= 1:
                        need(eng, halo_ready, m)
                else:
                    need(eng, x_loaded[p], 8 * (m - p) + 16)
                for b in (0, 1):
                    wait_bank(eng, f"conv{b}", m)
                    for k in range(TAPS):
                        mm = eng.matmul(prep[b][:, :], wconv[:, k, b, :], source(p, TAPS - 1 - k),
                                        start=(k == 0), stop=(k == TAPS - 1))
                    mm.then_inc(filled[b], 1)

            def gates(m, p):
                for b in (0, 1):
                    wait_bank(eng, f"gate{b}", m)
                    eng.matmul(prep[b][:, :], W["wz"][:, 128 * b:128 * b + 128], source(p, 0),
                               start=True, stop=True).then_inc(filled[b], 1)

            def bc(m, p, q):
                name = f"bc{q}"
                wait_bank(eng, name, m)
                out = prep[bank_of[name]][0:96, :]
                if layer3:
                    weight = W["wb"] if q < 2 else W["wc"]
                    eng.matmul(out, weight, xc[p][:, q % 2, :], start=True, stop=True).then_inc(filled[bank_of[name]], 1)
                else:
                    for b in (0, 1):
                        mm = eng.matmul(out, W["wbc"][:, 96 * b:96 * b + 96], xc[p][:, b, :],
                                        start=(b == 0), stop=(b == 1))
                    mm.then_inc(filled[0], 1)

            def rank_rows(m, p):
                wait_bank(eng, "dtr", m)
                for b in (0, 1):
                    mm = eng.matmul(prep[1][0:32, :], W["wdtr"][:, 32 * b:32 * b + 32], xc[p][:, b, :],
                                    start=(b == 0), stop=(b == 1))
                mm.then_inc(filled[1], 1)

            def dts(m, p):
                wait_drained(eng, "dtr", m)
                for b in (0, 1):
                    wait_bank(eng, f"dt{b}", m)
                    eng.matmul(prep[b][:, :], W["wdt"][0:32, 128 * b:128 * b + 128], dtr[:, :],
                               start=True, stop=True).then_inc(filled[b], 1)

            def project_out(m, p):
                need(eng, y_ready, m + 1)
                wait_bank(eng, "out", m)
                for b in (0, 1):
                    mm = eng.matmul(prep[1][:, :], W["wout"][:, 128 * b:128 * b + 128], yv[:, b, :],
                                    start=(b == 0), stop=(b == 1))
                mm.then_inc(filled[1], 1)

            if layer3:
                steps = {5: [mean], 7: [var], 10: [conv], 11: [gates],
                         13: [lambda m, p: bc(m, p, 0), lambda m, p: bc(m, p, 1)],
                         17: [lambda m, p: bc(m, p, 2), lambda m, p: bc(m, p, 3)],
                         21: [rank_rows], 23: [dts]}
            else:
                steps = {5: [conv], 6: [gates], 10: [lambda m, p: bc(m, p, 0), rank_rows], 14: [dts]}

            def prepare(m, p):
                for pos in sorted(steps):
                    for step in steps[pos]:
                        step(m, p)

            LAG = 3

            def sum_state(c, p, u):
                g = c * UNITS + u
                need(eng, prod_done, g + 1)
                if u == 0:
                    need(eng, skip_added, 2 * c)
                eng.matmul(psY[u % 2][:, :], ident[:, :], hc[:, u % RING, :], start=(u < 2),
                           stop=(u >= UNITS - 2)).then_inc(sum_done, 1)

            def chunk(c, p, last):
                for u in range(UNITS):
                    if u % PER == 0:
                        k = c * KB + u // PER
                        kk = u // PER
                        if u == 0:
                            need(eng, lo_ready, (c + 1) * NBC)
                            need(eng, mid_ready, 2 * (c + 1) * NBC)
                        qb, qc = (u % 2, 2 + u % 2) if layer3 else (0, 0)
                        rb, rc = (u // 2, u // 2) if layer3 else (kk, STATE + kk)
                        need(eng, dbx_done, (k - 1) * PER)
                        eng.matmul(psB[kk % 2][:, :], select[:, rb, :], bcs[p][:, qb, :],
                                   start=True, stop=True).then_inc(b_filled, 1)
                        need(eng, c_copied, k - 1)
                        eng.matmul(psC[kk % 2][:, :], select[:, rc, :], bcs[p][:, qc, :],
                                   start=True, stop=True).then_inc(c_filled, 1)
                    if u >= LAG:
                        sum_state(c, p, u - LAG)
                    if u == 4 and not (isinstance(c, int) and c == 0):
                        project_out(c - 1, 1 - p)
                    if not last:
                        for step in steps.get(u, []):
                            step(c + 1, 1 - p)
                for u in range(UNITS - LAG, UNITS):
                    sum_state(c, p, u)

            run(eng, prepare, chunk, project_out)



def attention_phase(nc, vertical, x_dram, w_dram, out_dram):
    tag = "av" if vertical else "ah"
    at, width = offsets(ATTN_COLS)
    small = at["kc"][0]
    PAIRS = LINES // 2
    BLOCKS = LINES // BLOCK
    PB = BLOCK // 2
    BUFS = 3
    W2 = 2 * SIDE
    CORE = 6 * HD
    KROWS = CORE + 3 * S7
    Q_PARTS, K_PARTS = (0, 0, 1, 1, 2, 0), (0, 1, 0, 1, 0, 2)
    NUM, DEN = 0, 1

    with ExitStack() as ctx:
        def sb(name, shape, dt=F32):
            return ctx.enter_context(nc.sbuf_tensor(f"{tag}_{name}", shape, dt))

        def pb(name, shape):
            return ctx.enter_context(nc.psum_tensor(f"{tag}_{name}", shape, F32))

        sems = []

        def sem(name):
            sems.append(ctx.enter_context(nc.semaphore(f"{tag}_{name}")))
            return sems[-1]

        w = sb("w", [C, small])
        W = {n: w[:, a:b] for n, (a, b) in at.items() if b <= small}
        shape = [C, SIDE, BLOCK] if vertical else [C, BLOCK, SIDE]
        xb = [sb(f"xb{p}", shape) for p in range(BUFS)]
        kc = xb[2][:, :, :].rearrange("c a b -> c (a b)")[:, 0:HEADS * SIDE]
        ident = sb("ident", [C, 128])
        identb = sb("identb", [C, 128], BF16)
        sel = sb("sel", [C, 2, HEADS, 3, CORE], BF16)
        selm = sb("selm", [3 * HEADS, HEADS, HALF], BF16)
        ones = sb("ones", [HALF, 2, 32])
        zero_row = sb("zero_row", [C, SIDE])
        bqs = sb("bqs", [C, 1])
        tb1 = sb("tb1", [C, SIDE], BF16)
        tb2 = sb("tb2", [C, SIDE], BF16)
        tf = [sb(f"tf{i}", [C, SIDE]) for i in (0, 1)]
        xq = [sb(f"xq{p}", [C, W2]) for p in (0, 1)]
        xv = [sb(f"xv{p}", [C, W2]) for p in (0, 1)]
        full = sb("full", [C, 2, W2])
        rest = sb("rest", [C, 2, W2])
        parts = [sb(f"parts{p}", [C, 3, 2, W2], BF16) for p in (0, 1)]
        st = [sb(f"st{p}", [C, 2, HEADS, W2], BF16) for p in (0, 1)]
        va = [sb(f"va{p}", [HALF, 4, 4, 2, 32]) for p in (0, 1)]
        mx = sb("mx", [HALF, 4, HEADS])
        mxr = sb("mxr", [HALF, 4, HEADS])
        mxp = sb("mxp", [HALF, 4, 3, HEADS], BF16)
        mxs = [sb(f"mxs{p}", [3 * HEADS, W2], BF16) for p in (0, 1)]
        pt = sb("pt", [HALF, 16, 2, SIDE])
        rec = sb("rec", [C, SIDE])
        on = sb("on", [C, W2])
        obuf = [sb(f"obuf{p}", [C, W2]) for p in (0, 1)]

        psS = [pb(f"psS{b}", [HALF, 2, SIDE]) for b in (0, 1)]
        psT = [pb(f"psT{b}", [HALF, 2, SIDE]) for b in (0, 1)]
        psE = [pb(f"psE{b}", [C, SIDE]) for b in (0, 1)]
        psO = pb("psO", [C, 2, SIDE])
        psP = pb("psP", [C, 512])

        w_loaded = sem("w_loaded")
        zeroed = sem("zeroed")
        consts = sem("consts")
        setup = sem("setup")
        blk_loaded = [sem(f"blk_loaded{p}") for p in range(BUFS)]
        blk_stored = [sem(f"blk_stored{p}") for p in range(BUFS)]
        edge_stored = sem("edge_stored")
        xq_ready = sem("xq_ready")
        xv_ready = sem("xv_ready")
        q_filled = sem("q_filled")
        k_filled = sem("k_filled")
        v_filled = sem("v_filled")
        q_ready = sem("q_ready")
        k_ready = sem("k_ready")
        v_ready = sem("v_ready")
        part1_ready = sem("part1_ready")
        rest_ready = sem("rest_ready")
        part2_ready = sem("part2_ready")
        part3_ready = sem("part3_ready")
        e_filled = [sem("eq_filled"), sem("ek_filled")]
        e_ready = [sem("eq_ready"), sem("ek_ready")]
        s_filled = sem("s_filled")
        max_ready = sem("max_ready")
        max_split = sem("max_split")
        m_filled = sem("m_filled")
        m_ready = sem("m_ready")
        t_filled = sem("t_filled")
        p_ready = sem("p_ready")
        pv_done = sem("pv_done")
        rec_ready = sem("rec_ready")
        norm_done = sem("norm_done")
        obuf_ready = sem("obuf_ready")
        line_out = sem("line_out")

        def has(n):
            return not isinstance(n, int) or 0 <= n < PAIRS

        HEAD, TAIL = 2, PAIRS - 4

        def run(eng, iteration):
            for m in range(-3, HEAD):
                iteration(m, m % 2)
            with eng.Fori(HEAD // 2, TAIL // 2) as i:
                iteration(2 * i, 0)
                iteration(2 * i + 1, 1)
            for m in range(TAIL, PAIRS + 1):
                iteration(m, m % 2)

        def stacked(m, p, u):
            return (m + 2, p, u - 1) if u >= 1 else (m + 1, 1 - p, 15)

        def unit(v):
            return v % HEADS, slice(v // HEADS * SIDE, v // HEADS * SIDE + SIDE)

        CONSTS = 7
        SETUP = 3 + 12 + 7 * HEADS + 3 + 8

        ctx.callback(clear_semaphores, nc, sems)
        block = ctx.enter_context(nc.Block())

        @block.sync
        def _(eng):
            eng.dma_start(w[:, :], w_dram[:, 0:small]).then_inc(w_loaded, 16)
            eng.dma_start(kc[CORE:C, :], w_dram[CORE:C, small:width]).then_inc(w_loaded, 16)

            def part(dram, b, first_row):
                if vertical:
                    return dram[:, first_row:first_row + SIDE, b * BLOCK:(b + 1) * BLOCK]
                return dram[:, first_row + b * BLOCK:first_row + (b + 1) * BLOCK, :]

            def load(b):
                need(eng, blk_stored[b % BUFS], 16 * (b // BUFS))
                eng.dma_start(xb[b % BUFS][:, :, :], part(x_dram, b, 0)).then_inc(blk_loaded[b % BUFS], 16)

            load(0)
            load(1)
            eng.wait_ge(consts, CONSTS)
            eng.wait_ge(setup, SETUP)
            load(2)
            eng.dma_start(out_dram[:, 0, :], zero_row[:, :]).then_inc(edge_stored, 16)
            eng.dma_start(out_dram[:, SIDE + 1, :], zero_row[:, :]).then_inc(edge_stored, 16)
            for b in range(BLOCKS):
                eng.wait_ge(line_out, PB * (b + 1))
                eng.dma_start(part(out_dram, b, 1), xb[b % BUFS][:, :, :]).then_inc(blk_stored[b % BUFS], 16)
                if b + BUFS < BLOCKS:
                    load(b + BUFS)
            eng.wait_ge(edge_stored, 32)
            for p in range(BUFS):
                eng.wait_ge(blk_stored[p], 16 * len(range(p, BLOCKS, BUFS)))

        @block.gpsimd
        def _(eng):
            make_identity(eng, ident, 128, zeroed, consts)
            eng.memset(zero_row[:, :], 0.0).then_inc(consts, 1)
            eng.memset(sel[:, :, :, :, :], 0.0).then_inc(consts, 1)
            eng.memset(ones[:, :, :], 0.0).then_inc(zeroed, 1)
            eng.wait_ge(zeroed, 2)
            eng.memset(ones[:, 0, 0:HD], 1.0).then_inc(consts, 1)
            eng.memset(ones[:, 1, HD:2 * HD], 1.0).then_inc(consts, 1)
            for p in (0, 1):
                eng.memset(va[p][:, :, :, :, :], 0.0).then_inc(consts, 1)

            def lines(tile, r):
                at_r = slice(r, r + 2) if isinstance(r, int) else bass.ds(r, 2)
                if vertical:
                    return tile[:, :, at_r].rearrange("c s r -> c r s")
                return tile[:, at_r, :]

            two = lambda tile: tile[:, :].rearrange("c (r s) -> c r s", r=2)

            def take_q(n, p, tile, r):
                need(eng, k_filled, n - 1)
                eng.tensor_copy(two(xq[p]), lines(tile, r)).then_inc(xq_ready, 1)

            def take_v(n, p, tile, r):
                need(eng, v_filled, n - 1)
                eng.tensor_copy(two(xv[p]), lines(tile, r)).then_inc(xv_ready, 1)

            def put(n, p, tile, r):
                need(eng, obuf_ready, n + 1)
                eng.tensor_copy(lines(tile, r), two(obuf[p])).then_inc(line_out, 1)

            QA, VA = 5, 3

            def one_block(b):
                n0, buf, last = b * PB, xb[b % BUFS], b == BLOCKS - 1
                nxt = xb[(b + 1) % BUFS]
                with eng.Fori(0, (PB - QA) // 2) as k:
                    for j in (0, 1):
                        par = (n0 + j) % 2
                        take_q(n0 + 2 * k + j + QA, (par + QA) % 2, buf, 4 * k + 2 * j + 2 * QA)
                        take_v(n0 + 2 * k + j + VA, (par + VA) % 2, buf, 4 * k + 2 * j + 2 * VA)
                        put(n0 + 2 * k + j, par, buf, 4 * k + 2 * j)
                for r in range((PB - QA) // 2 * 2, PB):
                    n = n0 + r
                    for ahead, take in ((QA, take_q), (VA, take_v)):
                        if r + ahead < PB:
                            take(n + ahead, (n + ahead) % 2, buf, 2 * (r + ahead))
                        elif not last:
                            need(eng, blk_loaded[(b + 1) % BUFS], 16 * ((b + 1) // BUFS) + 16)
                            take(n + ahead, (n + ahead) % 2, nxt, 2 * (r + ahead - PB))
                    put(n, n % 2, buf, 2 * r)

            eng.wait_ge(blk_loaded[0], 16)
            for n in range(2):
                take_q(n, n % 2, xb[0], 2 * n)
                take_v(n, n % 2, xb[0], 2 * n)
            take_q(2, 0, xb[0], 4)
            take_q(3, 1, xb[0], 6)
            take_v(2, 0, xb[0], 4)
            take_q(4, 0, xb[0], 8)
            for b in range(BLOCKS):
                one_block(b)

        @block.scalar
        def _(eng):
            eng.wait_ge(w_loaded, 32)
            eng.wait_ge(consts, CONSTS)
            eng.wait_ge(setup, SETUP)

            def exponential(m, u):
                need(eng, t_filled, 16 * m + u + 1)
                if u % 8 == 0:
                    need(eng, pv_done, 2 * m - 1 + u // 8)
                eng.activation(pt[:, u, :, :], psT[u % 2][:, :, :], ACT.Exp).then_inc(p_ready, 1)

            def query_stack(n, p, v):
                need(eng, e_filled[0], 16 * n + v + 1)
                h, line = unit(v)
                eng.activation(st[p][0:CORE, 0, h, line], psE[0][0:CORE, :], ACT.Copy).then_inc(e_ready[0], 1)

            def queries(n):
                need(eng, q_filled, n + 1)
                need(eng, rest_ready, n)
                eng.activation(full[:, 0, :], psP[:, 0:W2], ACT.Identity, bias=bqs[:, 0:1],
                               scale=float(HD) ** -0.5).then_inc(q_ready, 1)

            def first_parts(n, p):
                need(eng, q_ready, n + 1)
                need(eng, k_ready, n + 1)
                need(eng, e_filled[1], 16 * (n - 1))
                eng.activation(parts[p][:, 0, :, :], full[:, :, :], ACT.Copy).then_inc(part1_ready, 1)

            def second_parts(n, p):
                need(eng, rest_ready, n + 1)
                eng.activation(parts[p][:, 1, :, :], rest[:, :, :], ACT.Copy).then_inc(part2_ready, 1)

            def values(n, p):
                need(eng, v_filled, n + 1)
                need(eng, pv_done, 2 * (n - 1))
                src = psP[0:HALF, 0:4 * C].rearrange("p (a j s d) -> p a j s d", a=4, j=4, s=2)
                for s in (0, 1):
                    eng.activation(va[p][:, :, :, s, HD * s:HD * s + HD], src[:, :, :, s, :],
                                   ACT.Copy).then_inc(v_ready, 1)

            def finished(n, p):
                need(eng, norm_done, 2 * n + 2)
                need(eng, line_out, n - 1)
                eng.activation(obuf[p][:, :], on[:, :], ACT.Identity, bias=W["bv"]).then_inc(obuf_ready, 1)

            def iteration(m, p):
                for u in range(16):
                    if has(m):
                        exponential(m, u)
                    n, pn, v = stacked(m, p, u)
                    if has(n):
                        query_stack(n, pn, v)
                    if u == 6 and has(m + 3):
                        queries(m + 3)
                    if u == 8 and has(m + 3):
                        first_parts(m + 3, 1 - p)
                    if u == 9 and has(m + 1):
                        values(m + 1, 1 - p)
                    if u == 10 and has(m - 1):
                        finished(m - 1, 1 - p)
                    if u == 12 and has(m + 3):
                        second_parts(m + 3, 1 - p)

            run(eng, iteration)

        @block.vector
        def _(eng):
            eng.wait_ge(w_loaded, 32)
            eng.wait_ge(consts, CONSTS)
            eng.tensor_scalar(bqs[:, :], W["bq"], float(HD) ** -0.5, None, ALU.mult).then_inc(setup, 1)
            eng.tensor_copy(identb[:, :], ident[:, :]).then_inc(setup, 1)
            eng.tensor_copy(selm[:, :, :], W["selm"][0:3 * HEADS, :].rearrange("c (h k) -> c h k", h=HEADS)
                            .broadcast_to([3 * HEADS, HEADS, HALF])).then_inc(setup, 1)
            heads = ident[:, :].rearrange("c (h d) -> c h d", h=HEADS)
            for t, of_slot in enumerate((Q_PARTS, K_PARTS)):
                for g, part in enumerate(of_slot):
                    eng.tensor_copy(sel[:, t, :, part, HD * g:HD * g + HD], heads).then_inc(setup, 1)
            rows = slice(CORE, C)
            done = 3 + 12
            for h in range(HEADS):
                table = kc[rows, h * SIDE:(h + 1) * SIDE]
                mask = lambda k: W["mask"][rows, k:k + 1]
                need(eng, setup, done)
                eng.tensor_copy(tb1[rows, :], table).then_inc(setup, 1)
                eng.wait_ge(setup, done + 1)
                eng.tensor_tensor(tf[0][rows, :], table, tb1[rows, :], ALU.subtract).then_inc(setup, 1)
                eng.wait_ge(setup, done + 2)
                eng.tensor_copy(tb2[rows, :], tf[0][rows, :]).then_inc(setup, 1)
                eng.wait_ge(setup, done + 3)
                eng.tensor_tensor(tf[1][rows, :], tf[0][rows, :], tb2[rows, :], ALU.subtract).then_inc(setup, 1)
                eng.wait_ge(setup, done + 4)
                eng.tensor_scalar(tf[0][rows, :], tb1[rows, :], mask(0), None, ALU.mult).then_inc(setup, 1)
                eng.wait_ge(setup, done + 5)
                eng.scalar_tensor_tensor(tf[0][rows, :], tb2[rows, :], mask(1), tf[0][rows, :],
                                         ALU.mult, ALU.add).then_inc(setup, 1)
                eng.wait_ge(setup, done + 6)
                eng.scalar_tensor_tensor(st[0][rows, 1, h, 0:SIDE], tf[1][rows, :], mask(2), tf[0][rows, :],
                                         ALU.mult, ALU.add).then_inc(setup, 1)
                done += 7
            eng.wait_ge(setup, done)
            places = [(p, l) for p in (0, 1) for l in (0, 1)]
            for p, l in places[1:]:
                eng.tensor_copy(st[p][rows, 1, :, SIDE * l:SIDE * l + SIDE], st[0][rows, 1, :, 0:SIDE]).then_inc(setup, 1)
            for p in (0, 1):
                for l in (0, 1):
                    for half in (0, 1):
                        onehot = W["onehot"][rows, :].rearrange("c (o s) -> c o s", o=1).broadcast_to([C - CORE, 4, SIDE])
                        eng.tensor_copy(st[p][rows, 0, 4 * half:4 * half + 4, SIDE * l:SIDE * l + SIDE],
                                        onehot).then_inc(setup, 1)
            eng.wait_ge(setup, SETUP)

            def maximum(n, u):
                if u == 0:
                    need(eng, max_split, 4 * n)
                need(eng, s_filled, 16 * n + u + 1)
                h, l = u % HEADS, u // HEADS
                eng.tensor_reduce(mx[:, 2 * l:2 * l + 2, h:h + 1], psS[u % 2][:, :, :], AX_X, ALU.max,
                                  negate=True).then_inc(max_ready, 1)

            def split_maxima(n):
                need(eng, max_ready, 16 * n + 16)
                need(eng, m_filled, n)
                eng.tensor_copy(mxp[:, :, 0, :], mx[:, :, :]).then_inc(max_split, 1)
                need(eng, max_split, 4 * n + 1)
                eng.tensor_tensor(mxr[:, :, :], mx[:, :, :], mxp[:, :, 0, :], ALU.subtract).then_inc(max_split, 1)
                need(eng, max_split, 4 * n + 2)
                eng.tensor_copy(mxp[:, :, 1, :], mxr[:, :, :]).then_inc(max_split, 1)
                need(eng, max_split, 4 * n + 3)
                eng.tensor_tensor(mxp[:, :, 2, :], mxr[:, :, :], mxp[:, :, 1, :], ALU.subtract).then_inc(max_split, 1)

            def spread_maxima(n, p):
                need(eng, m_filled, n + 1)
                need(eng, t_filled, 16 * (n - 1))
                eng.tensor_copy(mxs[p][:, :], psP[0:3 * HEADS, 0:W2]).then_inc(m_ready, 1)

            def key_stack(n, p, v):
                need(eng, e_filled[1], 16 * n + v + 1)
                h, line = unit(v)
                eng.tensor_copy(st[p][0:CORE, 1, h, line], psE[1][0:CORE, :]).then_inc(e_ready[1], 1)

            def keys(n):
                need(eng, k_filled, n + 1)
                need(eng, rest_ready, n)
                need(eng, part1_ready, n)
                eng.tensor_scalar(full[:, 1, :], psP[:, 0:W2], W["bk"], None, ALU.add).then_inc(k_ready, 1)

            def rests(n, p):
                need(eng, part1_ready, n + 1)
                need(eng, part3_ready, n)
                eng.tensor_tensor(rest[:, :, :], full[:, :, :], parts[p][:, 0, :, :], ALU.subtract).then_inc(rest_ready, 1)

            def third_parts(n, p):
                need(eng, part2_ready, n + 1)
                eng.tensor_tensor(parts[p][:, 2, :, :], rest[:, :, :], parts[p][:, 1, :, :],
                                  ALU.subtract).then_inc(part3_ready, 1)

            def normalize(n, l):
                need(eng, pv_done, 2 * n + l + 1)
                need(eng, norm_done, 2 * n + l)
                eng.reciprocal(rec[:, :], psO[:, DEN, :]).then_inc(rec_ready, 1)
                need(eng, rec_ready, 2 * n + l + 1)
                need(eng, obuf_ready, n)
                eng.tensor_tensor(on[:, SIDE * l:SIDE * l + SIDE], rec[:, :], psO[:, NUM, :],
                                  ALU.mult).then_inc(norm_done, 1)

            def iteration(m, p):
                for u in range(16):
                    if u < 8 and has(m + 1):
                        maximum(m + 1, 2 * u)
                        maximum(m + 1, 2 * u + 1)
                    n, pn, v = stacked(m, p, u)
                    if has(n):
                        key_stack(n, pn, v)
                    if u == 7 and has(m + 3):
                        keys(m + 3)
                    if u == 8 and has(m + 1):
                        split_maxima(m + 1)
                    if u == 8 and has(m - 1):
                        normalize(m - 1, 1)
                    if u == 10 and has(m + 3):
                        rests(m + 3, 1 - p)
                    if u == 11 and has(m + 1):
                        spread_maxima(m + 1, 1 - p)
                    if u == 13 and has(m + 3):
                        third_parts(m + 3, 1 - p)
                    if u == 14 and has(m):
                        normalize(m, 0)

            run(eng, iteration)

        @block.tensor
        def _(eng):
            eng.wait_ge(w_loaded, 32)
            eng.wait_ge(consts, CONSTS)
            eng.wait_ge(setup, SETUP)

            def scores_t(m, p, u):
                if u == 0:
                    need(eng, m_ready, m + 1)
                need(eng, p_ready, 16 * m + u - 1)
                h, line = unit(u)
                for a in (0, 1):
                    keys = slice(line.start + HALF * a, line.start + HALF * a + HALF)
                    eng.matmul(psT[u % 2][:, a, :], st[p][0:KROWS, 1, h, keys], st[p][0:KROWS, 0, h, line],
                               start=True, stop=False)
                    mm = eng.matmul(psT[u % 2][:, a, :], selm[:, h, :], mxs[p][:, line], start=False, stop=True)
                mm.then_inc(t_filled, 1)

            def scores(n, p, u):
                need(eng, e_ready[0], 16 * n + u + 1)
                need(eng, e_ready[1], 16 * n + u + 1)
                need(eng, max_ready, 16 * n + u - 1)
                h, line = unit(u)
                for half in (0, 1):
                    queries = slice(line.start + HALF * half, line.start + HALF * half + HALF)
                    mm = eng.matmul(psS[u % 2][:, half, :], st[p][0:KROWS, 0, h, queries],
                                    st[p][0:KROWS, 1, h, line], start=True, stop=True)
                mm.then_inc(s_filled, 1)

            def stacks(n, p, v):
                if v == 0:
                    need(eng, part3_ready, n + 1)
                h, line = unit(v)
                for t in (0, 1):
                    need(eng, e_ready[t], 16 * n + v)
                    for part in range(3):
                        mm = eng.matmul(psE[t][0:CORE, :], sel[:, t, h, part, :], parts[p][:, part, t, line],
                                        start=(part == 0), stop=(part == 2))
                    mm.then_inc(e_filled[t], 1)

            def products(n, p, l, quarter):
                what, s = quarter // 2, quarter % 2
                if quarter == 0:
                    need(eng, p_ready, 16 * n + 8 * l + 8)
                    need(eng, v_ready, 2 * n + 2)
                    need(eng, norm_done, 2 * n + l)
                for a in (0, 1):
                    for j in range(4):
                        lhsT = va[p][:, 2 * l + a, j, s, :] if what == NUM else ones[:, s, :]
                        mm = eng.matmul(psO[32 * j:32 * j + 32, what, :], lhsT, pt[:, 8 * l + 2 * j + s, a, :],
                                        start=(s == 0 and a == 0), stop=(s == 1 and a == 1))
                if quarter == 3:
                    mm.then_inc(pv_done, 1)

            def project_queries(n, p):
                need(eng, xq_ready, n + 1)
                need(eng, m_ready, n - 2)
                if isinstance(n, int) and n < 3:
                    need(eng, k_ready, n)
                eng.matmul(psP[:, 0:W2], W["wq"], xq[p][:, :], start=True, stop=True).then_inc(q_filled, 1)

            def project_keys(n, p):
                need(eng, q_ready, n + 1)
                eng.matmul(psP[:, 0:W2], W["wk"], xq[p][:, :], start=True, stop=True).then_inc(k_filled, 1)

            def project_values(n, p):
                need(eng, xv_ready, n + 1)
                if has(n + 2):
                    need(eng, k_ready, n + 3)
                else:
                    need(eng, m_ready, n)
                for a in range(4):
                    mm = eng.matmul(psP[0:HALF, C * a:C * a + C], xv[p][:, HALF * a:HALF * a + HALF], W["wv"],
                                    start=True, stop=True)
                mm.then_inc(v_filled, 1)

            def transpose_maxima(n):
                need(eng, max_split, 4 * n + 4)
                need(eng, v_ready, 2 * n + 2)
                for a in range(4):
                    mm = eng.matmul(psP[0:3 * HEADS, HALF * a:HALF * a + HALF], mxp[:, a, :, :],
                                    identb[0:HALF, 0:HALF], start=True, stop=True)
                mm.then_inc(m_filled, 1)

            def iteration(m, p):
                for u in range(16):
                    if has(m):
                        scores_t(m, p, u)
                    if u < 8 and has(m + 1):
                        scores(m + 1, 1 - p, 2 * u)
                        scores(m + 1, 1 - p, 2 * u + 1)
                    n, pn, v = stacked(m, p, u)
                    if has(n):
                        stacks(n, pn, v)
                    if 2 <= u < 6 and has(m - 1):
                        products(m - 1, 1 - p, 1, u - 2)
                    if 9 <= u < 13 and has(m):
                        products(m, p, 0, u - 9)
                    if u == 5 and has(m + 3):
                        project_queries(m + 3, 1 - p)
                    if u == 7 and has(m + 3):
                        project_keys(m + 3, 1 - p)
                    if u == 8 and has(m + 1):
                        project_values(m + 1, 1 - p)
                    if u == 11 and has(m + 1):
                        transpose_maxima(m + 1)

            run(eng, iteration)



def lepe_phase(nc, h_dram, v_dram, w_dram, out_dram):
    ROWS = 8
    PAIRS = ROWS // 2
    STEPS = SIDE // ROWS
    WIDE = SIDE + 2
    at, width = offsets(LEPE_COLS)

    with ExitStack() as ctx:
        def sb(name, shape):
            return ctx.enter_context(nc.sbuf_tensor(f"le_{name}", shape, F32))

        def pb(name, shape):
            return ctx.enter_context(nc.psum_tensor(f"le_{name}", shape, F32))

        sems = []

        def sem(name):
            sems.append(ctx.enter_context(nc.semaphore(f"le_{name}")))
            return sems[-1]

        w = sb("w", [C, width])
        W = {n: w[:, a:b] for n, (a, b) in at.items()}
        ident = sb("ident", [C, 128])
        taps = sb("taps", [C, 9, 128])
        hin = [sb(f"hin{p}", [C, ROWS + 2, WIDE]) for p in (0, 1)]
        vin = [sb(f"vin{p}", [C, ROWS + 2, WIDE]) for p in (0, 1)]
        acc = sb("acc", [C, ROWS, SIDE])
        gh = sb("gh", [C, ROWS, SIDE])
        gv = sb("gv", [C, ROWS, SIDE])
        both = sb("both", [C, ROWS, SIDE])
        total = sb("total", [C, ROWS, SIDE])
        xo = [sb(f"xo{p}", [C, ROWS * SIDE]) for p in (0, 1)]
        edge = sb("edge", [C, 1])
        psH = [pb(f"psH{b}", [C, 2, SIDE]) for b in (0, 1)]
        psP = [pb(f"psP{b}", [C, 2 * SIDE]) for b in (0, 1)]

        w_loaded = sem("w_loaded")
        zeroed = sem("zeroed")
        consts = sem("consts")
        taps_ready = sem("taps_ready")
        loaded = [sem(f"loaded{p}") for p in (0, 1)]
        stored = [sem(f"stored{p}") for p in (0, 1)]
        edge_stored = sem("edge_stored")
        h_filled = sem("h_filled")
        gh_ready = sem("gh_ready")
        tap_done = sem("tap_done")
        gv_ready = sem("gv_ready")
        both_ready = sem("both_ready")
        halfsum_ready = sem("halfsum_ready")
        total_ready = sem("total_ready")
        p_filled = sem("p_filled")
        out_ready = sem("out_ready")

        def run(eng, step):
            step(0, 0)
            step(1, 1)
            with eng.Fori(1, STEPS // 2) as i:
                step(2 * i, 0)
                step(2 * i + 1, 1)

        ctx.callback(clear_semaphores, nc, sems)
        block = ctx.enter_context(nc.Block())

        @block.sync
        def _(eng):
            eng.dma_start(w[:, :], w_dram).then_inc(w_loaded, 16)
            eng.wait_ge(consts, 6)
            eng.dma_start(out_dram[:, 0:1], edge[:, :], allow_slow_non_contiguous=True).then_inc(edge_stored, 16)
            eng.dma_start(out_dram[:, TOKENS + 1:TOKENS + 2], edge[:, :], allow_slow_non_contiguous=True).then_inc(edge_stored, 16)

            def load(n, p):
                need(eng, h_filled, PAIRS * (n - 1))
                need(eng, total_ready, n - 1)
                for tile, dram in ((hin, h_dram), (vin, v_dram)):
                    eng.dma_start(tile[p][:, :, 1:1 + SIDE],
                                  dram[:, bass.ds(ROWS * n, ROWS + 2), :]).then_inc(loaded[p], 16)

            def store(n, p):
                need(eng, out_ready, PAIRS * (n + 1))
                eng.dma_start(out_dram[:, bass.ds(ROWS * SIDE * n + 1, ROWS * SIDE)],
                              xo[p][:, :]).then_inc(stored[p], 16)

            load(0, 0)
            load(1, 1)
            with eng.Fori(0, STEPS // 2 - 1) as i:
                load(2 * i + 2, 0)
                store(2 * i, 0)
                load(2 * i + 3, 1)
                store(2 * i + 1, 1)
            store(STEPS - 2, 0)
            store(STEPS - 1, 1)
            eng.wait_ge(edge_stored, 32)
            for p in (0, 1):
                eng.wait_ge(stored[p], 8 * STEPS)

        @block.gpsimd
        def _(eng):
            make_identity(eng, ident, 128, zeroed, consts)
            eng.memset(edge[:, :], 0.0).then_inc(consts, 1)
            for tile in (*hin, *vin):
                eng.memset(tile[:, :, 0:WIDE:WIDE - 1], 0.0).then_inc(consts, 1)

            def step(n, p):
                need(eng, loaded[p], 16 * (n - p) + 32)
                need(eng, halfsum_ready, n)
                eng.tensor_tensor(both[:, :, :], hin[p][:, 1:1 + ROWS, 1:1 + SIDE],
                                  vin[p][:, 1:1 + ROWS, 1:1 + SIDE], ALU.add).then_inc(both_ready, 1)

            run(eng, step)

        @block.scalar
        def _(eng):
            eng.wait_ge(w_loaded, 16)

            def step(n, p):
                need(eng, total_ready, n)
                for u in range(PAIRS):
                    need(eng, h_filled, PAIRS * n + u + 1)
                    eng.activation(gh[:, 2 * u:2 * u + 2, :], psH[u % 2][:, :, :], ACT.Gelu,
                                   bias=W["b_h"]).then_inc(gh_ready, 1)
                need(eng, tap_done, 9 * (n + 1))
                eng.activation(gv[:, :, :], acc[:, :, :], ACT.Gelu, bias=W["b_v"]).then_inc(gv_ready, 1)
                need(eng, stored[p], 8 * (n - p))
                for u in range(PAIRS):
                    need(eng, p_filled, PAIRS * n + u + 1)
                    eng.activation(xo[p][:, 2 * SIDE * u:2 * SIDE * (u + 1)], psP[u % 2][:, :], ACT.Identity,
                                   bias=W["proj_b"]).then_inc(out_ready, 1)

            run(eng, step)

        @block.vector
        def _(eng):
            eng.wait_ge(w_loaded, 16)
            eng.wait_ge(consts, 6)
            for k in range(9):
                eng.tensor_scalar(taps[:, k, :], ident[:, :], W["tap_h"][:, k:k + 1], None,
                                  ALU.mult).then_inc(taps_ready, 1)

            def step(n, p):
                need(eng, loaded[p], 16 * (n - p) + 32)
                need(eng, gv_ready, n)
                for k in range(9):
                    dy, dx = k // 3, k % 3
                    source = vin[p][:, dy:dy + ROWS, dx:dx + SIDE]
                    tap = W["tap_v"][:, k:k + 1]
                    if k == 0:
                        eng.tensor_scalar(acc[:, :, :], source, tap, None, ALU.mult).then_inc(tap_done, 1)
                    else:
                        need(eng, tap_done, 9 * n + k)
                        eng.scalar_tensor_tensor(acc[:, :, :], source, tap, acc[:, :, :],
                                                 ALU.mult, ALU.add).then_inc(tap_done, 1)
                need(eng, both_ready, n + 1)
                need(eng, gh_ready, PAIRS * (n + 1))
                need(eng, p_filled, PAIRS * n)
                eng.tensor_tensor(total[:, :, :], both[:, :, :], gh[:, :, :], ALU.add).then_inc(halfsum_ready, 1)
                need(eng, gv_ready, n + 1)
                need(eng, halfsum_ready, n + 1)
                eng.tensor_tensor(total[:, :, :], total[:, :, :], gv[:, :, :], ALU.add).then_inc(total_ready, 1)

            run(eng, step)

        @block.tensor
        def _(eng):
            eng.wait_ge(taps_ready, 9)

            def convolve(n, p):
                need(eng, loaded[p], 16 * (n - p) + 32)
                for u in range(PAIRS):
                    need(eng, gh_ready, PAIRS * n + u - 1)
                    for k in range(9):
                        dy, dx = k // 3, k % 3
                        mm = eng.matmul(psH[u % 2][:, :, :], taps[:, k, :],
                                        hin[p][:, 2 * u + dy:2 * u + dy + 2, dx:dx + SIDE],
                                        start=(k == 0), stop=(k == 8))
                    mm.then_inc(h_filled, 1)

            def project(n):
                need(eng, total_ready, n + 1)
                for u in range(PAIRS):
                    need(eng, out_ready, PAIRS * n + u - 1)
                    eng.matmul(psP[u % 2][:, :], W["proj"],
                               total[:, 2 * u:2 * u + 2, :].rearrange("c r s -> c (r s)"),
                               start=True, stop=True).then_inc(p_filled, 1)

            convolve(0, 0)
            project(0)
            convolve(1, 1)
            project(1)
            with eng.Fori(1, STEPS // 2) as i:
                for p in (0, 1):
                    convolve(2 * i + p, p)
                    project(2 * i + p)



def kv_phase(nc, y_dram, stats_dram, x1_dram, w_dram, x2_dram, ut_dram):
    at, width = offsets(GLOBAL_COLS)
    SUB = T // 128
    GROUPS = 2 * HEADS

    with ExitStack() as ctx:
        def sb(name, shape):
            return ctx.enter_context(nc.sbuf_tensor(f"kv_{name}", shape, F32))

        def pb(name, shape):
            return ctx.enter_context(nc.psum_tensor(f"kv_{name}", shape, F32))

        sems = []

        def sem(name):
            sems.append(ctx.enter_context(nc.semaphore(f"kv_{name}")))
            return sems[-1]

        w = sb("w", [C, width])
        W = {n: w[:, a:b] for n, (a, b) in at.items()}
        ident = sb("ident", [C, 128])
        st = sb("st", [C, 2])
        moments = sb("moments", [C, 2])
        gm = sb("gm", [C, 2])
        gvar = sb("gvar", [C, 1])
        gsd = sb("gsd", [C, 1])
        ga = sb("ga", [C, 1])
        gb = sb("gb", [C, 1])
        epst = sb("epst", [C, 1])
        wmean = sb("wmean", [C, GROUPS, 1])
        wcen = sb("wcen", [C, GROUPS, HD])
        yin = [sb(f"yin{p}", [C, T]) for p in (0, 1)]
        xin = [sb(f"xin{p}", [C, T]) for p in (0, 1)]
        act = [sb(f"act{p}", [C, T]) for p in (0, 1)]
        x2 = [sb(f"x2{p}", [C, T]) for p in (0, 1)]
        sq = sb("sq", [C, SUB * GROUPS, HD])
        ss = sb("ss", [C, SUB * GROUPS, 1])
        sd = sb("sd", [C, SUB * GROUPS, 1])
        kvn = sb("kvn", [C, SUB, GROUPS * HD])
        kvw = sb("kvw", [C, SUB, GROUPS * HD])
        kvf = [sb(f"kvf{p}", [C, SUB, GROUPS * HD]) for p in (0, 1)]
        kvb = sb("kvb", [C, 128])
        gmat = sb("gmat", [C, 128])
        ut = sb("ut", [C, 128])
        psK = [pb(f"psK{b}", [C, 2, GROUPS * HD]) for b in range(4)]
        psG = pb("psG", [C, 128])
        psA = pb("psA", [C, 128])
        psU = pb("psU", [C, 128])

        w_loaded = sem("w_loaded")
        zeroed = sem("zeroed")
        consts = sem("consts")
        norm_step = sem("norm_step")
        sd_step = sem("sd_step")
        g_filled = sem("g_filled")
        affine_ready = sem("affine_ready")
        wcen_ready = sem("wcen_ready")
        loaded = [sem(f"loaded{p}") for p in (0, 1)]
        stored = [sem(f"stored{p}") for p in (0, 1)]
        act_ready = sem("act_ready")
        x2_ready = sem("x2_ready")
        k_filled = sem("k_filled")
        sq_ready = sem("sq_ready")
        ss_ready = sem("ss_ready")
        sd_ready = sem("sd_ready")
        sde_ready = sem("sde_ready")
        rsd_ready = sem("rsd_ready")
        kvn_ready = sem("kvn_ready")
        kvw_ready = sem("kvw_ready")
        kvf_ready = sem("kvf_ready")
        kv_summed = sem("kv_summed")
        tail = sem("tail")
        tail_mm = sem("tail_mm")
        ut_stored = sem("ut_stored")

        def run(eng, step):
            step(0, 0)
            step(1, 1)
            with eng.Fori(1, CHUNKS // 2) as i:
                step(2 * i, 0)
                step(2 * i + 1, 1)

        ctx.callback(clear_semaphores, nc, sems)
        block = ctx.enter_context(nc.Block())

        @block.sync
        def _(eng):
            eng.dma_start(w[:, :], w_dram).then_inc(w_loaded, 16)
            eng.dma_start(st[:, :], stats_dram).then_inc(w_loaded, 16)

            def load(n, p):
                need(eng, x2_ready, n - 1)
                eng.dma_start(yin[p][:, :], y_dram[:, bass.ds(T * n, T)]).then_inc(loaded[p], 16)
                eng.dma_start(xin[p][:, :], x1_dram[:, bass.ds(T * n + 1, T)]).then_inc(loaded[p], 16)

            def store(n, p):
                need(eng, x2_ready, n + 1)
                eng.dma_start(x2_dram[:, bass.ds(T * n, T)], x2[p][:, :]).then_inc(stored[p], 16)

            load(0, 0)
            load(1, 1)
            with eng.Fori(0, CHUNKS // 2 - 1) as i:
                load(2 * i + 2, 0)
                store(2 * i, 0)
                load(2 * i + 3, 1)
                store(2 * i + 1, 1)
            store(CHUNKS - 2, 0)
            store(CHUNKS - 1, 1)
            eng.wait_ge(tail, 5)
            eng.dma_start(ut_dram, ut[:, :]).then_inc(ut_stored, 16)
            eng.wait_ge(ut_stored, 16)
            for p in (0, 1):
                eng.wait_ge(stored[p], 8 * CHUNKS)

        @block.gpsimd
        def _(eng):
            make_identity(eng, ident, 128, zeroed, consts)
            eng.memset(epst[:, :], EPS).then_inc(consts, 1)
            eng.wait_ge(w_loaded, 32)

            def step(n, p):
                need(eng, act_ready, n + 1)
                need(eng, stored[p], 8 * (n - p))
                need(eng, k_filled, 4 * (n - 1))
                eng.tensor_tensor(x2[p][:, :], act[p][:, :], xin[p][:, :], ALU.add).then_inc(x2_ready, 1)
                need(eng, kvw_ready, n + 1)
                need(eng, kv_summed, n - 1)
                for s in range(SUB):
                    eng.tensor_tensor(kvf[p][:, s, :], kvw[:, s, :], W["ln_b"], ALU.add).then_inc(kvf_ready, 1)

            run(eng, step)

        @block.scalar
        def _(eng):
            eng.wait_ge(norm_step, 4)
            eng.activation(gsd[:, :], gvar[:, :], ACT.Sqrt, bias=epst[:, 0:1]).then_inc(sd_step, 1)
            eng.wait_ge(affine_ready, 3)

            def gated(n, p):
                need(eng, loaded[p], 16 * (n - p) + 32)
                need(eng, x2_ready, n - 1)
                eng.activation(act[p][:, :], yin[p][:, :], ACT.Silu, bias=gb[:, 0:1],
                               scale=ga[:, 0:1]).then_inc(act_ready, 1)

            def step(n, p):
                gated(n, p)
                need(eng, ss_ready, n)
                for half in (0, 1):
                    need(eng, k_filled, 4 * n + 2 * half + 2)
                    eng.activation(sq[:, 2 * GROUPS * half:2 * GROUPS * (half + 1), :],
                                   psK[2 * p + half][:, :, :].rearrange("p s (g e) -> p (s g) e", e=HD),
                                   ACT.Square).then_inc(sq_ready, 1)
                need(eng, ss_ready, n + 1)
                need(eng, kvn_ready, 2 * n)
                eng.activation(sd[:, :, :], ss[:, :, :], ACT.Sqrt, scale=1.0 / (HD - 1)).then_inc(sd_ready, 1)

            run(eng, step)

        @block.vector
        def _(eng):
            eng.wait_ge(w_loaded, 32)
            eng.wait_ge(consts, 2)
            eng.tensor_copy(moments[:, 0:1], st[:, 0:1]).then_inc(norm_step, 1)
            eng.scalar_tensor_tensor(moments[:, 1:2], st[:, 0:1], st[:, 0:1], st[:, 1:2],
                                     ALU.mult, ALU.add).then_inc(norm_step, 1)
            eng.wait_ge(g_filled, 1)
            eng.tensor_copy(gm[:, :], psG[:, 0:2]).then_inc(norm_step, 1)
            eng.wait_ge(norm_step, 3)
            eng.tensor_scalar(gb[:, :], gm[:, 0:1], -1.0, None, ALU.mult).then_inc(affine_ready, 1)
            eng.wait_ge(affine_ready, 1)
            eng.scalar_tensor_tensor(gvar[:, :], gm[:, 0:1], gb[:, 0:1], gm[:, 1:2],
                                     ALU.mult, ALU.add).then_inc(norm_step, 1)
            eng.wait_ge(sd_step, 1)
            eng.reciprocal(gsd[:, :], gsd[:, :]).then_inc(norm_step, 1)
            eng.wait_ge(norm_step, 5)
            eng.tensor_tensor(ga[:, :], gsd[:, :], W["gamma"], ALU.mult).then_inc(affine_ready, 1)
            eng.wait_ge(affine_ready, 2)
            eng.scalar_tensor_tensor(gb[:, :], gb[:, :], ga[:, 0:1], W["beta"],
                                     ALU.mult, ALU.add).then_inc(affine_ready, 1)
            wkv = W["wkv"].rearrange("c (g e) -> c g e", e=HD)
            eng.tensor_reduce(wmean[:, :, :], wkv, AX_X, ALU.add).then_inc(wcen_ready, 1)
            eng.wait_ge(wcen_ready, 1)
            eng.tensor_scalar(wmean[:, :, :], wmean[:, :, :], 1.0 / HD, None, ALU.mult).then_inc(wcen_ready, 1)
            eng.wait_ge(wcen_ready, 2)
            eng.tensor_tensor(wcen[:, :, :], wkv, wmean[:, :, :].broadcast_to([C, GROUPS, HD]),
                              ALU.subtract).then_inc(wcen_ready, 1)

            def step(n, p):
                need(eng, sq_ready, 2 * n + 2)
                need(eng, sd_ready, n)
                eng.tensor_reduce(ss[:, :, :], sq[:, :, :], AX_X, ALU.add).then_inc(ss_ready, 1)
                need(eng, sd_ready, n + 1)
                eng.tensor_scalar(sd[:, :, :], sd[:, :, :], EPS, None, ALU.add).then_inc(sde_ready, 1)
                need(eng, sde_ready, n + 1)
                eng.reciprocal(sd[:, :, :], sd[:, :, :]).then_inc(rsd_ready, 1)
                need(eng, rsd_ready, n + 1)
                need(eng, kvw_ready, n)
                for half in (0, 1):
                    eng.tensor_tensor(
                        kvn[:, 2 * half:2 * half + 2, :].rearrange("p s (g e) -> p (s g) e", e=HD),
                        sd[:, 2 * GROUPS * half:2 * GROUPS * (half + 1), :].broadcast_to([C, 2 * GROUPS, HD]),
                        psK[2 * p + half][:, :, :].rearrange("p s (g e) -> p (s g) e", e=HD),
                        ALU.mult).then_inc(kvn_ready, 1)
                need(eng, kvn_ready, 2 * n + 2)
                need(eng, kvf_ready, SUB * n)
                eng.tensor_tensor(kvw[:, :, :], kvn[:, :, :],
                                  W["ln_w"].unsqueeze(1).broadcast_to([C, SUB, GROUPS * HD]),
                                  ALU.mult).then_inc(kvw_ready, 1)

            run(eng, step)
            eng.wait_ge(kv_summed, CHUNKS)
            eng.tensor_tensor(kvb[:, :], W["headmask"], psA[:, :], ALU.mult).then_inc(tail, 1)
            eng.wait_ge(tail, 1)
            eng.tensor_scalar(kvb[:, :], kvb[:, :], 1.0 / TOKENS, None, ALU.mult).then_inc(tail, 1)
            eng.wait_ge(tail_mm, 1)
            eng.tensor_tensor(gmat[:, :], ident[:, :], psG[:, :], ALU.add).then_inc(tail, 1)
            eng.wait_ge(tail_mm, 2)
            eng.wait_ge(tail, 3)
            eng.tensor_copy(ut[:, :], psU[:, :]).then_inc(tail, 2)

        @block.tensor
        def _(eng):
            eng.wait_ge(w_loaded, 32)
            eng.wait_ge(norm_step, 2)
            eng.matmul(psG[:, 0:2], W["groups"], moments[:, :], start=True, stop=True).then_inc(g_filled, 1)
            eng.wait_ge(wcen_ready, 3)

            def keys_values(n, p):
                need(eng, x2_ready, n + 1)
                need(eng, kvn_ready, 2 * (n - 1))
                need(eng, sq_ready, 2 * (n - 1))
                for s in range(SUB):
                    eng.matmul(psK[2 * p + s // 2][:, s % 2, :], x2[p][:, 128 * s:128 * s + 128],
                               wcen[:, :, :].rearrange("c g e -> c (g e)"), start=True,
                               stop=True).then_inc(k_filled, 1)

            def accumulate(n, p, first, last):
                for s in range(SUB):
                    need(eng, kvf_ready, SUB * n + s + 1)
                    mm = eng.matmul(psA[:, :], kvf[p][:, s, 0:128], kvf[p][:, s, 128:256],
                                    start=(first and s == 0), stop=(last and s == SUB - 1))
                mm.then_inc(kv_summed, 1)

            keys_values(0, 0)
            keys_values(1, 1)
            accumulate(0, 0, True, False)
            keys_values(2, 0)
            accumulate(1, 1, False, False)
            with eng.Fori(1, CHUNKS // 2 - 1) as i:
                keys_values(2 * i + 1, 1)
                accumulate(2 * i, 0, False, False)
                keys_values(2 * i + 2, 0)
                accumulate(2 * i + 1, 1, False, False)
            keys_values(CHUNKS - 1, 1)
            accumulate(CHUNKS - 2, 0, False, False)
            accumulate(CHUNKS - 1, 1, False, True)
            eng.wait_ge(tail, 2)
            eng.matmul(psG[:, :], kvb[:, :], W["wq"], start=True, stop=True).then_inc(tail_mm, 1)
            eng.wait_ge(tail, 3)
            eng.matmul(psU[:, :], gmat[:, :], W["o1t"], start=True, stop=True).then_inc(tail_mm, 1)


def mlp_phase(nc, x2_dram, ut_dram, w_dram, out_dram):
    at, width = offsets(GLOBAL_COLS)
    lo, hi = at["o2t"]

    with ExitStack() as ctx:
        def sb(name, shape):
            return ctx.enter_context(nc.sbuf_tensor(f"ml_{name}", shape, F32))

        sems = []

        def sem(name):
            sems.append(ctx.enter_context(nc.semaphore(f"ml_{name}")))
            return sems[-1]

        ut = sb("ut", [C, 128])
        o2t = sb("o2t", [C, 128])
        xin = [sb(f"xin{p}", [C, T]) for p in (0, 1)]
        u = [sb(f"u{p}", [C, T]) for p in (0, 1)]
        t = [sb(f"t{p}", [C, T]) for p in (0, 1)]
        xo = [sb(f"xo{p}", [C, T]) for p in (0, 1)]
        psU = [ctx.enter_context(nc.psum_tensor(f"ml_psU{b}", [C, T], F32)) for b in (0, 1)]
        psO = [ctx.enter_context(nc.psum_tensor(f"ml_psO{b}", [C, T], F32)) for b in (0, 1)]
        w_loaded = sem("w_loaded")
        loaded = [sem(f"loaded{p}") for p in (0, 1)]
        stored = [sem(f"stored{p}") for p in (0, 1)]
        u_filled = sem("u_filled")
        u_ready = sem("u_ready")
        o_filled = sem("o_filled")
        t_ready = sem("t_ready")
        out_ready = sem("out_ready")

        def run(eng, step):
            step(0, 0)
            step(1, 1)
            with eng.Fori(1, CHUNKS // 2) as i:
                step(2 * i, 0)
                step(2 * i + 1, 1)

        ctx.callback(clear_semaphores, nc, sems)
        block = ctx.enter_context(nc.Block())

        @block.sync
        def _(eng):
            eng.dma_start(ut[:, :], ut_dram).then_inc(w_loaded, 16)
            eng.dma_start(o2t[:, :], w_dram[:, lo:hi]).then_inc(w_loaded, 16)

            def load(n, p):
                need(eng, u_filled, n - 1)
                need(eng, t_ready, n - 1)
                eng.dma_start(xin[p][:, :], x2_dram[:, bass.ds(T * n, T)]).then_inc(loaded[p], 16)

            def store(n, p):
                need(eng, out_ready, n + 1)
                eng.dma_start(out_dram[:, bass.ds(T * n, T)], xo[p][:, :]).then_inc(stored[p], 16)

            load(0, 0)
            load(1, 1)
            with eng.Fori(0, CHUNKS // 2 - 1) as i:
                load(2 * i + 2, 0)
                store(2 * i, 0)
                load(2 * i + 3, 1)
                store(2 * i + 1, 1)
            store(CHUNKS - 2, 0)
            store(CHUNKS - 1, 1)
            for p in (0, 1):
                eng.wait_ge(stored[p], 8 * CHUNKS)

        @block.scalar
        def _(eng):
            def inner(n, p):
                need(eng, u_filled, n + 1)
                need(eng, o_filled, n - 1)
                eng.activation(u[p][:, :], psU[p][:, :], ACT.Gelu).then_inc(u_ready, 1)

            def outer(n, p):
                need(eng, t_ready, n + 1)
                need(eng, stored[p], 8 * (n - p))
                eng.activation(xo[p][:, :], t[p][:, :], ACT.Gelu).then_inc(out_ready, 1)

            inner(0, 0)
            inner(1, 1)
            outer(0, 0)
            with eng.Fori(1, CHUNKS // 2) as i:
                inner(2 * i, 0)
                outer(2 * i - 1, 1)
                inner(2 * i + 1, 1)
                outer(2 * i, 0)
            outer(CHUNKS - 1, 1)

        @block.vector
        def _(eng):
            def step(n, p):
                need(eng, o_filled, n + 1)
                need(eng, loaded[p], 8 * (n - p) + 16)
                need(eng, out_ready, n - 1)
                eng.tensor_tensor(t[p][:, :], xin[p][:, :], psO[p][:, :], ALU.add).then_inc(t_ready, 1)

            run(eng, step)

        @block.tensor
        def _(eng):
            eng.wait_ge(w_loaded, 32)

            def inner(n, p):
                need(eng, loaded[p], 8 * (n - p) + 16)
                need(eng, u_ready, n - 1)
                eng.matmul(psU[p][:, :], ut[:, :], xin[p][:, :], start=True, stop=True).then_inc(u_filled, 1)

            def outer(n, p):
                need(eng, u_ready, n + 1)
                need(eng, t_ready, n - 1)
                eng.matmul(psO[p][:, :], o2t[:, :], u[p][:, :], start=True, stop=True).then_inc(o_filled, 1)

            inner(0, 0)
            inner(1, 1)
            outer(0, 0)
            with eng.Fori(1, CHUNKS // 2) as i:
                inner(2 * i, 0)
                outer(2 * i - 1, 1)
                inner(2 * i + 1, 1)
                outer(2 * i, 0)
            outer(CHUNKS - 1, 1)


def network_kernel(nc, x, w_row, w_col, w_lepe, w_fwd, w_bwd, w_global, w_chunked, out):
    def scratch(name, shape):
        return nc.dram_tensor(name, shape, F32).ap()

    h = scratch("h_att", (C, SIDE + 2, SIDE))
    v = scratch("v_att", (C, SIDE + 2, SIDE))
    x1 = scratch("x1", (C, TOKENS + 2))
    y_fwd = scratch("y_fwd", (C, TOKENS))
    y_sum = scratch("y_sum", (C, TOKENS))
    stats = scratch("stats", (C, 2))
    x2 = scratch("x2", (C, TOKENS))
    ut = scratch("ut", (C, C))
    x3 = scratch("x3", (C, TOKENS))

    attention_phase(nc, False, x, w_row, h)
    attention_phase(nc, True, x, w_col, v)
    lepe_phase(nc, h, v, w_lepe, x1)
    mamba_phase(nc, "forward", x1, w_fwd, y_fwd)
    mamba_phase(nc, "backward", x1, w_bwd, y_sum, y_fwd, stats)
    kv_phase(nc, y_sum, stats, x1, w_global, x2, ut)
    mlp_phase(nc, x2, ut, w_global, x3)
    mamba_phase(nc, "chunked", x3, w_chunked, out)





def _pack(cols, parts):
    at, width = offsets(cols)
    out = np.zeros((C, width), np.float32)
    for name, a in parts.items():
        lo, hi = at[name]
        a = a.reshape(a.shape[0], -1)
        assert a.shape[1] == hi - lo, (name, a.shape)
        out[:a.shape[0], lo:hi] = a
    return out


def _lay_mamba1(W_in, conv_w, conv_b, W_x, W_dt, b_dt, A_log, D, W_out):
    blocks = lambda a: a.reshape(2, 128, -1).transpose(1, 0, 2)
    units = lambda a: a.reshape(2, 128, STATE).transpose(1, 2, 0)
    x_rows = blocks(W_x)
    dtr = np.zeros((128, 2, 32), np.float32)
    dtr[:, :, 0:8] = x_rows[:, :, 0:8]
    return _pack(MAMBA1_COLS, {
        "win": W_in[:, 0:256], "wz": W_in[:, 256:512],
        "tapw": np.broadcast_to(conv_w.T.reshape(1, 2 * 256), (128, 512)),
        "wbc": np.tile(x_rows[:, :, 8:40], (1, 1, 3)), "wdtr": dtr, "wdt": W_dt,
        "bdt": blocks(b_dt), "convb": blocks(conv_b), "dskip": blocks(D), "alog": units(A_log),
        "wout": blocks(W_out)})


def _lay_mamba3(ln_g, ln_b, in_proj_w, conv_w, conv_b, x_proj_w, dt_proj_w, dt_proj_b, A_log, D, out_proj_w):
    win, wz = np.zeros((2, 128, 2, 128), np.float32)
    wb, wc = np.zeros((2, 128, 32), np.float32)
    dtr = np.zeros((128, 2, 32), np.float32)
    wdt = np.zeros((32, 2, 128), np.float32)
    wout = np.zeros((128, 2, 128), np.float32)
    for half in range(2):
        rows = slice(64 * half, 64 * half + 64)
        wb[rows, 16 * half:16 * half + 16] = x_proj_w[2:18].T
        wc[rows, 16 * half:16 * half + 16] = x_proj_w[18:34].T
        for b in range(2):
            q = 2 * b + half
            ch = slice(32 * q, 32 * q + 32)
            win[ch, b, rows] = in_proj_w[0:64].T
            wz[ch, b, rows] = in_proj_w[64:128].T
            dtr[rows, b, 2 * q:2 * q + 2] = x_proj_w[0:2].T
            wdt[2 * q:2 * q + 2, b, rows] = dt_proj_w.T
            wout[rows, b, ch] = out_proj_w.T
    both = lambda v: np.repeat(np.tile(v.reshape(64), 2).reshape(128, 1), 2, axis=1)
    return _pack(MAMBA3_COLS, {
        "win": win, "wz": wz, "wb": np.tile(wb, (1, 3)), "wc": np.tile(wc, (1, 3)), "wdtr": dtr,
        "tapw": np.broadcast_to(np.tile(conv_w.T.reshape(4, 64), (1, 4)).reshape(1, 1024), (128, 1024)),
        "wdt": wdt, "bdt": both(dt_proj_b), "convb": both(conv_b), "dskip": both(D),
        "alog": np.repeat(np.tile(A_log, (2, 1)), 2, axis=1), "wout": wout,
        "ln_g": ln_g.reshape(128, 1), "ln_b": ln_b.reshape(128, 1)})


def _lay_attention(qkv_w, qkv_b, table):
    onehot = np.zeros((C, SIDE), np.float32)
    kc = np.zeros((C, HEADS, SIDE), np.float32)
    mask = np.zeros((C, 3), np.float32)
    for part in range(3):
        for a in range(S7):
            row = 6 * HD + S7 * part + a
            onehot[row, a * SIDE // S7:(a + 1) * SIDE // S7] = 1.0
            kc[row] = np.repeat(table[a], SIDE // S7, axis=0).T
            mask[row, part] = 1.0
    return _pack(ATTN_COLS, {
        "wq": qkv_w[0:C].T, "wk": qkv_w[C:2 * C].T, "wv": qkv_w[2 * C:].T,
        "bq": qkv_b[0:C].reshape(C, 1), "bk": qkv_b[C:2 * C].reshape(C, 1), "bv": qkv_b[2 * C:].reshape(C, 1),
        "mask": mask, "onehot": onehot, "selm": np.tile(np.eye(HEADS), (3, 1)), "kc": kc})


def _lay_lepe(h_w, h_b, v_w, v_b, proj_w, proj_b):
    col = lambda a: a.reshape(C, -1)
    return _pack(LEPE_COLS, {"tap_h": col(h_w), "tap_v": col(v_w), "b_h": col(h_b), "b_v": col(v_b),
                             "proj_b": col(proj_b), "proj": proj_w.T})


def _lay_global(gamma, beta, qkv_w, o1_w, o2_w, kln_w, kln_b, vln_w, vln_b):
    qkv = qkv_w.reshape(HEADS, 3, HD, C)
    part = lambda i: qkv[:, i].reshape(C, C)
    row = lambda k, v: np.broadcast_to(np.concatenate([k.reshape(1, C), v.reshape(1, C)], axis=1), (C, 2 * C))
    return _pack(GLOBAL_COLS, {
        "gamma": gamma.reshape(C, 1), "beta": beta.reshape(C, 1),
        "wkv": np.concatenate([part(1).T, part(2).T], axis=1), "wq": part(0),
        "o1t": o1_w.T, "o2t": o2_w.T, "ln_w": row(kln_w, vln_w), "ln_b": row(kln_b, vln_b),
        "groups": np.kron(np.eye(4), np.full((32, 32), 1.0 / 32)),
        "headmask": np.kron(np.eye(HEADS), np.ones((HD, HD)))})


def kernel(**inputs):
    import concourse.bacc as _bacc
    from concourse.bass_utils import run_bass_kernel_spmd as _run

    part = lambda layer, names: [np.asarray(inputs[f"{layer}_conv_{n}"]) for n in names.split()]
    table_h, table_v = part("L0", "table_h table_v")
    tiles = np.arange(S7)
    rel = tiles[:, None] - tiles[None, :] + S7 - 1
    mamba1 = "W_in conv_w conv_b W_x W_dt b_dt A_log D W_out".split()
    arrays = {
        "x": np.asarray(inputs["x"]).reshape(C, SIDE, SIDE),
        "w_row": _lay_attention(*part("L0", "qkv_h_w qkv_h_b"), table_h[S7 - 1, rel]),
        "w_col": _lay_attention(*part("L0", "qkv_v_w qkv_v_b"), table_v[rel, S7 - 1]),
        "w_lepe": _lay_lepe(*part("L0", "lepe_h_w lepe_h_b lepe_v_w lepe_v_b proj_w proj_b")),
        "w_fwd": _lay_mamba1(*part("L1", " ".join(n + "_f" for n in mamba1))),
        "w_bwd": _lay_mamba1(*part("L1", " ".join(n + "_b" for n in mamba1))),
        "w_global": _lay_global(*part("L1", "gn_gamma gn_beta"),
                                *part("L2", "qkv_w o1_w o2_w kln_w kln_b vln_w vln_b")),
        "w_chunked": _lay_mamba3(*part("L3", "ln_g ln_b in_proj_w conv_w conv_b x_proj_w dt_proj_w "
                                             "dt_proj_b A_log D out_proj_w")),
    }
    nc = _bacc.Bacc("TRN2", target_bir_lowering=False, num_devices=1)
    args = [nc.dram_tensor(f"in_{n}_dram", a.shape, F32, kind="ExternalInput").ap() for n, a in arrays.items()]
    args.append(nc.dram_tensor("out_0_dram", (C, TOKENS), F32, kind="ExternalOutput").ap())
    network_kernel(nc, *args)
    r = _run(nc, [{f"in_{n}_dram": np.ascontiguousarray(a) for n, a in arrays.items()}], core_ids=[0])
    return r.results[0]["out_0_dram"].reshape(1, C, SIDE, SIDE)
```

```python
from contextlib import ExitStack

import numpy as np

import concourse.bass as bass
from concourse import mybir
from concourse.alu_op_type import AluOpType as ALU

ACT = mybir.ActivationFunctionType
F32 = mybir.dt.float32
BF16 = mybir.dt.bfloat16
AX_X = mybir.AxisListType.X

C = 128
SIDE = 224
TOKENS = SIDE * SIDE
T = 512
CHUNKS = TOKENS // T
EPS = 1e-5

S7 = 7
HEADS = 8
HD = C // HEADS
LINES = SIDE
BLOCK = 28
HALF = SIDE // 2

STATE = 16
UNITS = 2 * STATE
RING = 4
SUMS = 8

SCHEDULES = {
    "forward": dict(
        merges=(8, 11, 15, 18), decays=8, lag=8, cast=2, copy=6, skip=5, gate=7, out=21, result=26,
        conv=(7, 8), gates=(20, 21), bc=(21,), dts=(25, 25),
        silus=22, hi=(24,), mid=(27,), log=28,
        rest=(21,), lo=(25,), relu=26, lost=26, add_log=27, add_relu=28, scale=29),
    "backward": dict(
        merges=(14, 17), decays=8, lag=8, cast=2, copy=6, skip=5, gate=7, out=21, result=22,
        conv=(7, 9), gates=(19, 20), bc=(21,), dts=(23, 23),
        silus=21, hi=(22,), mid=(25,), log=26,
        rest=(21,), lo=(22,), relu=23, lost=24, add_log=25, add_relu=26, scale=27),
    "chunked": dict(
        merges=(10, 11, 25), decays=8, skip0=25, lag=4, cast=0, copy=0, skip=2, gate=4, out=6, result=6,
        mean=0, var=4, conv=(12, 12), gates=(13, 13), bc=(14, 14, 20, 20), dts=(25, 27),
        square=4, rstd=4, pair=8, silus=12, hi=(14, 18, 20, 22), mid=(18, 19, 22, 23), log=28,
        center=1, normalize=6, rest=(18, 19, 22, 23), lo=(19, 20, 23, 25), relu=28, lost=28, add_log=29, add_relu=30, scale=31),
}

ATTN_COLS = {"wq": 128, "wk": 128, "wv": 128, "bq": 1, "bk": 1, "bv": 1, "mask": 3, "onehot": SIDE,
             "selm": HEADS, "kc": HEADS * SIDE}
LEPE_COLS = {"tap_h": 9, "tap_v": 9, "b_h": 1, "b_v": 1, "proj_b": 1, "proj": 128}
MAMBA1_COLS = {"win": 256, "tapw": 2 * 256, "wz": 256, "wbc": 2 * 96, "wdtr": 256, "wdt": 256,
               "bdt": 2, "convb": 2, "dskip": 2, "alog": UNITS, "wout": 256}
MAMBA3_COLS = {"win": 256, "tapw": 4 * 256, "wz": 256, "wb": 96, "wc": 96, "wdtr": 256, "wdt": 256,
               "bdt": 2, "convb": 2, "dskip": 2, "alog": UNITS, "wout": 256, "ln_g": 1, "ln_b": 1}
GLOBAL_COLS = {"gamma": 1, "beta": 1, "wkv": 256, "wq": 128, "o1t": 128, "o2t": 128,
               "ln_w": 256, "ln_b": 256, "groups": 128, "headmask": 128}


def offsets(cols):
    at, out = 0, {}
    for name, n in cols.items():
        out[name] = (at, at + n)
        at += n
    return out, at


def need(eng, sem, count):
    if not isinstance(count, int) or count > 0:
        eng.wait_ge(sem, count)


def clear_semaphores(nc, sems):
    with nc.Block() as block:
        @block.sync
        def _(eng):
            for sem in sems:
                eng.sem_clear(sem)


def make_identity(pool, tile, n, zeroed, made):
    pool.memset(tile[:, :], 0.0).then_inc(zeroed, 1)
    pool.wait_ge(zeroed, 1)
    pool.affine_select(out=tile[:, :], in_=tile[:, :], compare_op=ALU.not_equal, fill=1.0, base=0,
                       pattern=[[-1, n]], channel_multiplier=1).then_inc(made, 1)



def mamba_phase(nc, kind, x_dram, w_dram, out_dram, addend_dram=None, stats_dram=None):
    layer3 = kind == "chunked"
    rev = kind == "backward"
    cols = MAMBA3_COLS if layer3 else MAMBA1_COLS
    at, width = offsets(cols)
    TAPS = 4 if layer3 else 2
    NBC = 4 if layer3 else 1
    PER = 1 if layer3 else 2
    KB = UNITS // PER
    HALO = TAPS - 1
    CONVS = 2
    plan = SCHEDULES[kind]
    DECAYS, LAG, CAST_LAG, COPY_LAG = plan["decays"], plan["lag"], plan["cast"], plan["copy"]
    def block_of(u):
        return u // STATE if layer3 else u % 2

    def state_of(u):
        return u % STATE if layer3 else u // 2

    MERGES = plan["merges"]

    def merges_before(c, u):
        return len(MERGES) * c + sum(1 for v in MERGES if v < u)

    def sums_before(c, u):
        return (UNITS - len(MERGES)) * c + u - sum(1 for v in MERGES if v - 2 < u)

    STATES = 16 if layer3 else UNITS
    SAVE = 8
    OUT_RANK = 1 if layer3 else 2

    if layer3:
        order = [("mean", 0), ("var", 1), ("conv0", 0), ("conv1", 1), ("gate0", 0), ("gate1", 1),
                 ("bc0", 0), ("bc1", 1), ("bc2", 0), ("bc3", 1), ("dt0", 0), ("dt1", 1)]
    else:
        order = [("conv0", 0), ("conv1", 1), ("gate0", 0), ("gate1", 1),
                 ("bc0", 0), ("dt0", 0), ("dt1", 1)]
    bank_of = dict(order)
    rank = {name: sum(1 for n, b in order[:i] if b == bank) for i, (name, bank) in enumerate(order)}
    fills = [sum(1 for _, b in order if b == bank) for bank in (0, 1)]

    def index(name, m):
        if name == "out":
            before = (m + 2) * fills[1] + OUT_RANK
            return (min(before, CHUNKS * fills[1]) if isinstance(m, int) else before) + m
        before = m * fills[bank_of[name]] + rank[name]
        if bank_of[name] == 1:
            outs = m - 2 if rank[name] < OUT_RANK else m - 1
            before = before + (max(outs, 0) if isinstance(m, int) else outs)
        return before

    with ExitStack() as ctx:
        def sb(name, shape, dt=F32):
            return ctx.enter_context(nc.sbuf_tensor(f"{kind}_{name}", shape, dt))

        def pb(name, shape):
            return ctx.enter_context(nc.psum_tensor(f"{kind}_{name}", shape, F32))

        sems = []

        def sem(name):
            sems.append(ctx.enter_context(nc.semaphore(f"{kind}_{name}")))
            return sems[-1]

        w = sb("w", [C, width])
        W = {n: w[:, a:b] for n, (a, b) in at.items()}
        wconv = sb("wconv", [C, CONVS, 2, 128])
        decay = sb("decay", [C, UNITS])
        epst = sb("epst", [C, 1])
        ident = sb("ident", [C, 128])
        ones = sb("ones", [C, 128])
        select = sb("select", [96, 32, 128], BF16)
        xin = [sb(f"xin{p}", [C, T + 2]) for p in (0, 1)]
        xn = [sb(f"xn{p}", [C, HALO + T]) for p in (0, 1)] if layer3 else None
        xpair = [sb(f"xpair{b}", [C, HALO + T]) for b in (0, 1)] if layer3 else None
        cen = sb("cen", [C, T]) if layer3 else None
        sq = sb("sq", [C, T]) if layer3 else None
        xc = [sb(f"xc{p}", [C, 2, T]) for p in (0, 1)]
        zs = [sb(f"zs{p}", [C, 2, T]) for p in (0, 1)]
        bcs = [sb(f"bcs{p}", [96, NBC, T], BF16) for p in (0, 1)]
        rest = sb("rest", [64, T])
        wdt = sb("wdt", [C, 2 if layer3 else 4, 128])
        sp = sb("sp", [C, 2, T])
        sp1 = sb("sp1", [C, 2, T])
        spl = sb("spl", [C, 2, T])
        dt = [sb(f"dt{p}", [C, 2, T]) for p in (0, 1)]
        dtx = [sb(f"dtx{p}", [C, 2, T]) for p in (0, 1)]
        da = sb("da", [C, DECAYS, T])
        dbx = sb("dbx", [C, RING, T])
        hs = sb("hs", [C, STATES, T])
        carry = sb("carry", [C, UNITS])
        cb = sb("cb", [C, RING, T])
        hc = sb("hc", [C, SUMS, T])
        yv = sb("yv", [C, 2, T])
        yout = [sb(f"yout{p}", [C, T]) for p in (0, 1)]
        yadd = [sb(f"yadd{p}", [C, T]) for p in (0, 1)] if rev else None
        stats = sb("stats", [C, CHUNKS, 6]) if rev else None
        aggr = sb("aggr", [C, 2]) if rev else None

        prep = [pb(f"prep{b}", [C, T]) for b in (0, 1)]
        psB = [pb(f"psB{b}", [C, T]) for b in (0, 1)]
        psC = [pb(f"psC{b}", [C, T]) for b in (0, 1)]
        psY = [pb(f"psY{b}", [C, T]) for b in (0, 1)]

        w_loaded = sem("w_loaded")
        zeroed = sem("zeroed")
        consts = sem("consts")
        wconv_ready = sem("wconv_ready")
        wdt_filled = sem("wdt_filled")
        wdt_ready = sem("wdt_ready")
        alog_min = sem("alog_min")
        alog_exp = sem("alog_exp")
        x_loaded = [sem(f"x_loaded{p}") for p in (0, 1)]
        add_loaded = [sem(f"add_loaded{p}") for p in (0, 1)]
        filled = [sem(f"filled{b}") for b in (0, 1)]
        drained = [sem(f"drained{b}") for b in (0, 1)]
        sq_ready = sem("sq_ready")
        lnvar_ready = sem("lnvar_ready")
        rstd_ready = sem("rstd_ready")
        xhat_ready = sem("xhat_ready")
        halo_ready = sem("halo_ready")
        paired = sem("paired")
        xn_ready = sem("xn_ready")
        hi_ready = sem("hi_ready")
        mid_ready = sem("mid_ready")
        lo_ready = sem("lo_ready")
        abs_ready = sem("abs_ready")
        expneg_ready = sem("expneg_ready")
        plus1_ready = sem("plus1_ready")
        log_ready = sem("log_ready")
        lost_ready = sem("lost_ready")
        log_added = sem("log_added")
        relu_ready = sem("relu_ready")
        dt_ready = sem("dt_ready")
        dtx_ready = sem("dtx_ready")
        b_filled = sem("b_filled")
        c_filled = sem("c_filled")
        c_copied = sem("c_copied")
        exp_done = sem("exp_done")
        dbx_done = sem("dbx_done")
        scan_done = sem("scan_done")
        saved = sem("saved")
        prod_done = sem("prod_done")
        merge_done = sem("merge_done")
        sum_done = sem("sum_done")
        skip_added = sem("skip_added")
        y_ready = sem("y_ready")
        stats_done = sem("stats_done")
        stored = [sem(f"stored{p}") for p in (0, 1)]

        def wait_filled(eng, name, m):
            b = 1 if name == "out" else bank_of[name]
            need(eng, filled[b], index(name, m) + 1)

        def wait_drained(eng, name, m):
            b = 1 if name == "out" else bank_of[name]
            need(eng, drained[b], index(name, m) + 1)

        def wait_bank(eng, name, m):
            b = 1 if name == "out" else bank_of[name]
            need(eng, drained[b], index(name, m))

        def token0(m):
            return m * -T + (CHUNKS - 1) * T if rev else m * T

        def due(steps, u):
            return [step for at_unit, step in steps if at_unit == u]

        def each(name, step):
            return [(at_unit, lambda m, p, q=q: step(m, p, q)) for q, at_unit in enumerate(plan[name])]

        def run(eng, steps, chunk, post):
            for u in range(UNITS):
                for step in due(steps, u):
                    step(0, 0)
            chunk(0, 0, False)
            chunk(1, 1, False)
            with eng.Fori(1, CHUNKS // 2 - 1) as i:
                chunk(2 * i, 0, False)
                chunk(2 * i + 1, 1, False)
            chunk(CHUNKS - 2, 0, False)
            chunk(CHUNKS - 1, 1, True)
            post(CHUNKS - 1, 1)

        ctx.callback(clear_semaphores, nc, sems)
        block = ctx.enter_context(nc.Block())

        @block.sync
        def _(eng):
            eng.dma_start(w[:, :], w_dram).then_inc(w_loaded, 16)

            def load(m, p):
                start = token0(m)
                if layer3:
                    if not isinstance(m, int) or m >= 2:
                        wait_drained(eng, "mean", m - 2)
                    eng.dma_start(xin[p][:, 0:T], x_dram[:, bass.ds(start, T)]).then_inc(x_loaded[p], 16)
                else:
                    if not isinstance(m, int) or m >= 2:
                            wait_filled(eng, "gate1", m - 2)
                    eng.dma_start(xin[p][:, :], x_dram[:, bass.ds(start, T + 2)]).then_inc(x_loaded[p], 16)
                if rev:
                    if not isinstance(m, int) or m >= 2:
                            wait_drained(eng, "out", m - 2)
                    eng.dma_start(yadd[p][:, :], addend_dram[:, bass.ds(start, T)]).then_inc(add_loaded[p], 16)

            def store(m, p):
                start = token0(m)
                wait_drained(eng, "out", m)
                eng.dma_start(out_dram[:, bass.ds(start, T)], yout[p][:, :]).then_inc(stored[p], 16)

            load(0, 0)
            load(1, 1)
            load(2, 0)
            store(0, 0)
            with eng.Fori(1, CHUNKS // 2 - 1) as i:
                load(2 * i + 1, 1)
                store(2 * i - 1, 1)
                load(2 * i + 2, 0)
                store(2 * i, 0)
            load(CHUNKS - 1, 1)
            store(CHUNKS - 3, 1)
            store(CHUNKS - 2, 0)
            store(CHUNKS - 1, 1)
            if rev:
                eng.wait_ge(stats_done, CHUNKS + 1)
                eng.dma_start(stats_dram, aggr[:, :]).then_inc(stored[0], 16)
            eng.wait_ge(stored[0], 8 * CHUNKS + (16 if rev else 0))
            eng.wait_ge(stored[1], 8 * CHUNKS)

        @block.gpsimd
        def _(eng):
            make_identity(eng, ident, 128, zeroed, consts)
            eng.memset(ones[:, :], 1.0 / C).then_inc(consts, 1)
            eng.memset(select[:, :, :], 0.0).then_inc(zeroed, 1)
            if layer3:
                for tile in (*xn, *xpair):
                    eng.memset(tile[:, 0:HALO], 0.0).then_inc(consts, 1)
            if STATES < UNITS:
                eng.memset(carry[:, :], 0.0).then_inc(consts, 1)
            else:
                eng.memset(hs[:, :, 0:1] if rev else hs[:, :, T - 1:T], 0.0).then_inc(consts, 1)
            eng.wait_ge(zeroed, 2)
            turn = 2
            for part in range(3):
                if layer3:
                    for half in range(2):
                        view = select[:, 0:STATE, 64 * half:64 * half + 64]
                        eng.affine_select(out=view, in_=view, compare_op=ALU.not_equal, fill=1.0,
                                          base=-32 * part - 16 * half, pattern=[[-1, STATE], [0, 64]],
                                          channel_multiplier=1).then_inc(zeroed, 1)
                        turn += 1
                        eng.wait_ge(zeroed, turn)
                else:
                    eng.affine_select(out=select[:, :, :], in_=select[:, :, :], compare_op=ALU.not_equal,
                                      fill=1.0, base=-32 * part, pattern=[[-1, 32], [0, 128]],
                                      channel_multiplier=1).then_inc(zeroed, 1)
                    turn += 1
                    eng.wait_ge(zeroed, turn)

            def chunk(c, p, last):
                for u in range(UNITS):
                    g = c * UNITS + u
                    k = c * KB + u // PER
                    need(eng, scan_done, g + 1)
                    need(eng, c_copied, k + 1)
                    cc, uu = (c, u - SUMS) if u >= SUMS else (c - 1, u - SUMS + UNITS)
                    need(eng, sum_done, sums_before(cc, uu + 1))
                    if uu + 2 in MERGES:
                        need(eng, merge_done, merges_before(cc, uu + 3))
                    eng.tensor_tensor(hc[:, u % SUMS, :], hs[:, u % STATES, :], cb[:, (u // PER) % RING, :],
                                      ALU.mult).then_inc(prod_done, 1)
                    if u in MERGES:
                        need(eng, prod_done, g + 1)
                        eng.tensor_tensor(hc[:, u % SUMS, :], hc[:, u % SUMS, :], hc[:, (u - 2) % SUMS, :],
                                          ALU.add).then_inc(merge_done, 1)

            run(eng, [], chunk, lambda m, p: None)

        ALL_CONSTS = 7 if layer3 else 3
        SELECT_MADE = 2 + (6 if layer3 else 3)

        @block.scalar
        def _(eng):
            eng.wait_ge(alog_min, 1)
            eng.activation(decay[:, :], decay[:, :], ACT.Exp).then_inc(alog_exp, 1)
            eng.wait_ge(wconv_ready, 2)

            eps_col = epst[:, 0:1]

            def silus(m, p):
                need(eng, y_ready, m - 1)
                for b in (0, 1):
                    wait_filled(eng, f"conv{b}", m)
                    eng.activation(xc[p][:, b, :], prep[b][:, :], ACT.Silu,
                                   bias=W["convb"][:, b:b + 1]).then_inc(drained[b], 1)
                for b in (0, 1):
                    wait_filled(eng, f"gate{b}", m)
                    eng.activation(zs[p][:, b, :], prep[b][:, :], ACT.Silu).then_inc(drained[b], 1)

            def split_hi(m, p, q):
                wait_filled(eng, f"bc{q}", m)
                need(eng, b_filled, KB * (m - 1))
                need(eng, c_filled, KB * (m - 1))
                eng.activation(bcs[p][:, q, :], prep[bank_of[f"bc{q}"]][0:96, :], ACT.Copy).then_inc(hi_ready, 1)

            def split_mid(m, p, q):
                wait_drained(eng, f"bc{q}", m)
                eng.activation(bcs[p][0:64, q, :], rest[0:64, :], ACT.Copy).then_inc(mid_ready, 1)

            def dt_abs(m, p):
                need(eng, dt_ready, m)
                for b in (0, 1):
                    wait_filled(eng, f"dt{b}", m)
                    eng.activation(sp[:, b, :], prep[b][:, :], ACT.Abs,
                                   bias=W["bdt"][:, b:b + 1]).then_inc(abs_ready, 1)

            def dt_log(m, p):
                need(eng, abs_ready, 2 * m + 2)
                eng.activation(sp[:, :, :], sp[:, :, :], ACT.Exp, scale=-1.0).then_inc(expneg_ready, 1)
                need(eng, expneg_ready, m + 1)
                eng.activation(sp1[:, :, :], sp[:, :, :], ACT.Identity, bias=1.0).then_inc(plus1_ready, 1)
                need(eng, plus1_ready, m + 1)
                eng.activation(spl[:, :, :], sp1[:, :, :], ACT.Ln).then_inc(log_ready, 1)

            def square(m, p):
                wait_drained(eng, "mean", m)
                if not isinstance(m, int) or m >= 1:
                    need(eng, xhat_ready, m)
                eng.activation(sq[:, :], cen[:, :], ACT.Square).then_inc(sq_ready, 1)

            def rstd(m, p):
                wait_filled(eng, "var", m)
                eng.activation(sq[:, :], prep[1][:, :], ACT.Ln, bias=eps_col).then_inc(lnvar_ready, 1)
                need(eng, lnvar_ready, m + 1)
                eng.activation(sq[:, :], sq[:, :], ACT.Exp, scale=-0.5).then_inc(drained[1], 1)

            def pair(m, p):
                need(eng, xhat_ready, m + 1)
                if not isinstance(m, int) or m >= 1:
                    wait_filled(eng, "conv0", m - 1)
                    wait_filled(eng, "conv1", m - 1)
                for b in (0, 1):
                    own, other = slice(64 * b, 64 * b + 64), slice(64 - 64 * b, 128 - 64 * b)
                    eng.dma_start(xpair[b][own, :], xn[p][own, :]).then_inc(paired, 16)
                    eng.dma_start(xpair[b][other, 1:HALO + T], xn[p][own, 0:HALO + T - 1]).then_inc(paired, 16)

            def evacuate(m, p):
                wait_filled(eng, "out", m)
                need(eng, stored[p], 8 * (m - p))
                eng.activation(yout[p][:, :], prep[1][:, :], ACT.Copy).then_inc(drained[1], 1)

            steps = [(plan["square"], square), (plan["rstd"], rstd), (plan["pair"], pair)] if layer3 else []
            steps += [(plan["silus"], silus)]
            for (at_mid, mid_step), (at_hi, hi_step) in zip(each("mid", split_mid), each("hi", split_hi)):
                steps += [(at_hi, hi_step), (at_mid, mid_step)]
            steps += [(plan["log"], dt_abs), (plan["log"], dt_log)]

            def copy_c(c, u):
                if u % PER == 0:
                    k = c * KB + u // PER
                    need(eng, c_filled, k + 1)
                    need(eng, prod_done, (k - RING + 1) * PER)
                    eng.activation(cb[:, (u // PER) % RING, :], psC[(u // PER) % 2][:, :],
                                   ACT.Copy).then_inc(c_copied, 1)

            def chunk(c, p, last):
                first = isinstance(c, int) and c == 0
                for u in range(UNITS):
                    g = c * UNITS + u
                    if u == 0:
                        need(eng, dt_ready, c + 1)
                    need(eng, scan_done, g - DECAYS + 1)
                    column = 2 * state_of(u) + block_of(u)
                    eng.activation(da[:, u % DECAYS, :], dt[p][:, block_of(u), :], ACT.Exp,
                                   scale=decay[:, column:column + 1]).then_inc(exp_done, 1)
                    if u >= COPY_LAG:
                        copy_c(c, u - COPY_LAG)
                    elif not first:
                        copy_c(c - 1, UNITS + u - COPY_LAG)
                    if u == plan["result"] and kind == "forward" and not first:
                        evacuate(c - 1, 1 - p)
                    if not last:
                        for step in due(steps, u):
                            step(c + 1, 1 - p)

            def post(m, p):
                for u in range(UNITS - COPY_LAG, UNITS):
                    copy_c(m, u)
                if kind == "forward":
                    evacuate(m, p)

            run(eng, steps, chunk, post)

        @block.vector
        def _(eng):
            eng.wait_ge(w_loaded, 16)
            eng.tensor_scalar(decay[:, :], W["alog"], 80.0, None, ALU.min).then_inc(alog_min, 1)
            eng.wait_ge(alog_exp, 1)
            eng.tensor_scalar(decay[:, :], decay[:, :], -1.0, None, ALU.mult).then_inc(wconv_ready, 1)
            eng.memset(epst[:, :], EPS).then_inc(wconv_ready, 1)
            win = W["win"].rearrange("p (b m) -> p b m", b=2)
            tap = lambda k: W["tapw"][:, 256 * k:256 * k + 256].rearrange("p (b m) -> p b m", b=2)
            for k in range(CONVS):
                for b in (0, 1):
                    if layer3:
                        own, other = slice(64 * b, 64 * b + 64), slice(64 - 64 * b, 128 - 64 * b)
                        for rows, t in ((own, 2 * k + 1), (other, 2 * k)):
                            eng.tensor_tensor(wconv[rows, k, b, :], win[rows, b, :], tap(t)[rows, b, :],
                                              ALU.mult).then_inc(wconv_ready, 1)
                    else:
                        eng.tensor_tensor(wconv[:, k, b, :], win[:, b, :], tap(k)[:, b, :],
                                          ALU.mult).then_inc(wconv_ready, 1)
            eng.wait_ge(consts, ALL_CONSTS)
            eng.wait_ge(wdt_filled, 1)
            eng.tensor_copy(wdt[:, :, :], prep[0][:, 0:256 if layer3 else 512]
                            .rearrange("p (k m) -> p k m", m=128)).then_inc(wdt_ready, 1)

            def center(m, p):
                wait_filled(eng, "mean", m)
                need(eng, x_loaded[p], 8 * (m - p) + 16)
                need(eng, xhat_ready, m)
                need(eng, sq_ready, m)
                eng.tensor_tensor(cen[:, :], xin[p][:, 0:T], prep[0][:, :], ALU.subtract).then_inc(drained[0], 1)

            def normalize(m, p):
                wait_drained(eng, "var", m)
                eng.tensor_tensor(cen[:, :], cen[:, :], sq[:, :], ALU.mult).then_inc(rstd_ready, 1)
                if not isinstance(m, int) or m >= 2:
                    wait_filled(eng, "gate1", m - 2)
                    wait_drained(eng, "out", m - 2)
                if not isinstance(m, int) or m >= 1:
                    eng.tensor_copy(xn[p][:, 0:HALO], xn[1 - p][:, T:T + HALO]).then_inc(halo_ready, 1)
                need(eng, rstd_ready, m + 1)
                eng.tensor_scalar(xn[p][:, HALO:HALO + T], cen[:, :], W["ln_g"], W["ln_b"],
                                  ALU.mult, ALU.add).then_inc(xhat_ready, 1)

            def split_rest(m, p, q):
                n = m * NBC + q
                need(eng, hi_ready, n + 1)
                need(eng, lo_ready, n)
                b = bank_of[f"bc{q}"]
                eng.tensor_tensor(rest[:, :], prep[b][0:64, :], bcs[p][0:64, q, :],
                                  ALU.subtract).then_inc(drained[b], 1)

            def split_lo(m, p, q):
                n = m * NBC + q
                need(eng, mid_ready, n + 1)
                eng.tensor_tensor(bcs[p][32:64, q, :], rest[32:64, :], bcs[p][32:64, q, :],
                                  ALU.subtract).then_inc(lo_ready, 1)

            def relu_dt(m, p):
                need(eng, exp_done, UNITS * (m - 1))
                for b in (0, 1):
                    need(eng, abs_ready, 2 * m + 1 + b)
                    eng.tensor_scalar(dt[p][:, b, :], prep[b][:, :], W["bdt"][:, b:b + 1], 0.0,
                                      ALU.add, ALU.max).then_inc(drained[b], 1)

            def lost_part(m, p):
                need(eng, plus1_ready, m + 1)
                eng.scalar_tensor_tensor(sp[:, :, :], sp1[:, :, :], -1.0, sp[:, :, :],
                                         ALU.add, ALU.subtract).then_inc(lost_ready, 1)

            def add_log(m, p):
                need(eng, log_ready, m + 1)
                need(eng, lost_ready, m + 1)
                eng.tensor_tensor(spl[:, :, :], spl[:, :, :], sp[:, :, :], ALU.subtract).then_inc(log_added, 1)

            def add_relu(m, p):
                need(eng, log_added, m + 1)
                for b in (0, 1):
                    wait_drained(eng, f"dt{b}", m)
                eng.tensor_tensor(dt[p][:, :, :], dt[p][:, :, :], spl[:, :, :], ALU.add).then_inc(dt_ready, 1)

            def scale_x(m, p):
                need(eng, dt_ready, m + 1)
                wait_drained(eng, "conv0", m)
                wait_drained(eng, "conv1", m)
                eng.tensor_tensor(dtx[p][:, :, :], dt[p][:, :, :], xc[p][:, :, :], ALU.mult).then_inc(dtx_ready, 1)

            def skip(m, p, b):
                last = max(u for u in range(UNITS) if block_of(u) == b)
                need(eng, sum_done, sums_before(m, last + 1))
                if not isinstance(m, int) or m >= 1:
                    wait_filled(eng, "out", m - 1)
                eng.scalar_tensor_tensor(yv[:, b, :], xc[p][:, b, :], W["dskip"][:, b:b + 1],
                                         psY[b][:, :], ALU.mult, ALU.add).then_inc(skip_added, 1)

            def gate(m, p):
                need(eng, skip_added, 2 * m + 2)
                wait_drained(eng, "gate0", m)
                wait_drained(eng, "gate1", m)
                eng.tensor_tensor(yv[:, :, :], yv[:, :, :], zs[p][:, :, :], ALU.mult).then_inc(y_ready, 1)

            def add_out(m, p):
                wait_filled(eng, "out", m)
                need(eng, stored[p], 8 * (m - p))
                if rev:
                    need(eng, add_loaded[p], 8 * (m - p) + 16)
                    other = yadd[p][:, :]
                else:
                    other = xn[p][:, HALO:HALO + T]
                eng.tensor_tensor(yout[p][:, :], other, prep[1][:, :], ALU.add).then_inc(drained[1], 1)
                wait_drained(eng, "out", m)
                if rev:
                    eng.bn_stats(stats[:, m, :] if isinstance(m, int) else stats[:, bass.ds(m, 1), :],
                                 yout[p][:, :]).then_inc(stats_done, 1)

            steps = [(plan["center"], center), (plan["normalize"], normalize)] if layer3 else []
            for rest_step, lo_step in zip(each("rest", split_rest), each("lo", split_lo)):
                steps += [rest_step, lo_step]
            steps += [(plan["relu"], relu_dt), (plan["lost"], lost_part), (plan["add_log"], add_log),
                      (plan["add_relu"], add_relu), (plan["scale"], scale_x)]

            def product(c, p, u):
                k = c * KB + u // PER
                need(eng, b_filled, k + 1)
                if u == 0:
                    need(eng, dtx_ready, c + 1)
                need(eng, scan_done, c * UNITS + u - RING + 1)
                eng.tensor_tensor(dbx[:, u % RING, :], dtx[p][:, block_of(u), :], psB[(u // PER) % 2][:, :],
                                  ALU.mult).then_inc(dbx_done, 1)

            def scan(c, p, u):
                g = c * UNITS + u
                need(eng, exp_done, g + 1)
                need(eng, dbx_done, g + 1)
                need(eng, prod_done, g - STATES + 1)
                need(eng, scan_done, g - STATES + 1)
                if STATES < UNITS:
                    need(eng, saved, (UNITS // SAVE) * (c - 1) + u // SAVE + 1)
                    need(eng, saved, (UNITS // SAVE) * c + (u - STATES) // SAVE + 1)
                    eng.tensor_tensor_scan(hs[:, u % STATES, :], da[:, u % DECAYS, :], dbx[:, u % RING, :],
                                           carry[:, u:u + 1], ALU.mult, ALU.add).then_inc(scan_done, 1)
                    if u % SAVE == SAVE - 1:
                        need(eng, scan_done, g + 1)
                        lo = (u + 1 - SAVE) % STATES
                        eng.tensor_copy(carry[:, u + 1 - SAVE:u + 1], hs[:, lo:lo + SAVE, T - 1:T]
                                        .rearrange("p u t -> p (u t)")).then_inc(saved, 1)
                elif rev:
                    eng.tensor_tensor_scan(hs[:, u, ::-1], da[:, u % DECAYS, ::-1], dbx[:, u % RING, ::-1],
                                           hs[:, u, 0:1], ALU.mult, ALU.add).then_inc(scan_done, 1)
                else:
                    eng.tensor_tensor_scan(hs[:, u, :], da[:, u % DECAYS, :], dbx[:, u % RING, :],
                                           hs[:, u, T - 1:T], ALU.mult, ALU.add).then_inc(scan_done, 1)

            def chunk(c, p, last):
                first = isinstance(c, int) and c == 0
                for u in range(UNITS):
                    product(c, p, u)
                    if u > 0:
                        scan(c, p, u - 1)
                    if layer3 and u == plan["skip0"]:
                        skip(c, p, 0)
                    if not first:
                        if u == plan["skip"]:
                            for b in ((1,) if layer3 else (0, 1)):
                                skip(c - 1, 1 - p, b)
                        if u == plan["gate"]:
                            gate(c - 1, 1 - p)
                        if u == plan["result"] and kind != "forward":
                            add_out(c - 1, 1 - p)
                    if not last:
                        for step in due(steps, u):
                            step(c + 1, 1 - p)
                scan(c, p, UNITS - 1)

            def post(m, p):
                for b in ((1,) if layer3 else (0, 1)):
                    skip(m, p, b)
                gate(m, p)
                if kind != "forward":
                    add_out(m, p)
                if rev:
                    eng.wait_ge(stats_done, CHUNKS)
                    eng.bn_aggr(aggr[:, :], stats[:, :, :].rearrange("p n s -> p (n s)")).then_inc(stats_done, 1)

            run(eng, steps, chunk, post)

        @block.tensor
        def _(eng):
            eng.wait_ge(w_loaded, 16)
            eng.wait_ge(wconv_ready, 2 + (8 if layer3 else 4))
            eng.wait_ge(consts, ALL_CONSTS)
            eng.wait_ge(zeroed, SELECT_MADE)
            for k in range(2 if layer3 else 4):
                i, b = (k, k) if layer3 else (k // 2, k % 2)
                mm = eng.matmul(prep[0][:, 128 * k:128 * k + 128], W["wdtr"][0:32, 128 * i:128 * i + 128],
                                W["wdt"][0:32, 128 * b:128 * b + 128], start=True, stop=True)
            mm.then_inc(wdt_filled, 1)
            eng.wait_ge(wdt_ready, 1)

            def source(p, shift):
                if layer3:
                    return xn[p][:, HALO - shift:HALO - shift + T]
                first = 1 + shift if rev else 1 - shift
                return xin[p][:, first:first + T]

            def mean(m, p):
                need(eng, x_loaded[p], 8 * (m - p) + 16)
                wait_bank(eng, "mean", m)
                eng.matmul(prep[0][:, :], ones[:, :], xin[p][:, 0:T], start=True, stop=True).then_inc(filled[0], 1)

            def var(m, p):
                need(eng, sq_ready, m + 1)
                wait_bank(eng, "var", m)
                eng.matmul(prep[1][:, :], ones[:, :], sq[:, :], start=True, stop=True).then_inc(filled[1], 1)

            def conv(m, p, b):
                if layer3:
                    need(eng, xhat_ready, m + 1)
                    if not isinstance(m, int) or m >= 1:
                        need(eng, halo_ready, m)
                    need(eng, paired, 64 * m + 64)
                else:
                    need(eng, x_loaded[p], 8 * (m - p) + 16)
                wait_bank(eng, f"conv{b}", m)
                for k in range(CONVS):
                    moving = xpair[b][:, 2 * k + 1:2 * k + 1 + T] if layer3 else source(p, TAPS - 1 - k)
                    mm = eng.matmul(prep[b][:, :], wconv[:, k, b, :], moving, start=(k == 0), stop=(k == CONVS - 1))
                mm.then_inc(filled[b], 1)

            def gates(m, p, b):
                wait_bank(eng, f"gate{b}", m)
                eng.matmul(prep[b][:, :], W["wz"][:, 128 * b:128 * b + 128], source(p, 0),
                           start=True, stop=True).then_inc(filled[b], 1)

            def bc(m, p, q):
                name = f"bc{q}"
                wait_bank(eng, name, m)
                out = prep[bank_of[name]][0:96, :]
                if layer3:
                    weight = W["wb"] if q < 2 else W["wc"]
                    eng.matmul(out, weight, xc[p][:, q % 2, :], start=True, stop=True).then_inc(filled[bank_of[name]], 1)
                else:
                    for b in (0, 1):
                        mm = eng.matmul(out, W["wbc"][:, 96 * b:96 * b + 96], xc[p][:, b, :],
                                        start=(b == 0), stop=(b == 1))
                    mm.then_inc(filled[0], 1)

            def dts(m, p, b):
                wait_bank(eng, f"dt{b}", m)
                inner = [b] if layer3 else [0, 1]
                for i in inner:
                    mm = eng.matmul(prep[b][:, :], wdt[:, b if layer3 else 2 * i + b, :], xc[p][:, i, :],
                                    start=(i == inner[0]), stop=(i == inner[-1]))
                mm.then_inc(filled[b], 1)

            def project_out(m, p):
                need(eng, y_ready, m + 1)
                wait_bank(eng, "out", m)
                for b in (0, 1):
                    mm = eng.matmul(prep[1][:, :], W["wout"][:, 128 * b:128 * b + 128], yv[:, b, :],
                                    start=(b == 0), stop=(b == 1))
                mm.then_inc(filled[1], 1)

            steps = [(plan["mean"], mean), (plan["var"], var)] if layer3 else []
            steps += (each("conv", conv) + each("gates", gates) + each("bc", bc) + each("dts", dts))

            def broadcast_c(c, p, u):
                if u % PER == 0:
                    k, kk = c * KB + u // PER, u // PER
                    qc, rc = (2 + block_of(u), state_of(u)) if layer3 else (0, STATE + kk)
                    need(eng, c_copied, k - 1)
                    eng.matmul(psC[kk % 2][:, :], select[:, rc, :], bcs[p][:, qc, :],
                               start=True, stop=True).then_inc(c_filled, 1)


            def sum_state(c, p, u):
                if u + 2 in MERGES:
                    return
                if u in MERGES:
                    need(eng, merge_done, merges_before(c, u + 1))
                else:
                    need(eng, prod_done, c * UNITS + u + 1)
                if state_of(u) == 0:
                    need(eng, skip_added, 2 * c - 1 + block_of(u))
                eng.matmul(psY[block_of(u)][:, :], ident[:, :], hc[:, u % SUMS, :], start=(state_of(u) == 0),
                           stop=(state_of(u) == STATE - 1)).then_inc(sum_done, 1)

            def chunk(c, p, last):
                for u in range(UNITS):
                    if u % PER == 0:
                        k = c * KB + u // PER
                        kk = u // PER
                        if u == 0:
                            need(eng, lo_ready, (c + 1) * NBC)
                            need(eng, mid_ready, (c + 1) * NBC)
                        qb, rb = (block_of(u), state_of(u)) if layer3 else (0, kk)
                        need(eng, dbx_done, (k - 1) * PER)
                        eng.matmul(psB[kk % 2][:, :], select[:, rb, :], bcs[p][:, qb, :],
                                   start=True, stop=True).then_inc(b_filled, 1)
                    first = isinstance(c, int) and c == 0
                    if u >= CAST_LAG:
                        broadcast_c(c, p, u - CAST_LAG)
                    elif not first:
                        broadcast_c(c - 1, 1 - p, UNITS + u - CAST_LAG)
                    if u >= LAG:
                        sum_state(c, p, u - LAG)
                    elif not first:
                        sum_state(c - 1, 1 - p, UNITS + u - LAG)
                    if not last:
                        for step in due(steps, u):
                            step(c + 1, 1 - p)
                    if u == plan["out"] and not first:
                        project_out(c - 1, 1 - p)

            def post(m, p):
                for u in range(UNITS - CAST_LAG, UNITS):
                    broadcast_c(m, p, u)
                for u in range(UNITS - LAG, UNITS):
                    sum_state(m, p, u)
                project_out(m, p)

            run(eng, steps, chunk, post)



ATTN_SLOTS = dict(
    line1=0, queries=3, keys=7, values=9, line0=9, maxima=12,
    stack=0, queries_out=6, first=8, values_out=9, finish=10, second=12,
    keys_out=7, split=8, norm1=8, rests=8, spread=9, third=11, norm0=15, scores=9)


def attention_phase(nc, vertical, x_dram, w_dram, out_dram):
    tag = "av" if vertical else "ah"
    at, width = offsets(ATTN_COLS)
    small = at["kc"][0]
    PAIRS = LINES // 2
    BLOCKS = LINES // BLOCK
    PB = BLOCK // 2
    BUFS = 3
    W2 = 2 * SIDE
    CORE = 6 * HD
    KROWS = CORE + 3 * S7
    Q_PARTS, K_PARTS = (0, 0, 1, 1, 2, 0), (0, 1, 0, 1, 0, 2)
    NUM, DEN = 0, 1
    STACKS = 4

    with ExitStack() as ctx:
        def sb(name, shape, dt=F32):
            return ctx.enter_context(nc.sbuf_tensor(f"{tag}_{name}", shape, dt))

        def pb(name, shape):
            return ctx.enter_context(nc.psum_tensor(f"{tag}_{name}", shape, F32))

        sems = []

        def sem(name):
            sems.append(ctx.enter_context(nc.semaphore(f"{tag}_{name}")))
            return sems[-1]

        w = sb("w", [C, small])
        W = {n: w[:, a:b] for n, (a, b) in at.items() if b <= small}
        shape = [C, SIDE, BLOCK] if vertical else [C, BLOCK, SIDE]
        xb = [sb(f"xb{p}", shape) for p in range(BUFS)]
        kc = xb[2][:, :, :].rearrange("c a b -> c (a b)")[:, 0:HEADS * SIDE]
        ident = sb("ident", [C, 128])
        identb = sb("identb", [C, 128], BF16)
        selm = sb("selm", [3 * HEADS, HEADS, HALF], BF16)
        ones = sb("ones", [HALF, 2, 32])
        zero_row = sb("zero_row", [C, SIDE])
        bqs = sb("bqs", [C, 1])
        tb1 = sb("tb1", [C, SIDE], BF16)
        tb2 = sb("tb2", [C, SIDE], BF16)
        tf = [sb(f"tf{i}", [C, SIDE]) for i in (0, 1)]
        xq = [sb(f"xq{p}", [C, W2]) for p in (0, 1)]
        xv = [sb(f"xv{p}", [C, W2]) for p in (0, 1)]
        full = sb("full", [C, 2, W2])
        rest = sb("rest", [C, 2, W2])
        parts = [sb(f"parts{p}", [C, 3, 2, W2], BF16) for p in (0, 1)]
        st = [sb(f"st{q}", [C, 2, HEADS, W2], BF16) for q in range(STACKS)]
        va = [sb(f"va{p}", [HALF, 4, 4, 2, 32]) for p in (0, 1)]
        mx = sb("mx", [HALF, 4, HEADS])
        mxr = sb("mxr", [HALF, 4, HEADS])
        mxp = sb("mxp", [HALF, 4, 3, HEADS], BF16)
        mxs = [sb(f"mxs{p}", [3 * HEADS, W2], BF16) for p in (0, 1)]
        pt = sb("pt", [HALF, 16, 2, SIDE])
        rec = sb("rec", [C, SIDE])
        on = sb("on", [C, W2])
        obuf = [sb(f"obuf{p}", [C, W2]) for p in (0, 1)]

        psS = [pb(f"psS{b}", [HALF, 2, SIDE]) for b in (0, 1)]
        psT = [pb(f"psT{b}", [HALF, 2, SIDE]) for b in (0, 1)]
        psO = [pb(f"psO{l}", [C, 2, SIDE]) for l in (0, 1)]
        psP = pb("psP", [C, 512])

        w_loaded = sem("w_loaded")
        zeroed = sem("zeroed")
        consts = sem("consts")
        setup = sem("setup")
        blk_loaded = [sem(f"blk_loaded{p}") for p in range(BUFS)]
        blk_stored = [sem(f"blk_stored{p}") for p in range(BUFS)]
        edge_stored = sem("edge_stored")
        xq_ready = sem("xq_ready")
        xv_ready = sem("xv_ready")
        q_filled = sem("q_filled")
        k_filled = sem("k_filled")
        v_filled = sem("v_filled")
        q_ready = sem("q_ready")
        k_ready = sem("k_ready")
        v_ready = sem("v_ready")
        part1_ready = sem("part1_ready")
        rest_ready = sem("rest_ready")
        part2_ready = sem("part2_ready")
        part3_ready = sem("part3_ready")
        stacked = [sem(f"stacked{p}") for p in (0, 1)]
        s_filled = sem("s_filled")
        max_ready = sem("max_ready")
        max_split = sem("max_split")
        m_filled = sem("m_filled")
        m_ready = sem("m_ready")
        t_filled = sem("t_filled")
        p_ready = sem("p_ready")
        pv_done = sem("pv_done")
        rec_ready = sem("rec_ready")
        norm_done = sem("norm_done")
        obuf_ready = sem("obuf_ready")
        line_out = sem("line_out")

        def has(n):
            return not isinstance(n, int) or 0 <= n < PAIRS

        HEAD, TAIL = 4, PAIRS - 4

        def run(eng, iteration):
            for m in range(-3, HEAD):
                iteration(m, m % STACKS)
            with eng.Fori(HEAD // STACKS, TAIL // STACKS) as i:
                for q in range(STACKS):
                    iteration(STACKS * i + q, q)
            for m in range(TAIL, PAIRS + 1):
                iteration(m, m % STACKS)

        at_slot = ATTN_SLOTS

        def scored(u):
            slots = at_slot["scores"]
            return range(min(16, -(-16 * u // slots)), min(16, -(-16 * (u + 1) // slots)))

        def unit(v):
            return v % HEADS, slice(v // HEADS * SIDE, v // HEADS * SIDE + SIDE)

        CONSTS = 6
        SETUP = 3 + 7 * HEADS + 3 + 2 * (STACKS - 1)

        ctx.callback(clear_semaphores, nc, sems)
        block = ctx.enter_context(nc.Block())

        @block.sync
        def _(eng):
            eng.dma_start(w[:, :], w_dram[:, 0:small]).then_inc(w_loaded, 16)
            eng.dma_start(kc[CORE:C, :], w_dram[CORE:C, small:width]).then_inc(w_loaded, 16)

            def part(dram, b, first_row):
                if vertical:
                    return dram[:, first_row:first_row + SIDE, b * BLOCK:(b + 1) * BLOCK]
                return dram[:, first_row + b * BLOCK:first_row + (b + 1) * BLOCK, :]

            def load(b):
                need(eng, blk_stored[b % BUFS], 16 * (b // BUFS))
                eng.dma_start(xb[b % BUFS][:, :, :], part(x_dram, b, 0)).then_inc(blk_loaded[b % BUFS], 16)

            load(0)
            load(1)
            eng.wait_ge(consts, CONSTS)
            eng.wait_ge(setup, SETUP)
            load(2)
            eng.dma_start(out_dram[:, 0, :], zero_row[:, :]).then_inc(edge_stored, 16)
            eng.dma_start(out_dram[:, SIDE + 1, :], zero_row[:, :]).then_inc(edge_stored, 16)
            for b in range(BLOCKS):
                eng.wait_ge(line_out, PB * (b + 1))
                eng.dma_start(part(out_dram, b, 1), xb[b % BUFS][:, :, :]).then_inc(blk_stored[b % BUFS], 16)
                if b + BUFS < BLOCKS:
                    load(b + BUFS)
            eng.wait_ge(edge_stored, 32)
            for p in range(BUFS):
                eng.wait_ge(blk_stored[p], 16 * len(range(p, BLOCKS, BUFS)))

        @block.gpsimd
        def _(eng):
            make_identity(eng, ident, 128, zeroed, consts)
            eng.memset(zero_row[:, :], 0.0).then_inc(consts, 1)
            eng.memset(ones[:, :, :], 0.0).then_inc(zeroed, 1)
            eng.wait_ge(zeroed, 2)
            eng.memset(ones[:, 0, 0:HD], 1.0).then_inc(consts, 1)
            eng.memset(ones[:, 1, HD:2 * HD], 1.0).then_inc(consts, 1)
            for p in (0, 1):
                eng.memset(va[p][:, :, :, :, :], 0.0).then_inc(consts, 1)

            def lines(tile, r):
                at_r = slice(r, r + 2) if isinstance(r, int) else bass.ds(r, 2)
                if vertical:
                    return tile[:, :, at_r].rearrange("c s r -> c r s")
                return tile[:, at_r, :]

            two = lambda tile: tile[:, :].rearrange("c (r s) -> c r s", r=2)

            def take_q(n, p, tile, r):
                need(eng, k_filled, n - 1)
                eng.tensor_copy(two(xq[p]), lines(tile, r)).then_inc(xq_ready, 1)

            def take_v(n, p, tile, r):
                need(eng, v_filled, n - 1)
                eng.tensor_copy(two(xv[p]), lines(tile, r)).then_inc(xv_ready, 1)

            def put(n, p, tile, r):
                need(eng, obuf_ready, n + 1)
                eng.tensor_copy(lines(tile, r), two(obuf[p])).then_inc(line_out, 1)

            QA, VA = 5, 3

            def one_block(b):
                n0, buf, last = b * PB, xb[b % BUFS], b == BLOCKS - 1
                nxt = xb[(b + 1) % BUFS]
                with eng.Fori(0, (PB - QA) // 2) as k:
                    for j in (0, 1):
                        par = (n0 + j) % 2
                        take_q(n0 + 2 * k + j + QA, (par + QA) % 2, buf, 4 * k + 2 * j + 2 * QA)
                        take_v(n0 + 2 * k + j + VA, (par + VA) % 2, buf, 4 * k + 2 * j + 2 * VA)
                        put(n0 + 2 * k + j, par, buf, 4 * k + 2 * j)
                for r in range((PB - QA) // 2 * 2, PB):
                    n = n0 + r
                    for ahead, take in ((QA, take_q), (VA, take_v)):
                        if r + ahead < PB:
                            take(n + ahead, (n + ahead) % 2, buf, 2 * (r + ahead))
                        elif not last:
                            need(eng, blk_loaded[(b + 1) % BUFS], 16 * ((b + 1) // BUFS) + 16)
                            take(n + ahead, (n + ahead) % 2, nxt, 2 * (r + ahead - PB))
                    put(n, n % 2, buf, 2 * r)

            eng.wait_ge(blk_loaded[0], 16)
            for n in range(2):
                take_q(n, n % 2, xb[0], 2 * n)
                take_v(n, n % 2, xb[0], 2 * n)
            take_q(2, 0, xb[0], 4)
            take_q(3, 1, xb[0], 6)
            take_v(2, 0, xb[0], 4)
            take_q(4, 0, xb[0], 8)
            for b in range(BLOCKS):
                one_block(b)

        @block.scalar
        def _(eng):
            eng.wait_ge(w_loaded, 32)
            eng.wait_ge(consts, CONSTS)
            eng.wait_ge(setup, SETUP)

            def exponential(m, u):
                need(eng, t_filled, 16 * m + u + 1)
                if u % 8 == 0:
                    need(eng, pv_done, 2 * m - 1 + u // 8)
                eng.activation(pt[:, u, :, :], psT[u % 2][:, :, :], ACT.Exp).then_inc(p_ready, 1)

            def stack(n, q, t):
                need(eng, part3_ready, n + 1)
                need(eng, t_filled, 16 * (n - STACKS + 1))
                need(eng, s_filled, 16 * (n - 1))
                for g, part in enumerate(K_PARTS if t else Q_PARTS):
                    eng.dma_start(st[q][HD * g:HD * g + HD, t, :, :],
                                  parts[q % 2][:, part, t, :]).then_inc(stacked[q % 2], 16)

            def queries(n):
                need(eng, q_filled, n + 1)
                need(eng, rest_ready, n)
                eng.activation(full[:, 0, :], psP[:, 0:W2], ACT.Identity, bias=bqs[:, 0:1],
                               scale=float(HD) ** -0.5).then_inc(q_ready, 1)

            def first_parts(n, p):
                need(eng, q_ready, n + 1)
                need(eng, k_ready, n + 1)
                need(eng, stacked[p], 12 * 8 * (n - p))
                eng.activation(parts[p][:, 0, :, :], full[:, :, :], ACT.Copy).then_inc(part1_ready, 1)

            def second_parts(n, p):
                need(eng, rest_ready, n + 1)
                eng.activation(parts[p][:, 1, :, :], rest[:, :, :], ACT.Copy).then_inc(part2_ready, 1)

            def values(n, p):
                need(eng, v_filled, n + 1)
                need(eng, pv_done, 2 * (n - 1))
                src = psP[0:HALF, 0:4 * C].rearrange("p (a j s d) -> p a j s d", a=4, j=4, s=2)
                for s in (0, 1):
                    eng.activation(va[p][:, :, :, s, HD * s:HD * s + HD], src[:, :, :, s, :],
                                   ACT.Copy).then_inc(v_ready, 1)

            def finished(n, p):
                need(eng, norm_done, 2 * n + 2)
                need(eng, line_out, n - 1)
                eng.activation(obuf[p][:, :], on[:, :], ACT.Identity, bias=W["bv"]).then_inc(obuf_ready, 1)

            def iteration(m, q):
                p = q % 2
                for u in range(16):
                    if has(m):
                        exponential(m, u)
                    if u in (at_slot["stack"], at_slot["stack"] + 1) and has(m + 2):
                        stack(m + 2, (q + 2) % STACKS, u - at_slot["stack"])
                    if u == at_slot["queries_out"] and has(m + 3):
                        queries(m + 3)
                    if u == at_slot["first"] and has(m + 3):
                        first_parts(m + 3, 1 - p)
                    if u == at_slot["values_out"] and has(m + 1):
                        values(m + 1, 1 - p)
                    if u == at_slot["finish"] and has(m - 1):
                        finished(m - 1, 1 - p)
                    if u == at_slot["second"] and has(m + 3):
                        second_parts(m + 3, 1 - p)

            run(eng, iteration)

        @block.vector
        def _(eng):
            eng.wait_ge(w_loaded, 32)
            eng.wait_ge(consts, CONSTS)
            eng.tensor_scalar(bqs[:, :], W["bq"], float(HD) ** -0.5, None, ALU.mult).then_inc(setup, 1)
            eng.tensor_copy(identb[:, :], ident[:, :]).then_inc(setup, 1)
            eng.tensor_copy(selm[:, :, :], W["selm"][0:3 * HEADS, :].rearrange("c (h k) -> c h k", h=HEADS)
                            .broadcast_to([3 * HEADS, HEADS, HALF])).then_inc(setup, 1)
            rows = slice(CORE, C)
            done = 3
            for h in range(HEADS):
                table = kc[rows, h * SIDE:(h + 1) * SIDE]
                mask = lambda k: W["mask"][rows, k:k + 1]
                need(eng, setup, done)
                eng.tensor_copy(tb1[rows, :], table).then_inc(setup, 1)
                eng.wait_ge(setup, done + 1)
                eng.tensor_tensor(tf[0][rows, :], table, tb1[rows, :], ALU.subtract).then_inc(setup, 1)
                eng.wait_ge(setup, done + 2)
                eng.tensor_copy(tb2[rows, :], tf[0][rows, :]).then_inc(setup, 1)
                eng.wait_ge(setup, done + 3)
                eng.tensor_tensor(tf[1][rows, :], tf[0][rows, :], tb2[rows, :], ALU.subtract).then_inc(setup, 1)
                eng.wait_ge(setup, done + 4)
                eng.tensor_scalar(tf[0][rows, :], tb1[rows, :], mask(0), None, ALU.mult).then_inc(setup, 1)
                eng.wait_ge(setup, done + 5)
                eng.scalar_tensor_tensor(tf[0][rows, :], tb2[rows, :], mask(1), tf[0][rows, :],
                                         ALU.mult, ALU.add).then_inc(setup, 1)
                eng.wait_ge(setup, done + 6)
                eng.scalar_tensor_tensor(st[0][rows, 1, h, 0:SIDE], tf[1][rows, :], mask(2), tf[0][rows, :],
                                         ALU.mult, ALU.add).then_inc(setup, 1)
                done += 7
            eng.wait_ge(setup, done)
            eng.tensor_copy(st[0][rows, 1, :, SIDE:W2], st[0][rows, 1, :, 0:SIDE]).then_inc(setup, 1)
            onehot = W["onehot"][rows, :].unsqueeze(1).broadcast_to([C - CORE, HEADS, SIDE])
            for l in (0, 1):
                eng.tensor_copy(st[0][rows, 0, :, SIDE * l:SIDE * l + SIDE], onehot).then_inc(setup, 1)
            eng.wait_ge(setup, done + 3)
            for q in range(1, STACKS):
                for t in (0, 1):
                    eng.tensor_copy(st[q][rows, t, :, :], st[0][rows, t, :, :]).then_inc(setup, 1)
            eng.wait_ge(setup, SETUP)

            def maximum(n, u):
                if u == 0:
                    need(eng, max_split, 4 * n)
                need(eng, s_filled, 16 * n + u + 1)
                h, l = u % HEADS, u // HEADS
                eng.tensor_reduce(mx[:, 2 * l:2 * l + 2, h:h + 1], psS[u % 2][:, :, :], AX_X, ALU.max,
                                  negate=True).then_inc(max_ready, 1)

            def split_maxima(n):
                need(eng, max_ready, 16 * n + 16)
                need(eng, m_filled, n)
                eng.tensor_copy(mxp[:, :, 0, :], mx[:, :, :]).then_inc(max_split, 1)
                need(eng, max_split, 4 * n + 1)
                eng.tensor_tensor(mxr[:, :, :], mx[:, :, :], mxp[:, :, 0, :], ALU.subtract).then_inc(max_split, 1)
                need(eng, max_split, 4 * n + 2)
                eng.tensor_copy(mxp[:, :, 1, :], mxr[:, :, :]).then_inc(max_split, 1)
                need(eng, max_split, 4 * n + 3)
                eng.tensor_tensor(mxp[:, :, 2, :], mxr[:, :, :], mxp[:, :, 1, :], ALU.subtract).then_inc(max_split, 1)

            def spread_maxima(n, p):
                need(eng, m_filled, n + 1)
                need(eng, t_filled, 16 * (n - 1))
                eng.tensor_copy(mxs[p][:, :], psP[0:3 * HEADS, 0:W2]).then_inc(m_ready, 1)

            def keys(n):
                need(eng, k_filled, n + 1)
                need(eng, rest_ready, n)
                need(eng, part1_ready, n)
                eng.tensor_scalar(full[:, 1, :], psP[:, 0:W2], W["bk"], None, ALU.add).then_inc(k_ready, 1)

            def rests(n, p):
                need(eng, part1_ready, n + 1)
                need(eng, part3_ready, n)
                eng.tensor_tensor(rest[:, :, :], full[:, :, :], parts[p][:, 0, :, :], ALU.subtract).then_inc(rest_ready, 1)

            def third_parts(n, p):
                need(eng, part2_ready, n + 1)
                eng.tensor_tensor(parts[p][:, 2, :, :], rest[:, :, :], parts[p][:, 1, :, :],
                                  ALU.subtract).then_inc(part3_ready, 1)

            def normalize(n, l):
                need(eng, pv_done, 2 * n + l + 1)
                need(eng, norm_done, 2 * n + l)
                eng.reciprocal(rec[:, :], psO[l][:, DEN, :]).then_inc(rec_ready, 1)
                need(eng, rec_ready, 2 * n + l + 1)
                need(eng, obuf_ready, n)
                eng.tensor_tensor(on[:, SIDE * l:SIDE * l + SIDE], rec[:, :], psO[l][:, NUM, :],
                                  ALU.mult).then_inc(norm_done, 1)

            def iteration(m, q):
                p = q % 2
                for u in range(16):
                    if has(m + 1):
                        for v in scored(u):
                            maximum(m + 1, v)
                    if u == at_slot["keys_out"] and has(m + 3):
                        keys(m + 3)
                    if u == at_slot["split"] and has(m + 1):
                        split_maxima(m + 1)
                    if u == at_slot["norm1"] and has(m - 1):
                        normalize(m - 1, 1)
                    if u == at_slot["rests"] and has(m + 3):
                        rests(m + 3, 1 - p)
                    if u == at_slot["spread"] and has(m + 1):
                        spread_maxima(m + 1, 1 - p)
                    if u == at_slot["third"] and has(m + 3):
                        third_parts(m + 3, 1 - p)
                    if u == at_slot["norm0"] and has(m):
                        normalize(m, 0)

            run(eng, iteration)

        @block.tensor
        def _(eng):
            eng.wait_ge(w_loaded, 32)
            eng.wait_ge(consts, CONSTS)
            eng.wait_ge(setup, SETUP)

            def scores_t(m, q, u):
                if u == 0:
                    need(eng, m_ready, m + 1)
                need(eng, p_ready, 16 * m + u - 1)
                h, line = unit(u)
                for a in (0, 1):
                    keys = slice(line.start + HALF * a, line.start + HALF * a + HALF)
                    eng.matmul(psT[u % 2][:, a, :], st[q][0:KROWS, 1, h, keys], st[q][0:KROWS, 0, h, line],
                               start=True, stop=False)
                    mm = eng.matmul(psT[u % 2][:, a, :], selm[:, h, :], mxs[q % 2][:, line], start=False, stop=True)
                mm.then_inc(t_filled, 1)

            def scores(n, q, u):
                if u == 0:
                    need(eng, stacked[q % 2], 12 * 8 * (n - q % 2) + 12 * 16)
                need(eng, max_ready, 16 * n + u - 1)
                h, line = unit(u)
                for half in (0, 1):
                    queries = slice(line.start + HALF * half, line.start + HALF * half + HALF)
                    mm = eng.matmul(psS[u % 2][:, half, :], st[q][0:KROWS, 0, h, queries],
                                    st[q][0:KROWS, 1, h, line], start=True, stop=True)
                mm.then_inc(s_filled, 1)

            def products(n, p, l, quarter):
                what, s = quarter // 2, quarter % 2
                if quarter == 0:
                    need(eng, p_ready, 16 * n + 8 * l + 8)
                    need(eng, v_ready, 2 * n + 2)
                    need(eng, norm_done, 2 * n + l - 1)
                for a in (0, 1):
                    for j in range(4):
                        lhsT = va[p][:, 2 * l + a, j, s, :] if what == NUM else ones[:, s, :]
                        mm = eng.matmul(psO[l][32 * j:32 * j + 32, what, :], lhsT, pt[:, 8 * l + 2 * j + s, a, :],
                                        start=(s == 0 and a == 0), stop=(s == 1 and a == 1))
                if quarter == 3:
                    mm.then_inc(pv_done, 1)

            def project_queries(n, p):
                need(eng, xq_ready, n + 1)
                need(eng, m_ready, n - 2)
                if isinstance(n, int) and n < 3:
                    need(eng, k_ready, n)
                eng.matmul(psP[:, 0:W2], W["wq"], xq[p][:, :], start=True, stop=True).then_inc(q_filled, 1)

            def project_keys(n, p):
                need(eng, q_ready, n + 1)
                eng.matmul(psP[:, 0:W2], W["wk"], xq[p][:, :], start=True, stop=True).then_inc(k_filled, 1)

            def project_values(n, p):
                need(eng, xv_ready, n + 1)
                if has(n + 2):
                    need(eng, k_ready, n + 3)
                else:
                    need(eng, m_ready, n)
                for a in range(4):
                    mm = eng.matmul(psP[0:HALF, C * a:C * a + C], xv[p][:, HALF * a:HALF * a + HALF], W["wv"],
                                    start=True, stop=True)
                mm.then_inc(v_filled, 1)

            def transpose_maxima(n):
                need(eng, max_split, 4 * n + 4)
                need(eng, v_ready, 2 * n + 2)
                for a in range(4):
                    mm = eng.matmul(psP[0:3 * HEADS, HALF * a:HALF * a + HALF], mxp[:, a, :, :],
                                    identb[0:HALF, 0:HALF], start=True, stop=True)
                mm.then_inc(m_filled, 1)

            def iteration(m, q):
                p = q % 2
                for u in range(16):
                    if has(m):
                        scores_t(m, q, u)
                    if has(m + 1):
                        for v in scored(u):
                            scores(m + 1, (q + 1) % STACKS, v)
                    line1, line0 = u - at_slot["line1"], u - at_slot["line0"]
                    if 0 <= line1 < 4 and has(m - 1):
                        products(m - 1, 1 - p, 1, line1)
                    if 0 <= line0 < 4 and has(m):
                        products(m, p, 0, line0)
                    if u == at_slot["queries"] and has(m + 3):
                        project_queries(m + 3, 1 - p)
                    if u == at_slot["keys"] and has(m + 3):
                        project_keys(m + 3, 1 - p)
                    if u == at_slot["values"] and has(m + 1):
                        project_values(m + 1, 1 - p)
                    if u == at_slot["maxima"] and has(m + 1):
                        transpose_maxima(m + 1)

            run(eng, iteration)



def lepe_phase(nc, h_dram, v_dram, w_dram, out_dram):
    ROWS = 8
    PAIRS = ROWS // 2
    STEPS = SIDE // ROWS
    WIDE = SIDE + 2
    at, width = offsets(LEPE_COLS)

    with ExitStack() as ctx:
        def sb(name, shape):
            return ctx.enter_context(nc.sbuf_tensor(f"le_{name}", shape, F32))

        def pb(name, shape):
            return ctx.enter_context(nc.psum_tensor(f"le_{name}", shape, F32))

        sems = []

        def sem(name):
            sems.append(ctx.enter_context(nc.semaphore(f"le_{name}")))
            return sems[-1]

        w = sb("w", [C, width])
        W = {n: w[:, a:b] for n, (a, b) in at.items()}
        ident = sb("ident", [C, 128])
        taps = sb("taps", [C, 8, 128])
        hin = [sb(f"hin{p}", [C, ROWS + 2, WIDE]) for p in (0, 1)]
        vin = [sb(f"vin{p}", [C, ROWS + 2, WIDE]) for p in (0, 1)]
        acc = sb("acc", [C, ROWS, SIDE])
        ah = sb("ah", [C, ROWS, SIDE])
        gh = [sb(f"gh{p}", [C, ROWS, SIDE]) for p in (0, 1)]
        gv = sb("gv", [C, ROWS, SIDE])
        both = sb("both", [C, ROWS, SIDE])
        total = [sb(f"total{p}", [C, ROWS, SIDE]) for p in (0, 1)]
        xo = [sb(f"xo{p}", [C, ROWS * SIDE]) for p in (0, 1)]
        edge = sb("edge", [C, 1])
        psH = [pb(f"psH{b}", [C, 2, SIDE]) for b in range(PAIRS)]
        psP = [pb(f"psP{b}", [C, 2 * SIDE]) for b in (0, 1)]

        w_loaded = sem("w_loaded")
        zeroed = sem("zeroed")
        consts = sem("consts")
        taps_ready = sem("taps_ready")
        loaded = [sem(f"loaded{p}") for p in (0, 1)]
        stored = [sem(f"stored{p}") for p in (0, 1)]
        edge_stored = sem("edge_stored")
        h_filled = sem("h_filled")
        h_added = sem("h_added")
        gh_ready = sem("gh_ready")
        tap_done = sem("tap_done")
        gv_ready = sem("gv_ready")
        both_ready = sem("both_ready")
        halfsum_ready = sem("halfsum_ready")
        total_ready = sem("total_ready")
        p_filled = sem("p_filled")
        out_ready = sem("out_ready")

        def has(n):
            return not isinstance(n, int) or 0 <= n < STEPS

        def run(eng, step):
            for n in (-1, 0, 1):
                step(n, n % 2)
            with eng.Fori(1, STEPS // 2 - 1) as i:
                step(2 * i, 0)
                step(2 * i + 1, 1)
            for n in (STEPS - 2, STEPS - 1, STEPS):
                step(n, n % 2)

        ctx.callback(clear_semaphores, nc, sems)
        block = ctx.enter_context(nc.Block())

        @block.sync
        def _(eng):
            eng.dma_start(w[:, :], w_dram).then_inc(w_loaded, 16)
            eng.wait_ge(consts, 6)
            eng.dma_start(out_dram[:, 0:1], edge[:, :], allow_slow_non_contiguous=True).then_inc(edge_stored, 16)
            eng.dma_start(out_dram[:, TOKENS + 1:TOKENS + 2], edge[:, :], allow_slow_non_contiguous=True).then_inc(edge_stored, 16)

            def load(n, p):
                need(eng, h_added, PAIRS * (n - 1))
                need(eng, both_ready, n - 1)
                eng.dma_start(hin[p][:, :, 1:1 + SIDE],
                              h_dram[:, bass.ds(ROWS * n, ROWS + 2), :]).then_inc(loaded[p], 16)
                need(eng, tap_done, 9 * (n - 1))
                eng.dma_start(vin[p][:, :, 1:1 + SIDE],
                              v_dram[:, bass.ds(ROWS * n, ROWS + 2), :]).then_inc(loaded[p], 16)

            def store(n, p):
                need(eng, out_ready, PAIRS * (n + 1))
                eng.dma_start(out_dram[:, bass.ds(ROWS * SIDE * n + 1, ROWS * SIDE)],
                              xo[p][:, :]).then_inc(stored[p], 16)

            load(0, 0)
            load(1, 1)
            load(2, 0)
            with eng.Fori(1, STEPS // 2 - 1) as i:
                load(2 * i + 1, 1)
                store(2 * i - 2, 0)
                load(2 * i + 2, 0)
                store(2 * i - 1, 1)
            load(STEPS - 1, 1)
            store(STEPS - 4, 0)
            store(STEPS - 3, 1)
            store(STEPS - 2, 0)
            store(STEPS - 1, 1)
            eng.wait_ge(edge_stored, 32)
            for p in (0, 1):
                eng.wait_ge(stored[p], 8 * STEPS)

        @block.gpsimd
        def _(eng):
            make_identity(eng, ident, 128, zeroed, consts)
            eng.memset(edge[:, :], 0.0).then_inc(consts, 1)
            for tile in (*hin, *vin):
                eng.memset(tile[:, :, 0:WIDE:WIDE - 1], 0.0).then_inc(consts, 1)

            def step(n, p):
                if not has(n):
                    return
                need(eng, loaded[p], 16 * (n - p) + 32)
                need(eng, halfsum_ready, n)
                eng.tensor_tensor(both[:, :, :], hin[p][:, 1:1 + ROWS, 1:1 + SIDE],
                                  vin[p][:, 1:1 + ROWS, 1:1 + SIDE], ALU.add).then_inc(both_ready, 1)

            run(eng, step)

        @block.scalar
        def _(eng):
            eng.wait_ge(w_loaded, 16)

            def horizontal(n, p):
                need(eng, halfsum_ready, n - 1)
                for u in range(PAIRS):
                    need(eng, h_added, PAIRS * n + u + 1)
                    eng.activation(gh[p][:, 2 * u:2 * u + 2, :], ah[:, 2 * u:2 * u + 2, :], ACT.Gelu,
                                   bias=W["b_h"]).then_inc(gh_ready, 1)

            def vertical(n):
                need(eng, total_ready, n)
                need(eng, tap_done, 9 * (n + 1))
                eng.activation(gv[:, :, :], acc[:, :, :], ACT.Gelu, bias=W["b_v"]).then_inc(gv_ready, 1)

            def results(n, p):
                need(eng, stored[p], 8 * (n - p))
                for u in range(PAIRS):
                    need(eng, p_filled, PAIRS * n + u + 1)
                    eng.activation(xo[p][:, 2 * SIDE * u:2 * SIDE * (u + 1)], psP[u % 2][:, :], ACT.Identity,
                                   bias=W["proj_b"]).then_inc(out_ready, 1)

            def step(n, p):
                if has(n):
                    vertical(n)
                if has(n + 1):
                    horizontal(n + 1, 1 - p)
                if has(n - 1):
                    results(n - 1, 1 - p)

            run(eng, step)

        @block.vector
        def _(eng):
            eng.wait_ge(w_loaded, 16)
            eng.wait_ge(consts, 6)
            for k in range(8):
                eng.tensor_scalar(taps[:, k, :], ident[:, :], W["tap_h"][:, k:k + 1], None,
                                  ALU.mult).then_inc(taps_ready, 1)

            def vertical(n, p):
                need(eng, loaded[p], 16 * (n - p) + 32)
                need(eng, gv_ready, n)
                for k in range(9):
                    dy, dx = k // 3, k % 3
                    source = vin[p][:, dy:dy + ROWS, dx:dx + SIDE]
                    tap = W["tap_v"][:, k:k + 1]
                    if k == 0:
                        eng.tensor_scalar(acc[:, :, :], source, tap, None, ALU.mult).then_inc(tap_done, 1)
                    else:
                        need(eng, tap_done, 9 * n + k)
                        eng.scalar_tensor_tensor(acc[:, :, :], source, tap, acc[:, :, :],
                                                 ALU.mult, ALU.add).then_inc(tap_done, 1)

            def last_tap(n, p):
                need(eng, loaded[p], 16 * (n - p) + 32)
                for u in range(PAIRS):
                    need(eng, h_filled, PAIRS * n + u + 1)
                    need(eng, gh_ready, PAIRS * (n - 1) + u + 1)
                    eng.scalar_tensor_tensor(ah[:, 2 * u:2 * u + 2, :], hin[p][:, 2 * u + 2:2 * u + 4, 2:2 + SIDE],
                                             W["tap_h"][:, 8:9], psH[u][:, :, :],
                                             ALU.mult, ALU.add).then_inc(h_added, 1)

            def sums(n, p):
                need(eng, both_ready, n + 1)
                need(eng, gh_ready, PAIRS * (n + 1))
                need(eng, p_filled, PAIRS * (n - 1))
                eng.tensor_tensor(total[p][:, :, :], both[:, :, :], gh[p][:, :, :], ALU.add).then_inc(halfsum_ready, 1)
                need(eng, gv_ready, n + 1)
                need(eng, halfsum_ready, n + 1)
                eng.tensor_tensor(total[p][:, :, :], total[p][:, :, :], gv[:, :, :], ALU.add).then_inc(total_ready, 1)

            def step(n, p):
                if has(n):
                    vertical(n, p)
                if has(n + 1):
                    last_tap(n + 1, 1 - p)
                if has(n):
                    sums(n, p)

            run(eng, step)

        @block.tensor
        def _(eng):
            eng.wait_ge(taps_ready, 8)

            def convolve(n, p):
                need(eng, loaded[p], 16 * (n - p) + 32)
                for u in range(PAIRS):
                    need(eng, h_added, PAIRS * (n - 1) + u + 1)
                    for k in range(8):
                        dy, dx = k // 3, k % 3
                        mm = eng.matmul(psH[u][:, :, :], taps[:, k, :],
                                        hin[p][:, 2 * u + dy:2 * u + dy + 2, dx:dx + SIDE],
                                        start=(k == 0), stop=(k == 7))
                    mm.then_inc(h_filled, 1)

            def project(n, p):
                need(eng, total_ready, n + 1)
                for u in range(PAIRS):
                    need(eng, out_ready, PAIRS * n + u - 1)
                    eng.matmul(psP[u % 2][:, :], W["proj"],
                               total[p][:, 2 * u:2 * u + 2, :].rearrange("c r s -> c (r s)"),
                               start=True, stop=True).then_inc(p_filled, 1)

            def step(n, p):
                if has(n + 1):
                    convolve(n + 1, 1 - p)
                if has(n - 1):
                    project(n - 1, 1 - p)

            run(eng, step)



def kv_phase(nc, y_dram, stats_dram, x1_dram, w_dram, x2_dram, ut_dram):
    at, width = offsets(GLOBAL_COLS)
    SUB = T // 128
    GROUPS = 2 * HEADS

    with ExitStack() as ctx:
        def sb(name, shape):
            return ctx.enter_context(nc.sbuf_tensor(f"kv_{name}", shape, F32))

        def pb(name, shape):
            return ctx.enter_context(nc.psum_tensor(f"kv_{name}", shape, F32))

        sems = []

        def sem(name):
            sems.append(ctx.enter_context(nc.semaphore(f"kv_{name}")))
            return sems[-1]

        w = sb("w", [C, width])
        W = {n: w[:, a:b] for n, (a, b) in at.items()}
        ident = sb("ident", [C, 128])
        st = sb("st", [C, 2])
        moments = sb("moments", [C, 2])
        gm = sb("gm", [C, 2])
        gvar = sb("gvar", [C, 1])
        gsd = sb("gsd", [C, 1])
        ga = sb("ga", [C, 1])
        gb = sb("gb", [C, 1])
        epst = sb("epst", [C, 1])
        wmean = sb("wmean", [C, GROUPS, 1])
        wcen = sb("wcen", [C, GROUPS, HD])
        yin = [sb(f"yin{p}", [C, T]) for p in (0, 1)]
        xin = [sb(f"xin{p}", [C, T]) for p in (0, 1)]
        act = [sb(f"act{p}", [C, T]) for p in (0, 1)]
        x2 = [sb(f"x2{p}", [C, T]) for p in (0, 1)]
        sq = sb("sq", [C, SUB * GROUPS, HD])
        ss = sb("ss", [C, SUB * GROUPS, 1])
        sd = sb("sd", [C, SUB * GROUPS, 1])
        kvn = sb("kvn", [C, SUB, GROUPS * HD])
        kvw = [sb(f"kvw{p}", [C, SUB, GROUPS * HD]) for p in (0, 1)]
        kvf = [sb(f"kvf{p}", [C, SUB, GROUPS * HD]) for p in (0, 1)]
        kvb = sb("kvb", [C, 128])
        gmat = sb("gmat", [C, 128])
        ut = sb("ut", [C, 128])
        psK = [pb(f"psK{b}", [C, 2, GROUPS * HD]) for b in range(4)]
        psG = pb("psG", [C, 128])
        psA = pb("psA", [C, 128])
        psU = pb("psU", [C, 128])

        w_loaded = sem("w_loaded")
        zeroed = sem("zeroed")
        consts = sem("consts")
        norm_step = sem("norm_step")
        sd_step = sem("sd_step")
        g_filled = sem("g_filled")
        affine_ready = sem("affine_ready")
        wcen_ready = sem("wcen_ready")
        loaded = [sem(f"loaded{p}") for p in (0, 1)]
        stored = [sem(f"stored{p}") for p in (0, 1)]
        act_ready = sem("act_ready")
        x2_ready = sem("x2_ready")
        k_filled = sem("k_filled")
        sq_ready = sem("sq_ready")
        ss_ready = sem("ss_ready")
        sd_ready = sem("sd_ready")
        sde_ready = sem("sde_ready")
        rsd_ready = sem("rsd_ready")
        kvn_ready = sem("kvn_ready")
        kvw_ready = sem("kvw_ready")
        kvf_ready = sem("kvf_ready")
        kv_summed = sem("kv_summed")
        tail = sem("tail")
        tail_mm = sem("tail_mm")
        ut_stored = sem("ut_stored")

        def has(n):
            return not isinstance(n, int) or 0 <= n < CHUNKS

        def run(eng, step):
            for n in (-1, 0, 1):
                step(n, n % 2)
            with eng.Fori(1, CHUNKS // 2 - 1) as i:
                step(2 * i, 0)
                step(2 * i + 1, 1)
            for n in (CHUNKS - 2, CHUNKS - 1, CHUNKS, CHUNKS + 1):
                step(n, n % 2)

        ctx.callback(clear_semaphores, nc, sems)
        block = ctx.enter_context(nc.Block())

        @block.sync
        def _(eng):
            eng.dma_start(w[:, :], w_dram).then_inc(w_loaded, 16)
            eng.dma_start(st[:, :], stats_dram).then_inc(w_loaded, 16)

            def load(n, p):
                need(eng, x2_ready, n - 1)
                eng.dma_start(yin[p][:, :], y_dram[:, bass.ds(T * n, T)]).then_inc(loaded[p], 16)
                eng.dma_start(xin[p][:, :], x1_dram[:, bass.ds(T * n + 1, T)]).then_inc(loaded[p], 16)

            def store(n, p):
                need(eng, x2_ready, n + 1)
                eng.dma_start(x2_dram[:, bass.ds(T * n, T)], x2[p][:, :]).then_inc(stored[p], 16)

            load(0, 0)
            load(1, 1)
            with eng.Fori(0, CHUNKS // 2 - 1) as i:
                load(2 * i + 2, 0)
                store(2 * i, 0)
                load(2 * i + 3, 1)
                store(2 * i + 1, 1)
            store(CHUNKS - 2, 0)
            store(CHUNKS - 1, 1)
            eng.wait_ge(tail, 5)
            eng.dma_start(ut_dram, ut[:, :]).then_inc(ut_stored, 16)
            eng.wait_ge(ut_stored, 16)
            for p in (0, 1):
                eng.wait_ge(stored[p], 8 * CHUNKS)

        @block.gpsimd
        def _(eng):
            make_identity(eng, ident, 128, zeroed, consts)
            eng.memset(epst[:, :], EPS).then_inc(consts, 1)
            eng.wait_ge(w_loaded, 32)

            def residual(n, p):
                need(eng, act_ready, n + 1)
                need(eng, stored[p], 8 * (n - p))
                need(eng, k_filled, 4 * (n - 1))
                eng.tensor_tensor(x2[p][:, :], act[p][:, :], xin[p][:, :], ALU.add).then_inc(x2_ready, 1)

            def add_bias(n, p):
                need(eng, kvw_ready, n + 1)
                need(eng, kv_summed, n - 1)
                for s in range(SUB):
                    eng.tensor_tensor(kvf[p][:, s, :], kvw[p][:, s, :], W["ln_b"], ALU.add).then_inc(kvf_ready, 1)

            def step(n, p):
                if has(n + 1):
                    residual(n + 1, 1 - p)
                if has(n - 1):
                    add_bias(n - 1, 1 - p)

            run(eng, step)

        @block.scalar
        def _(eng):
            eng.wait_ge(norm_step, 4)
            eng.activation(gsd[:, :], gvar[:, :], ACT.Sqrt, bias=epst[:, 0:1]).then_inc(sd_step, 1)
            eng.wait_ge(affine_ready, 3)

            def gated(n, p):
                need(eng, loaded[p], 16 * (n - p) + 32)
                need(eng, x2_ready, n - 1)
                eng.activation(act[p][:, :], yin[p][:, :], ACT.Silu, bias=gb[:, 0:1],
                               scale=ga[:, 0:1]).then_inc(act_ready, 1)

            def square(n, p):
                need(eng, ss_ready, n)
                for half in (0, 1):
                    need(eng, k_filled, 4 * n + 2 * half + 2)
                    eng.activation(sq[:, 2 * GROUPS * half:2 * GROUPS * (half + 1), :],
                                   psK[2 * p + half][:, :, :].rearrange("p s (g e) -> p (s g) e", e=HD),
                                   ACT.Square).then_inc(sq_ready, 1)

            def deviation(n):
                need(eng, ss_ready, n + 1)
                need(eng, kvn_ready, 2 * n)
                eng.activation(sd[:, :, :], ss[:, :, :], ACT.Sqrt, scale=1.0 / (HD - 1)).then_inc(sd_ready, 1)

            def step(n, p):
                if has(n + 1):
                    gated(n + 1, 1 - p)
                if has(n - 1):
                    deviation(n - 1)
                if has(n):
                    square(n, p)

            run(eng, step)

        @block.vector
        def _(eng):
            eng.wait_ge(w_loaded, 32)
            eng.wait_ge(consts, 2)
            eng.tensor_copy(moments[:, 0:1], st[:, 0:1]).then_inc(norm_step, 1)
            eng.scalar_tensor_tensor(moments[:, 1:2], st[:, 0:1], st[:, 0:1], st[:, 1:2],
                                     ALU.mult, ALU.add).then_inc(norm_step, 1)
            eng.wait_ge(g_filled, 1)
            eng.tensor_copy(gm[:, :], psG[:, 0:2]).then_inc(norm_step, 1)
            eng.wait_ge(norm_step, 3)
            eng.tensor_scalar(gb[:, :], gm[:, 0:1], -1.0, None, ALU.mult).then_inc(affine_ready, 1)
            eng.wait_ge(affine_ready, 1)
            eng.scalar_tensor_tensor(gvar[:, :], gm[:, 0:1], gb[:, 0:1], gm[:, 1:2],
                                     ALU.mult, ALU.add).then_inc(norm_step, 1)
            eng.wait_ge(sd_step, 1)
            eng.reciprocal(gsd[:, :], gsd[:, :]).then_inc(norm_step, 1)
            eng.wait_ge(norm_step, 5)
            eng.tensor_tensor(ga[:, :], gsd[:, :], W["gamma"], ALU.mult).then_inc(affine_ready, 1)
            eng.wait_ge(affine_ready, 2)
            eng.scalar_tensor_tensor(gb[:, :], gb[:, :], ga[:, 0:1], W["beta"],
                                     ALU.mult, ALU.add).then_inc(affine_ready, 1)
            wkv = W["wkv"].rearrange("c (g e) -> c g e", e=HD)
            eng.tensor_reduce(wmean[:, :, :], wkv, AX_X, ALU.add).then_inc(wcen_ready, 1)
            eng.wait_ge(wcen_ready, 1)
            eng.tensor_scalar(wmean[:, :, :], wmean[:, :, :], 1.0 / HD, None, ALU.mult).then_inc(wcen_ready, 1)
            eng.wait_ge(wcen_ready, 2)
            eng.tensor_tensor(wcen[:, :, :], wkv, wmean[:, :, :].broadcast_to([C, GROUPS, HD]),
                              ALU.subtract).then_inc(wcen_ready, 1)

            def sum_squares(n, p):
                need(eng, sq_ready, 2 * n + 2)
                need(eng, sd_ready, n)
                eng.tensor_reduce(ss[:, :, :], sq[:, :, :], AX_X, ALU.add).then_inc(ss_ready, 1)

            def normalize(n, p):
                need(eng, sd_ready, n + 1)
                eng.tensor_scalar(sd[:, :, :], sd[:, :, :], EPS, None, ALU.add).then_inc(sde_ready, 1)
                need(eng, sde_ready, n + 1)
                eng.reciprocal(sd[:, :, :], sd[:, :, :]).then_inc(rsd_ready, 1)
                need(eng, rsd_ready, n + 1)
                need(eng, kvw_ready, n)
                for half in (0, 1):
                    eng.tensor_tensor(
                        kvn[:, 2 * half:2 * half + 2, :].rearrange("p s (g e) -> p (s g) e", e=HD),
                        sd[:, 2 * GROUPS * half:2 * GROUPS * (half + 1), :].broadcast_to([C, 2 * GROUPS, HD]),
                        psK[2 * p + half][:, :, :].rearrange("p s (g e) -> p (s g) e", e=HD),
                        ALU.mult).then_inc(kvn_ready, 1)

            def weigh(n, p):
                need(eng, kvn_ready, 2 * n + 2)
                need(eng, kvf_ready, SUB * (n - 1))
                eng.tensor_tensor(kvw[p][:, :, :], kvn[:, :, :],
                                  W["ln_w"].unsqueeze(1).broadcast_to([C, SUB, GROUPS * HD]),
                                  ALU.mult).then_inc(kvw_ready, 1)

            def step(n, p):
                if has(n - 1):
                    normalize(n - 1, 1 - p)
                if has(n):
                    sum_squares(n, p)
                if has(n - 1):
                    weigh(n - 1, 1 - p)

            run(eng, step)
            eng.wait_ge(kv_summed, CHUNKS)
            eng.tensor_tensor(kvb[:, :], W["headmask"], psA[:, :], ALU.mult).then_inc(tail, 1)
            eng.wait_ge(tail, 1)
            eng.tensor_scalar(kvb[:, :], kvb[:, :], 1.0 / TOKENS, None, ALU.mult).then_inc(tail, 1)
            eng.wait_ge(tail_mm, 1)
            eng.tensor_tensor(gmat[:, :], ident[:, :], psG[:, :], ALU.add).then_inc(tail, 1)
            eng.wait_ge(tail_mm, 2)
            eng.wait_ge(tail, 3)
            eng.tensor_copy(ut[:, :], psU[:, :]).then_inc(tail, 2)

        @block.tensor
        def _(eng):
            eng.wait_ge(w_loaded, 32)
            eng.wait_ge(norm_step, 2)
            eng.matmul(psG[:, 0:2], W["groups"], moments[:, :], start=True, stop=True).then_inc(g_filled, 1)
            eng.wait_ge(wcen_ready, 3)

            def keys_values(n, p):
                need(eng, x2_ready, n + 1)
                need(eng, kvn_ready, 2 * (n - 1))
                need(eng, sq_ready, 2 * (n - 1))
                for s in range(SUB):
                    eng.matmul(psK[2 * p + s // 2][:, s % 2, :], x2[p][:, 128 * s:128 * s + 128],
                               wcen[:, :, :].rearrange("c g e -> c (g e)"), start=True,
                               stop=True).then_inc(k_filled, 1)

            def accumulate(n, p):
                first, last = isinstance(n, int) and n == 0, isinstance(n, int) and n == CHUNKS - 1
                for s in range(SUB):
                    need(eng, kvf_ready, SUB * n + s + 1)
                    mm = eng.matmul(psA[:, :], kvf[p][:, s, 0:128], kvf[p][:, s, 128:256],
                                    start=(first and s == 0), stop=(last and s == SUB - 1))
                mm.then_inc(kv_summed, 1)

            def step(n, p):
                if has(n + 1):
                    keys_values(n + 1, 1 - p)
                if has(n - 1):
                    accumulate(n - 1, 1 - p)

            run(eng, step)

            eng.wait_ge(tail, 2)
            eng.matmul(psG[:, :], kvb[:, :], W["wq"], start=True, stop=True).then_inc(tail_mm, 1)
            eng.wait_ge(tail, 3)
            eng.matmul(psU[:, :], gmat[:, :], W["o1t"], start=True, stop=True).then_inc(tail_mm, 1)


def mlp_phase(nc, x2_dram, ut_dram, w_dram, out_dram):
    at, width = offsets(GLOBAL_COLS)
    lo, hi = at["o2t"]
    WIDE = 2 * T
    STEPS = TOKENS // WIDE
    assert STEPS % 2 == 1

    with ExitStack() as ctx:
        def sb(name, shape):
            return ctx.enter_context(nc.sbuf_tensor(f"ml_{name}", shape, F32))

        sems = []

        def sem(name):
            sems.append(ctx.enter_context(nc.semaphore(f"ml_{name}")))
            return sems[-1]

        ut = sb("ut", [C, 128])
        o2t = sb("o2t", [C, 128])
        xin = [sb(f"xin{p}", [C, WIDE]) for p in range(2)]
        xt = [sb(f"xt{p}", [C, WIDE]) for p in range(2)]
        u = [sb(f"u{p}", [C, WIDE]) for p in range(2)]
        t = [sb(f"t{p}", [C, WIDE]) for p in range(2)]
        xo = [sb(f"xo{p}", [C, WIDE]) for p in range(2)]
        psU = [ctx.enter_context(nc.psum_tensor(f"ml_psU{b}", [C, WIDE], F32)) for b in (0, 1)]
        psO = [ctx.enter_context(nc.psum_tensor(f"ml_psO{b}", [C, WIDE], F32)) for b in (0, 1)]
        w_loaded = sem("w_loaded")
        loaded = [sem(f"loaded{p}") for p in (0, 1)]
        stored = [sem(f"stored{p}") for p in (0, 1)]
        u_filled = sem("u_filled")
        x_kept = sem("x_kept")
        u_ready = sem("u_ready")
        o_filled = sem("o_filled")
        t_ready = sem("t_ready")
        out_ready = sem("out_ready")

        def run(eng, first, step, last):
            first()
            step(1, 1)
            step(2, 0)
            with eng.Fori(1, STEPS // 2) as i:
                step(2 * i + 1, 1)
                step(2 * i + 2, 0)
            last()

        ctx.callback(clear_semaphores, nc, sems)
        block = ctx.enter_context(nc.Block())

        @block.sync
        def _(eng):
            eng.dma_start(ut[:, :], ut_dram).then_inc(w_loaded, 16)
            eng.dma_start(o2t[:, :], w_dram[:, lo:hi]).then_inc(w_loaded, 16)

            def load(n, p):
                need(eng, u_filled, n - 1)
                need(eng, x_kept, n - 1)
                eng.dma_start(xin[p][:, :], x2_dram[:, bass.ds(WIDE * n, WIDE)]).then_inc(loaded[p], 16)

            load(0, 0)
            load(1, 1)
            load(2, 0)
            with eng.Fori(1, STEPS // 2) as i:
                load(2 * i + 1, 1)
                load(2 * i + 2, 0)

        @block.gpsimd
        def _(eng):
            def store(n, p):
                need(eng, out_ready, n + 1)
                eng.dma_start(out_dram[:, bass.ds(WIDE * n, WIDE)], xo[p][:, :]).then_inc(stored[p], 16)

            run(eng, lambda: store(0, 0), store, lambda: None)
            eng.wait_ge(stored[0], 16 * (STEPS // 2 + 1))
            eng.wait_ge(stored[1], 16 * (STEPS // 2))

        @block.scalar
        def _(eng):
            def inner(n, p):
                need(eng, u_filled, n + 1)
                need(eng, o_filled, n - 1)
                eng.activation(u[p][:, :], psU[p][:, :], ACT.Gelu).then_inc(u_ready, 1)

            def outer(n, p):
                need(eng, t_ready, n + 1)
                need(eng, stored[p], 8 * (n - p))
                eng.activation(xo[p][:, :], t[p][:, :], ACT.Gelu).then_inc(out_ready, 1)

            def step(n, p):
                inner(n, p)
                outer(n - 1, 1 - p)

            run(eng, lambda: inner(0, 0), step, lambda: outer(STEPS - 1, 0))

        @block.vector
        def _(eng):
            def keep(n, p):
                need(eng, loaded[p], 8 * (n - p) + 16)
                need(eng, t_ready, n - 1)
                eng.tensor_copy(xt[p][:, :], xin[p][:, :]).then_inc(x_kept, 1)

            def add(n, p):
                need(eng, o_filled, n + 1)
                need(eng, x_kept, n + 1)
                need(eng, out_ready, n - 1)
                eng.tensor_tensor(t[p][:, :], xt[p][:, :], psO[p][:, :], ALU.add).then_inc(t_ready, 1)

            def step(n, p):
                keep(n, p)
                add(n - 1, 1 - p)

            run(eng, lambda: keep(0, 0), step, lambda: add(STEPS - 1, 0))

        @block.tensor
        def _(eng):
            eng.wait_ge(w_loaded, 32)

            def inner(n, p):
                need(eng, loaded[p], 8 * (n - p) + 16)
                need(eng, u_ready, n - 1)
                for half in (slice(0, T), slice(T, WIDE)):
                    mm = eng.matmul(psU[p][:, half], ut[:, :], xin[p][:, half], start=True, stop=True)
                mm.then_inc(u_filled, 1)

            def outer(n, p):
                need(eng, u_ready, n + 1)
                need(eng, t_ready, n - 1)
                for half in (slice(0, T), slice(T, WIDE)):
                    mm = eng.matmul(psO[p][:, half], o2t[:, :], u[p][:, half], start=True, stop=True)
                mm.then_inc(o_filled, 1)

            def step(n, p):
                inner(n, p)
                outer(n - 1, 1 - p)

            run(eng, lambda: inner(0, 0), step, lambda: outer(STEPS - 1, 0))


def network_kernel(nc, x, w_row, w_col, w_lepe, w_fwd, w_bwd, w_global, w_chunked, out):
    def scratch(name, shape):
        return nc.dram_tensor(name, shape, F32).ap()

    h = scratch("h_att", (C, SIDE + 2, SIDE))
    v = scratch("v_att", (C, SIDE + 2, SIDE))
    x1 = scratch("x1", (C, TOKENS + 2))
    y_fwd = scratch("y_fwd", (C, TOKENS))
    y_sum = scratch("y_sum", (C, TOKENS))
    stats = scratch("stats", (C, 2))
    x2 = scratch("x2", (C, TOKENS))
    ut = scratch("ut", (C, C))
    x3 = scratch("x3", (C, TOKENS))

    attention_phase(nc, False, x, w_row, h)
    attention_phase(nc, True, x, w_col, v)
    lepe_phase(nc, h, v, w_lepe, x1)
    mamba_phase(nc, "forward", x1, w_fwd, y_fwd)
    mamba_phase(nc, "backward", x1, w_bwd, y_sum, y_fwd, stats)
    kv_phase(nc, y_sum, stats, x1, w_global, x2, ut)
    mlp_phase(nc, x2, ut, w_global, x3)
    mamba_phase(nc, "chunked", x3, w_chunked, out)





def _pack(cols, parts):
    at, width = offsets(cols)
    out = np.zeros((C, width), np.float32)
    for name, a in parts.items():
        lo, hi = at[name]
        a = a.reshape(a.shape[0], -1)
        assert a.shape[1] == hi - lo, (name, a.shape)
        out[:a.shape[0], lo:hi] = a
    return out


def _lay_mamba1(W_in, conv_w, conv_b, W_x, W_dt, b_dt, A_log, D, W_out):
    blocks = lambda a: a.reshape(2, 128, -1).transpose(1, 0, 2)
    units = lambda a: a.reshape(2, 128, STATE).transpose(1, 2, 0)
    x_rows = blocks(W_x)
    dtr = np.zeros((128, 2, 32), np.float32)
    dtr[:, :, 0:8] = x_rows[:, :, 0:8]
    return _pack(MAMBA1_COLS, {
        "win": W_in[:, 0:256], "wz": W_in[:, 256:512],
        "tapw": np.broadcast_to(conv_w.T.reshape(1, 2 * 256), (128, 512)),
        "wbc": np.tile(x_rows[:, :, 8:40], (1, 1, 3)), "wdtr": dtr.transpose(2, 1, 0), "wdt": W_dt,
        "bdt": blocks(b_dt), "convb": blocks(conv_b), "dskip": blocks(D), "alog": units(A_log),
        "wout": blocks(W_out)})


def _lay_mamba3(ln_g, ln_b, in_proj_w, conv_w, conv_b, x_proj_w, dt_proj_w, dt_proj_b, A_log, D, out_proj_w):
    win, wz = np.zeros((2, 128, 2, 128), np.float32)
    wb, wc = np.zeros((2, 128, 32), np.float32)
    dtr = np.zeros((128, 2, 32), np.float32)
    wdt = np.zeros((32, 2, 128), np.float32)
    wout = np.zeros((128, 2, 128), np.float32)
    for half in range(2):
        rows = slice(64 * half, 64 * half + 64)
        wb[rows, 16 * half:16 * half + 16] = x_proj_w[2:18].T
        wc[rows, 16 * half:16 * half + 16] = x_proj_w[18:34].T
        for b in range(2):
            q = 2 * b + half
            ch = slice(32 * q, 32 * q + 32)
            for copy in range(2):
                at = 32 * ((q + 2 * copy) % 4)
                win[at:at + 32, b, rows] = in_proj_w[0:64].T
            wz[ch, b, rows] = in_proj_w[64:128].T
            dtr[rows, b, 2 * q:2 * q + 2] = x_proj_w[0:2].T
            wdt[2 * q:2 * q + 2, b, rows] = dt_proj_w.T
            wout[rows, b, ch] = out_proj_w.T
    both = lambda v: np.repeat(np.tile(v.reshape(64), 2).reshape(128, 1), 2, axis=1)
    return _pack(MAMBA3_COLS, {
        "win": win, "wz": wz, "wb": np.tile(wb, (1, 3)), "wc": np.tile(wc, (1, 3)), "wdtr": dtr.transpose(2, 1, 0),
        "tapw": np.broadcast_to(np.tile(conv_w.T.reshape(4, 64), (1, 4)).reshape(1, 1024), (128, 1024)),
        "wdt": wdt, "bdt": both(dt_proj_b), "convb": both(conv_b), "dskip": both(D),
        "alog": np.repeat(np.tile(A_log, (2, 1)), 2, axis=1), "wout": wout,
        "ln_g": ln_g.reshape(128, 1), "ln_b": ln_b.reshape(128, 1)})


def _lay_attention(qkv_w, qkv_b, table):
    by_channel = lambda a: a.reshape(HEADS, HD, -1).transpose(1, 0, 2).reshape(C, -1)
    onehot = np.zeros((C, SIDE), np.float32)
    kc = np.zeros((C, HEADS, SIDE), np.float32)
    mask = np.zeros((C, 3), np.float32)
    for part in range(3):
        for a in range(S7):
            row = 6 * HD + S7 * part + a
            onehot[row, a * SIDE // S7:(a + 1) * SIDE // S7] = 1.0
            kc[row] = np.repeat(table[a], SIDE // S7, axis=0).T
            mask[row, part] = 1.0
    return _pack(ATTN_COLS, {
        "wq": by_channel(qkv_w[0:C]).T, "wk": by_channel(qkv_w[C:2 * C]).T, "wv": qkv_w[2 * C:].T,
        "bq": by_channel(qkv_b[0:C]), "bk": by_channel(qkv_b[C:2 * C]), "bv": qkv_b[2 * C:].reshape(C, 1),
        "mask": mask, "onehot": onehot, "selm": np.tile(np.eye(HEADS), (3, 1)), "kc": kc})


def _lay_lepe(h_w, h_b, v_w, v_b, proj_w, proj_b):
    col = lambda a: a.reshape(C, -1)
    return _pack(LEPE_COLS, {"tap_h": col(h_w), "tap_v": col(v_w), "b_h": col(h_b), "b_v": col(v_b),
                             "proj_b": col(proj_b), "proj": proj_w.T})


def _lay_global(gamma, beta, qkv_w, o1_w, o2_w, kln_w, kln_b, vln_w, vln_b):
    qkv = qkv_w.reshape(HEADS, 3, HD, C)
    part = lambda i: qkv[:, i].reshape(C, C)
    row = lambda k, v: np.broadcast_to(np.concatenate([k.reshape(1, C), v.reshape(1, C)], axis=1), (C, 2 * C))
    return _pack(GLOBAL_COLS, {
        "gamma": gamma.reshape(C, 1), "beta": beta.reshape(C, 1),
        "wkv": np.concatenate([part(1).T, part(2).T], axis=1), "wq": part(0),
        "o1t": o1_w.T, "o2t": o2_w.T, "ln_w": row(kln_w, vln_w), "ln_b": row(kln_b, vln_b),
        "groups": np.kron(np.eye(4), np.full((32, 32), 1.0 / 32)),
        "headmask": np.kron(np.eye(HEADS), np.ones((HD, HD)))})


def kernel(**inputs):
    import concourse.bacc as _bacc
    from concourse.bass_utils import run_bass_kernel_spmd as _run

    part = lambda layer, names: [np.asarray(inputs[f"{layer}_conv_{n}"]) for n in names.split()]
    table_h, table_v = part("L0", "table_h table_v")
    tiles = np.arange(S7)
    rel = tiles[:, None] - tiles[None, :] + S7 - 1
    mamba1 = "W_in conv_w conv_b W_x W_dt b_dt A_log D W_out".split()
    arrays = {
        "x": np.asarray(inputs["x"]).reshape(C, SIDE, SIDE),
        "w_row": _lay_attention(*part("L0", "qkv_h_w qkv_h_b"), table_h[S7 - 1, rel]),
        "w_col": _lay_attention(*part("L0", "qkv_v_w qkv_v_b"), table_v[rel, S7 - 1]),
        "w_lepe": _lay_lepe(*part("L0", "lepe_h_w lepe_h_b lepe_v_w lepe_v_b proj_w proj_b")),
        "w_fwd": _lay_mamba1(*part("L1", " ".join(n + "_f" for n in mamba1))),
        "w_bwd": _lay_mamba1(*part("L1", " ".join(n + "_b" for n in mamba1))),
        "w_global": _lay_global(*part("L1", "gn_gamma gn_beta"),
                                *part("L2", "qkv_w o1_w o2_w kln_w kln_b vln_w vln_b")),
        "w_chunked": _lay_mamba3(*part("L3", "ln_g ln_b in_proj_w conv_w conv_b x_proj_w dt_proj_w "
                                             "dt_proj_b A_log D out_proj_w")),
    }
    nc = _bacc.Bacc("TRN2", target_bir_lowering=False, num_devices=1)
    args = [nc.dram_tensor(f"in_{n}_dram", a.shape, F32, kind="ExternalInput").ap() for n, a in arrays.items()]
    args.append(nc.dram_tensor("out_0_dram", (C, TOKENS), F32, kind="ExternalOutput").ap())
    network_kernel(nc, *args)
    r = _run(nc, [{f"in_{n}_dram": np.ascontiguousarray(a) for n, a in arrays.items()}], core_ids=[0])
    return r.results[0]["out_0_dram"].reshape(1, C, SIDE, SIDE)
```
